# Optimizing a Trainium2 kernel written in Bass

```python
import numpy as np
import jax
import jax.numpy as jnp

def _softmax(x, axis=-1):
    return jax.nn.softmax(x, axis=axis)

def _gelu(x):
    return jax.nn.gelu(x, approximate=True)

def _silu(x):
    return jax.nn.silu(x)

def _sigmoid(x):
    return jax.nn.sigmoid(x)

def _layernorm(x, axis=-1, eps=1e-05):
    m = jnp.mean(x, axis=axis, keepdims=True)
    v = jnp.var(x, axis=axis, keepdims=True)
    return (x - m) / jnp.sqrt(v + eps)

def _scatter_add(tgt, idx, src, axis=0):
    return tgt.at[idx].add(src)

def _segment_sum(src, seg, n):
    return jax.ops.segment_sum(src, seg, n)
kernel_name = 'mk_decoder_postln_d1_seqx_r8_209747'

def setup_inputs(seed: int=0):
    np.random.seed(seed)
    _w = jnp.asarray

    def _rec_inputs():
        import jax
        import jax.numpy as jnp
        _rk = jax.random.key(seed)
        x = 7.22e-05 + 1 * jax.random.normal(jax.random.fold_in(_rk, 1), (64, 64, 256), jnp.float32)
        _lenS = 64 - jax.random.randint(jax.random.fold_in(_rk, 7), (64,), 0, max(1, 64 // 4) + 1, jnp.int32)
        _lenS2 = 64 - jax.random.randint(jax.random.fold_in(_rk, 8), (64,), 0, max(1, 64 // 4) + 1, jnp.int32)
        _ctx_512P = jax.random.normal(jax.random.fold_in(_rk, 11), (64, 16, 64), jnp.float32)
        _ctx_512c = jax.random.dirichlet(jax.random.fold_in(_rk, 511), 0.3 * jnp.ones((16,), jnp.float32), (64, 64))
        _ctx_512t = jnp.einsum('bsk,bkd->bsd', _ctx_512c, _ctx_512P)
        _ctx_512t = _ctx_512t * jax.lax.rsqrt(jnp.mean(jnp.square(_ctx_512t)) + 1e-12) * 0.953939
        ctx_512 = -0.000514642 + 1.00011 * (_ctx_512t + 0.3 * jax.random.normal(jax.random.fold_in(_rk, 611), (64, 64, 64), jnp.float32))
        return (x, ctx_512)
    x, ctx_512 = _rec_inputs()

    def _L0_attn_setup():
        import jax, jax.numpy as jnp
        import numpy as np
        B, N, E, H = (1, 512, 256, 16)
        D = E // H
        DEGREE = 4
        LN_EPS = 1e-05
        ROPE_BASE = 10000.0

        def rope_cos_sin(n, d):
            inv_freq = 1.0 / ROPE_BASE ** (jnp.arange(0, d, 2, dtype=jnp.float32) / d)
            t = jnp.arange(n, dtype=jnp.float32)[:, None] * inv_freq[None, :]
            return (jnp.cos(t), jnp.sin(t))

        def apply_rope(x, cos, sin):
            x1, x2 = jnp.split(x, 2, axis=-1)
            c = cos[None, :, None, :]
            s = sin[None, :, None, :]
            return jnp.concatenate([x1 * c - x2 * s, x1 * s + x2 * c], axis=-1)

        def layernorm(x, scale, bias, eps=LN_EPS):
            m = jnp.mean(x, axis=-1, keepdims=True)
            v = jnp.var(x, axis=-1, keepdims=True)
            return (x - m) * jax.lax.rsqrt(v + eps) * scale + bias

        def polynomial_attention(q, k, v, degree, is_causal):
            a = jnp.einsum('bhnd,bhmd->bhnm', q, k) ** degree
            if is_causal:
                a = jnp.tril(a)
            denom = jnp.sum(a, axis=-1, keepdims=True)
            return jnp.einsum('bhnm,bhmd->bhnd', a / denom, v)
        key = jax.random.key(seed)
        k0, k1, k2 = jax.random.split(key, 3)
        x = jax.random.normal(k0, (B, N, E), dtype=jnp.float32)
        w_qkv = jax.random.normal(k1, (E, 3 * E), dtype=jnp.float32) * (1.0 / np.sqrt(E))
        w_out = jax.random.normal(k2, (E, E), dtype=jnp.float32) * (1.0 / np.sqrt(E))
        ln_scale = jnp.ones((D,), dtype=jnp.float32)
        ln_bias = jnp.zeros((D,), dtype=jnp.float32)
        return {'x': x, 'w_qkv': w_qkv, 'w_out': w_out, 'ln_scale': ln_scale, 'ln_bias': ln_bias}
    _L0_attn_all = _L0_attn_setup()
    _L0_attn_in = {k: v for k, v in _L0_attn_all.items() if k in ('w_qkv', 'w_out', 'ln_scale', 'ln_bias')}
    del _L0_attn_all

    def _L0_xattn_setup():
        import jax, jax.numpy as jnp
        import numpy as np
        N_HEADS = 16
        N_KV_HEADS = 4
        ROPE_THETA = 10000.0
        EPS = 1e-05

        def _rms_norm(x, w):
            var = jnp.mean(x * x, axis=-1, keepdims=True)
            return x * jax.lax.rsqrt(var + EPS) * w

        def _rope_sin_cos(T, head_dim, dtype):
            inv_freq = 1.0 / ROPE_THETA ** (jnp.arange(0, head_dim, 2, dtype=jnp.float32) / head_dim)
            t = jnp.arange(T, dtype=jnp.float32)
            freqs = jnp.outer(t, inv_freq)
            emb = jnp.concatenate([freqs, freqs], -1)
            return (jnp.sin(emb).astype(dtype)[None, None], jnp.cos(emb).astype(dtype)[None, None])

        def _rotate_half(x):
            h = x.shape[-1] // 2
            x1, x2 = (x[..., :h], x[..., h:])
            return jnp.concatenate([-x2, x1], axis=-1)
        key = jax.random.key(seed)
        ks = jax.random.split(key, 6)
        B, T, C = (2, 256, 256)
        Ckv = C // N_HEADS * N_KV_HEADS
        return {'q': jax.random.normal(ks[0], (B, T, C), jnp.float32), 'k': jax.random.normal(ks[1], (B, T, Ckv), jnp.float32), 'v': jax.random.normal(ks[2], (B, T, Ckv), jnp.float32), 'q_norm_w': jnp.ones((C,), jnp.float32), 'k_norm_w': jnp.ones((Ckv,), jnp.float32), 'w_out': jax.random.normal(ks[3], (C, C), jnp.float32) * C ** (-0.5)}
    _L0_xattn_all = _L0_xattn_setup()
    _L0_xattn_in = {k: v for k, v in _L0_xattn_all.items() if k in ('q_norm_w', 'k_norm_w', 'w_out')}
    del _L0_xattn_all

    def _L0_ffn_setup():
        import jax, jax.numpy as jnp
        import numpy as np
        NUM_EXPERTS = 8
        EXPERTS_PER_TOK = 2
        key = jax.random.key(seed)
        k1, k2, k3, k4, k5 = jax.random.split(key, 5)
        B, T, D, F, E = (4, 128, 256, 128, NUM_EXPERTS)
        return {'x': jax.random.normal(k1, (B, T, D), dtype=jnp.float32), 'router_w': jax.random.normal(k2, (D, E), dtype=jnp.float32) * 0.02, 'gate_proj': jax.random.normal(k3, (E, D, F), dtype=jnp.float32) * 0.02, 'up_proj': jax.random.normal(k4, (E, D, F), dtype=jnp.float32) * 0.02, 'down_proj': jax.random.normal(k5, (E, F, D), dtype=jnp.float32) * 0.02}
    _L0_ffn_all = _L0_ffn_setup()
    _L0_ffn_in = {k: v for k, v in _L0_ffn_all.items() if k in ('router_w', 'gate_proj', 'up_proj', 'down_proj')}
    del _L0_ffn_all
    return {'x': x, 'ctx_512': ctx_512, 'L0_attn_w_qkv': _L0_attn_in['w_qkv'], 'L0_attn_w_out': _L0_attn_in['w_out'], 'L0_attn_ln_scale': _L0_attn_in['ln_scale'], 'L0_attn_ln_bias': _L0_attn_in['ln_bias'], 'L0_xattn_q_norm_w': _L0_xattn_in['q_norm_w'], 'L0_xattn_k_norm_w': _L0_xattn_in['k_norm_w'], 'L0_xattn_w_out': _L0_xattn_in['w_out'], 'L0_ffn_router_w': _L0_ffn_in['router_w'], 'L0_ffn_gate_proj': _L0_ffn_in['gate_proj'], 'L0_ffn_up_proj': _L0_ffn_in['up_proj'], 'L0_ffn_down_proj': _L0_ffn_in['down_proj']}

def reference(x, ctx_512, L0_attn_w_qkv, L0_attn_w_out, L0_attn_ln_scale, L0_attn_ln_bias, L0_xattn_q_norm_w, L0_xattn_k_norm_w, L0_xattn_w_out, L0_ffn_router_w, L0_ffn_gate_proj, L0_ffn_up_proj, L0_ffn_down_proj):
    import jax
    import jax.numpy as jnp

    def _L0_attn_ref(x, w_qkv, w_out, ln_scale, ln_bias):
        import jax, jax.numpy as jnp
        import numpy as np
        B, N, E, H = (1, 512, 256, 16)
        D = E // H
        DEGREE = 4
        LN_EPS = 1e-05
        ROPE_BASE = 10000.0

        def rope_cos_sin(n, d):
            inv_freq = 1.0 / ROPE_BASE ** (jnp.arange(0, d, 2, dtype=jnp.float32) / d)
            t = jnp.arange(n, dtype=jnp.float32)[:, None] * inv_freq[None, :]
            return (jnp.cos(t), jnp.sin(t))

        def apply_rope(x, cos, sin):
            x1, x2 = jnp.split(x, 2, axis=-1)
            c = cos[None, :, None, :]
            s = sin[None, :, None, :]
            return jnp.concatenate([x1 * c - x2 * s, x1 * s + x2 * c], axis=-1)

        def layernorm(x, scale, bias, eps=LN_EPS):
            m = jnp.mean(x, axis=-1, keepdims=True)
            v = jnp.var(x, axis=-1, keepdims=True)
            return (x - m) * jax.lax.rsqrt(v + eps) * scale + bias

        def polynomial_attention(q, k, v, degree, is_causal):
            a = jnp.einsum('bhnd,bhmd->bhnm', q, k) ** degree
            if is_causal:
                a = jnp.tril(a)
            denom = jnp.sum(a, axis=-1, keepdims=True)
            return jnp.einsum('bhnm,bhmd->bhnd', a / denom, v)
        b, n, e = x.shape
        proj = x @ w_qkv
        q, k, v = jnp.split(proj, 3, axis=-1)
        q = q.reshape(b, n, H, D)
        k = k.reshape(b, n, H, D)
        v = v.reshape(b, n, H, D)
        cos, sin = rope_cos_sin(n, D)
        q = apply_rope(q, cos, sin)
        k = apply_rope(k, cos, sin)
        q = q.transpose(0, 2, 1, 3)
        k = k.transpose(0, 2, 1, 3)
        v = v.transpose(0, 2, 1, 3)
        q = layernorm(q, ln_scale, ln_bias)
        k = layernorm(k, ln_scale, ln_bias)
        out = polynomial_attention(q, k, v, DEGREE, True)
        out = out.transpose(0, 2, 1, 3).reshape(b, n, e)
        out = out @ w_out
        return out

    def _L0_xattn_ref(q, k, v, q_norm_w, k_norm_w, w_out):
        import jax, jax.numpy as jnp
        import numpy as np
        N_HEADS = 16
        N_KV_HEADS = 4
        ROPE_THETA = 10000.0
        EPS = 1e-05

        def _rms_norm(x, w):
            var = jnp.mean(x * x, axis=-1, keepdims=True)
            return x * jax.lax.rsqrt(var + EPS) * w

        def _rope_sin_cos(T, head_dim, dtype):
            inv_freq = 1.0 / ROPE_THETA ** (jnp.arange(0, head_dim, 2, dtype=jnp.float32) / head_dim)
            t = jnp.arange(T, dtype=jnp.float32)
            freqs = jnp.outer(t, inv_freq)
            emb = jnp.concatenate([freqs, freqs], -1)
            return (jnp.sin(emb).astype(dtype)[None, None], jnp.cos(emb).astype(dtype)[None, None])

        def _rotate_half(x):
            h = x.shape[-1] // 2
            x1, x2 = (x[..., :h], x[..., h:])
            return jnp.concatenate([-x2, x1], axis=-1)
        B, T, C = q.shape
        hd = C // N_HEADS
        g = N_HEADS // N_KV_HEADS
        q = _rms_norm(q, q_norm_w)
        k = _rms_norm(k, k_norm_w)
        q = q.reshape(B, T, N_HEADS, hd).transpose(0, 2, 1, 3)
        k = k.reshape(B, T, N_KV_HEADS, hd).transpose(0, 2, 1, 3)
        v = v.reshape(B, T, N_KV_HEADS, hd).transpose(0, 2, 1, 3)
        sin, cos = _rope_sin_cos(T, hd, q.dtype)
        q = q * cos + _rotate_half(q) * sin
        k = k * cos + _rotate_half(k) * sin
        qg = q.reshape(B, N_KV_HEADS, g, T, hd)
        scale = 1.0 / jnp.sqrt(jnp.asarray(hd, q.dtype))
        scores = jnp.einsum('bgnqd,bgkd->bgnqk', qg, k) * scale
        causal = jnp.tril(jnp.ones((T, T), bool))
        scores = jnp.where(causal, scores, jnp.asarray(-1e+30, scores.dtype))
        attn = jax.nn.softmax(scores, axis=-1)
        out = jnp.einsum('bgnqk,bgkd->bgnqd', attn, v)
        out = out.reshape(B, N_HEADS, T, hd).transpose(0, 2, 1, 3).reshape(B, T, C)
        return out @ w_out.T

    def _L0_ffn_ref(x, router_w, gate_proj, up_proj, down_proj):
        import jax, jax.numpy as jnp
        import numpy as np
        NUM_EXPERTS = 8
        EXPERTS_PER_TOK = 2
        E, K = (NUM_EXPERTS, EXPERTS_PER_TOK)
        scores = jnp.einsum('btd,de->bte', x, router_w).astype(jnp.float32)
        routing_weights, routing_idx = jax.lax.top_k(jax.nn.softmax(scores, axis=-1), K)
        routing_weights = (routing_weights / jnp.sum(routing_weights, axis=-1, keepdims=True)).astype(x.dtype)
        onehot = jax.nn.one_hot(routing_idx, E, dtype=x.dtype)
        dispatch_mask = jnp.sum(onehot, axis=2)
        combine_weights = jnp.einsum('btke,btk->bte', onehot, routing_weights)
        dispatched = x[:, :, None, :] * dispatch_mask[..., None]
        gate = jnp.einsum('bted,edf->btef', dispatched, gate_proj)
        up = jnp.einsum('bted,edf->btef', dispatched, up_proj)
        act = jax.nn.silu(gate) * up
        expert_out = jnp.einsum('btef,efd->bted', act, down_proj)
        return jnp.einsum('bted,bte->btd', expert_out, combine_weights)
    x = _layernorm(x + _L0_attn_ref(x, L0_attn_w_qkv, L0_attn_w_out, L0_attn_ln_scale, L0_attn_ln_bias), axis=-1)
    x = _layernorm(x + _L0_xattn_ref(x, ctx_512, ctx_512, L0_xattn_q_norm_w, L0_xattn_k_norm_w, L0_xattn_w_out), axis=-1)
    x = _layernorm(x + _L0_ffn_ref(x, L0_ffn_router_w, L0_ffn_gate_proj, L0_ffn_up_proj, L0_ffn_down_proj), axis=-1)
    return x

_drawn_inputs = setup_inputs


def setup_inputs(seed=0):
    import zlib

    import numpy as np

    out = dict(_drawn_inputs(seed))
    spreads = {'L0_attn_ln_scale': (1.0, 0.2),
     'L0_attn_ln_bias': (0.0, 0.1),
     'L0_xattn_q_norm_w': (1.0, 0.2),
     'L0_xattn_k_norm_w': (1.0, 0.2)}
    factors = {'L0_ffn_router_w': 7.697,
     'L0_ffn_gate_proj': 6.725,
     'L0_ffn_up_proj': 6.67,
     'L0_ffn_down_proj': 6.666}
    for name, (base, spread) in spreads.items():
        noise = np.random.default_rng([zlib.crc32(name.encode()), seed]).standard_normal(out[name].shape)
        drawn = base * np.exp(spread * noise) if base else spread * noise
        out[name] = jnp.asarray(drawn.astype(out[name].dtype))
    for name, factor in factors.items():
        out[name] = (out[name] * factor).astype(out[name].dtype)
    return out
```

```python
from contextlib import ExitStack

import numpy as np

import concourse.bass as bass
from concourse import mybir

P = 128
SEQS, SEQ, E = 64, 64, 256
TOKENS = SEQS * SEQ
T = TOKENS // P
CTX = 64
HEADS, D = 16, 16
KV_HEADS = 4
PAIRS = HEADS // 2
EXPERTS, F = 8, 128
KC = E // P
UNROLL = 4
TABLES = 11
GROUP_TILES = 4
GROUP = GROUP_TILES * P
GROUPS = T // GROUP_TILES
EPS = 1e-5
VW = D + 1


class Tile:

    def __init__(self, n, rest):
        self.n, self.rest = n, rest % UNROLL

    def back(self, k):
        return Tile(self.n - k, self.rest - k)

    def slot(self, slots):
        return self.rest % slots

    @property
    def live(self):
        return not isinstance(self.n, int) or 0 <= self.n < T


class Turn:

    def __init__(self, n, parity=0):
        self.n, self.parity = n, parity % 2

    def back(self, k):
        return Turn(self.n - k, self.parity - k)


def over_tiles(eng, step, lag):
    for i in range(UNROLL):
        step(Tile(i, i))
    with eng.Fori(UNROLL, T - UNROLL + 1, UNROLL) as base:
        for u in range(UNROLL):
            step(Tile(base + u, u))
    for i in range(T, T + lag):
        step(Tile(i, i))


def wait_tile(eng, sem, tile, back=0):
    count = tile.n + 1 - back
    if isinstance(count, int) and count <= 0:
        return
    eng.wait_ge(sem, count)


def build_decoder(nc, x, x_t, ctx, w_qkv, w_out1, ln_scale, ln_bias, q_w, k_w, w_out2_t, router,
                  gate_w, up_w, down_w, cos_t, sin_t, keep_t, causal_add, quarter, identity, experts_iota, out):
    f32, f16, f32r = mybir.dt.float32, mybir.dt.float16, mybir.dt.float32r
    ALU, ACT, AX = mybir.AluOpType, mybir.ActivationFunctionType, mybir.AxisListType

    stack = ExitStack()
    with stack:
        def sb(name, shape, dt=f32):
            return stack.enter_context(nc.sbuf_tensor(name, shape, dt))

        def sem(name):
            return stack.enter_context(nc.semaphore(name))

        def bank(name):
            return stack.enter_context(nc.psum_tensor(name, [P, 512], f32))

        x_sb = sb("x_sb", [P, T, E])
        wqkv_hi, wqkv_lo = sb("wqkv_hi", [P, KC, 3 * E], f32r), sb("wqkv_lo", [P, KC, 3 * E], f32r)
        wo_raw = sb("wo_raw", [P, 2, KC, E])
        wo_hi, wo_lo = sb("wo_hi", [P, 2, KC, E], f32r), sb("wo_lo", [P, 2, KC, E], f32r)
        ffn_raw = sb("ffn_raw", [P, 3, EXPERTS, E])
        wqkv_raw = ffn_raw[:, 0, :, :].rearrange("p e n -> p (e n)")[:, 0:KC * 3 * E].rearrange(
            "p (k n) -> p k n", k=KC)
        ffn_hi, ffn_lo = sb("ffn_hi", [P, 3, EXPERTS, E], f32r), sb("ffn_lo", [P, 3, EXPERTS, E], f32r)
        router_raw = sb("router_raw", [P, KC, EXPERTS])
        router_hi, router_lo = sb("router_hi", [P, KC, EXPERTS], f32r), sb("router_lo", [P, KC, EXPERTS], f32r)
        cos_sb, sin_sb = sb("cos_sb", [P, D]), sb("sin_sb", [P, D])
        keep_sb, causal_sb = sb("keep_sb", [P, SEQ]), sb("causal_sb", [P, SEQ])
        quarter_sb = sb("quarter_sb", [P, 4])
        ident = sb("ident", [P, P])
        iota_sb = sb("iota_sb", [P, EXPERTS])
        scale_sb, bias_sb = sb("scale_sb", [P, 1]), sb("bias_sb", [P, 1])
        eps_sb, minus_half = sb("eps_sb", [P, GROUP_TILES]), sb("minus_half", [P, GROUP_TILES])
        qw_sb, kw_sb = sb("qw_sb", [P, E]), sb("kw_sb", [P, CTX])
        q_cos, q_sin = sb("q_cos", [P, HEADS, D]), sb("q_sin", [P, HEADS, D])
        k_cos, k_sin = sb("k_cos", [P, KV_HEADS, D]), sb("k_sin", [P, KV_HEADS, D])

        bank_qk, bank_v, bank_tr, bank_s0, bank_s1, bank_av, bank_ot, bank_out = (
            bank(n) for n in ("bank_qk", "bank_v", "bank_tr", "bank_s0", "bank_s1", "bank_av", "bank_ot", "bank_out"))
        bank_s = (bank_s0, bank_s1)

        block_names = ("weights_in", "tables_in", "x_in", "constants_set", "wqkv_split_hi", "weights_split",
                       "qk_tables_set")
        s = {n: sem(n) for n in block_names}
        weights_in, tables_in, x_in, constants_set, wqkv_split_hi, weights_split, qk_tables_set = (
            s[n] for n in block_names)
        ffn_in, ffn_hi_set, ffn_split = sem("ffn_in"), sem("ffn_hi_set"), sem("ffn_split")

        kq32 = sb("kq32", [P, 512])
        kq_hi, kq_lo = sb("kq_hi", [P, 512], f16), sb("kq_lo", [P, 512], f16)
        k_one = sb("k_one", [P, 2, KC, 2, 4, SEQ], f16)
        probs = [sb(f"probs{n}", [P, 1024]) for n in range(2)]
        v_pair = [[sb(f"v_pair{n}{q}", [P, PAIRS, 2 * VW]) for q in range(2)] for n in range(2)]
        o_inv, o_sb = sb("o_inv", [P, HEADS]), sb("o_sb", [P, HEADS, D])
        o_hi, o_lo = sb("o_hi", [P, KC, P], f32r), sb("o_lo", [P, KC, P], f32r)
        y_sb = sb("y_sb", [P, E])
        y_stats, y_mv, y_inv = sb("y_stats", [P, 6]), sb("y_mv", [P, 2]), sb("y_inv", [P, 1])
        y_std = sb("y_std", [P, 1])

        phase1 = ExitStack()

        def sb1(name, shape, dt=f32):
            return phase1.enter_context(nc.sbuf_tensor(name, shape, dt))

        xt_raw = [sb1(f"xt_raw{n}", [P, KC, P]) for n in range(4)]
        xt_hi = [sb1(f"xt_hi{n}", [P, KC, P], f32r) for n in range(2)]
        xt_lo = [sb1(f"xt_lo{n}", [P, KC, P], f32r) for n in range(2)]
        rot_cos, rot_sin = sb1("rot_cos", [P, 32, D]), sb1("rot_sin", [P, 32, D])
        rot = sb1("rot", [P, 32, D])
        centred, centred_sq = sb1("centred", [P, 32, D]), sb1("centred_sq", [P, 32, D])
        head_sum, head_mean, head_var = sb1("head_sum", [P, 32]), sb1("head_mean", [P, 32]), sb1("head_var", [P, 32])
        head_std, head_inv = sb1("head_std", [P, 32]), sb1("head_inv", [P, 32])
        qk_norm = [sb1(f"qk_norm{n}", [P, 32, D]) for n in range(2)]
        phase1.close()

        xt_loaded = [sem(f"xt_loaded{n}") for n in range(4)]
        names1 = ["xt_hi_set", "xt_split", "proj_qk_done", "proj_v_done", "rope_cos_done", "rope_sin_done",
                  "rope_sum_done", "head_sum_done", "head_mean_done", "centred_done", "centred_sq_done",
                  "head_var_done", "head_std_done", "head_inv_done", "qk_norm_done"]
        (xt_hi_set, xt_split, proj_qk_done, proj_v_done, rope_cos_done, rope_sin_done, rope_sum_done,
         head_sum_done, head_mean_done, centred_done, centred_sq_done, head_var_done, head_std_done,
         head_inv_done, qk_norm_done) = (sem(n) for n in names1)

        def attention_sems(layer):
            return {n: sem(f"{n}{layer}") for n in (
                "qk_turned", "qk_moved", "qk_hi_set", "qk_lo_set", "keys_set", "scores_done", "probs_masked",
                "probs_squared", "probs_set", "probs_turned", "probs_turned_moved", "v_set", "av_done",
                "o_inv_done", "o_done", "o_turned", "o_hi_set", "o_split", "out_done", "residual_done",
                "stats_done", "mv_done", "std_done", "inv_done", "norm_done")}

        first, second = attention_sems(1), attention_sems(2)

        phase2 = ExitStack()

        def sb2(name, shape, dt=f32):
            return phase2.enter_context(nc.sbuf_tensor(name, shape, dt))

        NH = HEADS + KV_HEADS
        ctx_sb = sb2("ctx_sb", [P, T, CTX])
        square_out = sb2("square_out", [P, E])
        mean_sq, rms_in, rms_inv = sb2("mean_sq", [P, 2]), sb2("rms_in", [P, 2]), sb2("rms_inv", [P, 2])
        cross_cos, cross_sin = sb2("cross_cos", [P, NH, D]), sb2("cross_sin", [P, NH, D])
        cross_rot = [sb2(f"cross_rot{n}", [P, 2 * HEADS, D]) for n in range(2)]
        probs_t = sb2("probs_t", [P, PAIRS, P])
        row_max = sb2("row_max", [P, HEADS])
        y_var = sb2("y_var", [P, 1])
        phase2.close()
        squares_q = sem("squares_q")
        (ctx_in, mean_sq_done, rms_in_done, rms_inv_done, cross_cos_done, cross_sin_done, cross_rot_done,
         row_max_done, shifted_done, y_var_done) = (sem(n) for n in (
             "ctx_in", "mean_sq_done", "rms_in_done", "rms_inv_done", "cross_cos_done", "cross_sin_done",
             "cross_rot_done", "row_max_done", "shifted_done", "y_var_done"))

        phase3 = ExitStack()

        def sb3(name, shape, dt=f32):
            return phase3.enter_context(nc.sbuf_tensor(name, shape, dt))

        x_group = sb3("x_group", [P, GROUP_TILES, E])
        xg_hi = [sb3(f"xg_hi{n}", [P, KC, GROUP], f32r) for n in range(2)]
        xg_lo = [sb3(f"xg_lo{n}", [P, KC, GROUP], f32r) for n in range(2)]
        silu_sb = [sb3(f"silu_sb{n}", [P, GROUP]) for n in range(2)]
        h_sb = [sb3(f"h_sb{n}", [P, GROUP]) for n in range(2)]
        h_hi = [sb3(f"h_hi{n}", [P, GROUP], f32r) for n in range(2)]
        h_lo = [sb3(f"h_lo{n}", [P, GROUP], f32r) for n in range(2)]
        acc = sb3("acc", [P, GROUP_TILES, E])
        out_sb = sb3("out_sb", [P, GROUP_TILES, E])
        logits_t = sb3("logits_t", [EXPERTS, GROUP])
        top_logit = sb3("top_logit", [P, GROUP_TILES])
        shifted = sb3("shifted", [P, GROUP_TILES, EXPERTS])
        expd = sb3("expd", [P, GROUP_TILES, EXPERTS])
        best = sb3("best", [P, GROUP_TILES, 8])
        best_at = sb3("best_at", [P, GROUP_TILES, 8], mybir.dt.uint32)
        best_at_f = sb3("best_at_f", [P, GROUP_TILES, 8])
        pair_sum, pair_inv = sb3("pair_sum", [P, GROUP_TILES]), sb3("pair_inv", [P, GROUP_TILES])
        pair_w = sb3("pair_w", [P, GROUP_TILES, 2])
        picked = [sb3(f"picked{n}", [P, GROUP_TILES, EXPERTS]) for n in range(2)]
        combine = [sb3(f"combine{n}", [P, GROUP_TILES, EXPERTS]) for n in range(2)]
        g_stats, g_mv = sb3("g_stats", [P, GROUP_TILES, 6]), sb3("g_mv", [P, GROUP_TILES, 2])
        g_var, g_inv = sb3("g_var", [P, GROUP_TILES]), sb3("g_inv", [P, GROUP_TILES])
        phase3.close()
        (x_copied, x_turned, xg_hi_set, xg_split, logits_t_done, logits_t_moved, logits_done, top_logit_done,
         shifted3_done, exp_done, best_done, best_at_done, best_f_done, pair_sum_done, pair_inv_done,
         pair_w_done, picked_done, combine_done, acc_done, g_stats_done, g_mv_done, g_var_done, g_inv_done,
         out_set, out_stored) = (sem(n) for n in (
             "x_copied", "x_turned", "xg_hi_set", "xg_split", "logits_t_done", "logits_t_moved", "logits_done",
             "top_logit_done", "shifted3_done", "exp_done", "best_done", "best_at_done", "best_f_done",
             "pair_sum_done", "pair_inv_done", "pair_w_done", "picked_done", "combine_done", "acc_done",
             "g_stats_done", "g_mv_done", "g_var_done", "g_inv_done", "out_set", "out_stored"))
        gate_up_done, silu_done, h_done, h_hi_done, h_split, down_done, weighed = (sem(n) for n in (
            "gate_up_done", "silu_done", "h_done", "h_hi_done", "h_split", "down_done", "weighed"))
        bank_gate, bank_up = (bank_qk, bank_tr), (bank_v, bank_s0)
        bank_down = (bank_s1, bank_av)

        def wait_turn(eng, sem, turn, back=0):
            count = turn.n + 1 - back
            if isinstance(count, int) and count <= 0:
                return
            eng.wait_ge(sem, count)

        def wait_stores(eng, turn, back):
            count = 16 * (turn.n + 1 - back)
            if isinstance(count, int) and count <= 0:
                return
            eng.wait_ge(out_stored, count)

        def more(g):
            return not isinstance(g.n, int) or g.n + 1 < GROUPS

        def later(g):
            return not isinstance(g.n, int) or g.n > 0

        def not_last(i):
            return not isinstance(i.n, int) or i.n < GROUPS * EXPERTS

        def after_first(eng):
            eng.wait_ge(first["norm_done"], T)

        def after_second(eng):
            eng.wait_ge(second["norm_done"], T)

        def over_experts(eng, step):
            def groups(first_n):
                for u in range(2):
                    for e in range(EXPERTS):
                        step(Turn((first_n + u) * EXPERTS + e), Turn(first_n + u, u), e)
            groups(0)
            with eng.Fori(2, GROUPS - 3, 2) as base:
                groups(base)
            groups(GROUPS - 2)
            step(Turn(GROUPS * EXPERTS), Turn(GROUPS, 0), 0)


        def alone(eng):
            eng.wait_ge(tables_in, TABLES * 16)

        def dve_split_qk(dve, a, t):
            wait_tile(dve, a["qk_moved"], t)
            wait_tile(dve, a["scores_done"], t, 1)
            dve.tensor_copy(kq_hi[:, :], kq32[:, :]).then_inc(a["qk_hi_set"], 1)
            wait_tile(dve, a["qk_hi_set"], t)
            dve.tensor_tensor(kq_lo[:, :], kq32[:, :], kq_hi[:, :], ALU.subtract).then_inc(a["qk_lo_set"], 1)
            wait_tile(dve, a["qk_lo_set"], t)
            for part, kq in enumerate((kq_hi, kq_lo)):
                for m in range(4):
                    last = dve.tensor_scalar(
                        k_one[:, part, :, :, m, :].rearrange("p c s n -> p (c s) n"),
                        kq[:, 256:512].rearrange("p (cs n) -> p cs n", n=SEQ),
                        quarter_sb[:, m:m + 1], None, ALU.mult)
            last.then_inc(a["keys_set"], 1)

        def dve_o_norm(dve, a, t):
            wait_tile(dve, a["av_done"], t)
            av = bank_av[:, 0:HEADS * VW].rearrange("p (h v) -> p h v", v=VW)
            dve.reciprocal(o_inv[:, :], av[:, :, D]).then_inc(a["o_inv_done"], 1)
            wait_tile(dve, a["o_inv_done"], t)
            wait_tile(dve, a["o_turned"], t, 1)
            dve.tensor_tensor(o_sb[:, :, :], av[:, :, 0:D],
                              o_inv[:, :].unsqueeze(2).broadcast_to([P, HEADS, D]), ALU.mult).then_inc(a["o_done"], 1)

        def dve_o_low(dve, a, t):
            wait_tile(dve, a["o_hi_set"], t)
            wait_tile(dve, a["out_done"], t, 1)
            dve.tensor_tensor(o_lo[:, :, :], bank_ot[:, 0:E].rearrange("p (k n) -> p k n", k=KC),
                              o_hi[:, :, :].bitcast(f32), ALU.subtract).then_inc(a["o_split"], 1)

        def dve_residual(dve, a, t):
            wait_tile(dve, a["out_done"], t)
            wait_tile(dve, a["norm_done"], t, 1)
            dve.tensor_tensor(y_sb[:, :], bank_out[:, 0:E], x_sb[:, t.n, :], ALU.add).then_inc(a["residual_done"], 1)
            wait_tile(dve, a["residual_done"], t)
            dve.bn_stats(y_stats[:, :], y_sb[:, :]).then_inc(a["stats_done"], 1)
            alone(dve)
            wait_tile(dve, a["stats_done"], t)
            dve.bn_aggr(y_mv[:, :], y_stats[:, :]).then_inc(a["mv_done"], 1)

        def dve_normalise(dve, a, t):
            dve.tensor_scalar(x_sb[:, t.n, :], y_sb[:, :], y_mv[:, 0:1], y_inv[:, 0:1],
                              ALU.subtract, ALU.mult).then_inc(a["norm_done"], 1)

        def act_move_qk(act, a, t, scale, bias):
            wait_tile(act, a["qk_turned"], t)
            wait_tile(act, a["qk_lo_set"], t, 1)
            act.activation(kq32[:, :], bank_tr[:, :], ACT.Identity, bias=bias, scale=scale).then_inc(a["qk_moved"], 1)

        def act_o_high(act, a, t):
            wait_tile(act, a["o_turned"], t)
            wait_tile(act, a["out_done"], t, 1)
            act.activation(o_hi[:, :, :], bank_ot[:, 0:E].rearrange("p (k n) -> p k n", k=KC),
                           ACT.Copy).then_inc(a["o_hi_set"], 1)

        def pe_turn(pe, a, t, source):
            for n in range(4):
                last = pe.transpose(bank_tr[:, n * P:(n + 1) * P], source(n), ident[:, :])
            last.then_inc(a["qk_turned"], 1)

        def pe_turn_o(pe, a, t):
            wait_tile(pe, a["o_done"], t)
            wait_tile(pe, a["o_split"], t, 1)
            flat = o_sb[:, :, :].rearrange("p h d -> p (h d)")
            for c in range(KC):
                last = pe.transpose(bank_ot[:, c * P:(c + 1) * P], flat[:, c * P:(c + 1) * P], ident[:, :])
            last.then_inc(a["o_turned"], 1)

        def pe_project(pe, a, t, layer):
            wait_tile(pe, a["o_split"], t)
            wait_tile(pe, a["residual_done"], t, 1)
            passes = [(l, w, c) for l, w in ((o_hi, wo_hi), (o_hi, wo_lo), (o_lo, wo_hi)) for c in range(KC)]
            for n, (l, w, c) in enumerate(passes):
                last = pe.matmul(bank_out[:, 0:E], l[:, c, :], w[:, layer, c, :], start=n == 0,
                                 stop=n == len(passes) - 1)
            last.then_inc(a["out_done"], 1)

        block = stack.enter_context(nc.Block())

        @block.sync
        def _(sp):
            sp.dma_start(wqkv_raw, w_qkv.rearrange("(k p) n -> p k n", p=P)).then_inc(weights_in, 16)
            sp.dma_start(wo_raw[:, 0, :, :], w_out1.rearrange("(k p) n -> p k n", p=P)).then_inc(weights_in, 16)
            sp.dma_start(wo_raw[:, 1, :, :], w_out2_t.rearrange("(k p) n -> p k n", p=P)).then_inc(weights_in, 16)
            sp.dma_start(router_raw[:, :, :], router.rearrange("(k p) n -> p k n", p=P)).then_inc(weights_in, 16)
            for dst, src in ((qw_sb, q_w), (kw_sb, k_w)):
                sp.dma_start(dst[:, :], src.partition_broadcast(P)).then_inc(tables_in, 16)

            def load_xt(t):
                wait_tile(sp, xt_split, t, 4)
                sp.dma_start(xt_raw[t.slot(4)][:, :, :],
                             x_t[:, bass.ds(t.n * P, P)].rearrange("(k p) n -> p k n", p=P)
                             ).then_inc(xt_loaded[t.slot(4)], 16)

            over_tiles(sp, load_xt, 0)
            sp.wait_ge(weights_split, 1)
            for n, w in enumerate((gate_w, up_w)):
                sp.dma_start(ffn_raw[:, n, :, :].rearrange("p e (k f) -> p e k f", k=KC),
                             w.rearrange("e (k p) f -> p e k f", p=P)).then_inc(ffn_in, 16)
            sp.dma_start(ffn_raw[:, 2, :, :], down_w.rearrange("e f n -> f e n")).then_inc(ffn_in, 16)

            outs = out.rearrange("(t p) n -> p t n", p=P)

            def store(i, g, e):
                if e == 0 and later(g):
                    b = g.back(1)
                    wait_turn(sp, out_set, b)
                    sp.dma_start(outs[:, bass.ds(b.n * GROUP_TILES, GROUP_TILES), :], out_sb[:, :, :]).then_inc(out_stored, 16)

            over_experts(sp, store)
            sp.wait_ge(out_stored, 16 * GROUPS)

        @block.gpsimd
        def _(pool):
            pool.memset(eps_sb[:, :], EPS).then_inc(constants_set, 1)
            pool.memset(minus_half[:, :], -0.5).then_inc(constants_set, 1)
            n = 2
            for pair in v_pair:
                for v in pair:
                    pool.memset(v[:, :, :], 0.0).then_inc(constants_set, 1)
                    n += 1
            pool.wait_ge(constants_set, n)
            for pair in v_pair:
                for v in pair:
                    pool.memset(v[0:64, :, D:D + 1], 1.0).then_inc(constants_set, 1)
                    pool.memset(v[64:128, :, VW + D:VW + D + 1], 1.0).then_inc(constants_set, 1)

            def step1(i):
                t = i
                if t.live:
                    wait_tile(pool, xt_hi_set, t)
                    wait_tile(pool, proj_v_done, t, 2)
                    pool.tensor_tensor(xt_lo[t.slot(2)][:, :, :], xt_raw[t.slot(4)][:, :, :],
                                       xt_hi[t.slot(2)][:, :, :].bitcast(f32), ALU.subtract).then_inc(xt_split, 1)
                t = i.back(1)
                if t.live:
                    wait_tile(pool, rope_cos_done, t)
                    wait_tile(pool, rope_sin_done, t)
                    wait_tile(pool, centred_done, t, 1)
                    pool.tensor_tensor(rot[:, :, :], rot_cos[:, :, :], rot_sin[:, :, :], ALU.add).then_inc(rope_sum_done, 1)
                    wait_tile(pool, head_mean_done, t)
                    wait_tile(pool, qk_norm_done, t, 1)
                    pool.tensor_tensor(centred[:, :, :], rot[:, :, :],
                                       head_mean[:, :].unsqueeze(2).broadcast_to([P, 32, D]), ALU.subtract
                                       ).then_inc(centred_done, 1)

            over_tiles(pool, step1, 1)

            after_first(pool)

            def step2(i):
                t = i
                if t.live:
                    wait_tile(pool, mean_sq_done, t)
                    wait_tile(pool, rms_inv_done, t, 1)
                    pool.tensor_tensor(rms_in[:, :], mean_sq[:, :], eps_sb[:, 0:2], ALU.add).then_inc(rms_in_done, 1)
                    wait_tile(pool, rms_in_done, t)
                    wait_tile(pool, cross_sin_done, t, 1)
                    pool.tensor_tensor(rms_inv[:, :], rms_in[:, :], minus_half[:, 0:2], ALU.pow).then_inc(rms_inv_done, 1)
                t = i.back(3)
                if t.live:
                    wait_tile(pool, second["mv_done"], t)
                    wait_tile(pool, second["inv_done"], t, 1)
                    pool.tensor_tensor(y_var[:, :], y_mv[:, 1:2], eps_sb[:, 0:1], ALU.add).then_inc(y_var_done, 1)
                    wait_tile(pool, y_var_done, t)
                    wait_tile(pool, second["norm_done"], t, 1)
                    pool.tensor_tensor(y_inv[:, :], y_var[:, :], minus_half[:, 0:1], ALU.pow).then_inc(second["inv_done"], 1)
                t = i
                if t.live:
                    wait_tile(pool, cross_cos_done, t)
                    wait_tile(pool, cross_sin_done, t)
                    wait_tile(pool, second["qk_turned"], t, 2)
                    rot_t = cross_rot[t.slot(2)]
                    pool.tensor_tensor(rot_t[:, 0:HEADS, :], cross_cos[:, 0:HEADS, :], cross_sin[:, 0:HEADS, :], ALU.add)
                    k_c, k_s = (v[:, HEADS:NH, :].unsqueeze(2).broadcast_to([P, KV_HEADS, HEADS // KV_HEADS, D])
                                for v in (cross_cos, cross_sin))
                    pool.tensor_tensor(rot_t[:, HEADS:2 * HEADS, :].rearrange("p (g r) d -> p g r d", g=KV_HEADS),
                                       k_c, k_s, ALU.add).then_inc(cross_rot_done, 1)

            over_tiles(pool, step2, 3)
            after_second(pool)

            def copy_group(g):
                wait_turn(pool, x_turned, g, 1)
                pool.tensor_copy(x_group[:, :, :], x_sb[:, bass.ds(g.n * GROUP_TILES, GROUP_TILES), :]).then_inc(x_copied, 1)

            copy_group(Turn(0))

            def step3(i, g, e):
                if e == 1 and more(g):
                    copy_group(g.back(-1))
                if e == 0 and later(g):
                    b = g.back(1)
                    wait_turn(pool, g_mv_done, b)
                    wait_turn(pool, g_inv_done, b, 1)
                    pool.tensor_tensor(g_var[:, :], g_mv[:, :, 1], eps_sb[:, :], ALU.add).then_inc(g_var_done, 1)
                    wait_turn(pool, g_var_done, b)
                    wait_turn(pool, out_set, b, 1)
                    pool.tensor_tensor(g_inv[:, :], g_var[:, :], minus_half[:, :], ALU.pow).then_inc(g_inv_done, 1)

            over_experts(pool, step3)

        @block.scalar
        def _(act):
            for dst, src in ((cos_sb, cos_t), (sin_sb, sin_t), (keep_sb, keep_t), (causal_sb, causal_add),
                             (quarter_sb, quarter), (ident, identity), (iota_sb, experts_iota),
                             (scale_sb, ln_scale), (bias_sb, ln_bias)):
                act.dma_start(dst[:, :], src).then_inc(tables_in, 16)
            xs = x.rearrange("(t p) n -> p t n", p=P)
            for n in range(4):
                act.dma_start(x_sb[:, 8 * n:8 * n + 8, :], xs[:, 8 * n:8 * n + 8, :]).then_inc(x_in, 16)
            act.wait_ge(tables_in, TABLES * 16)
            act.wait_ge(weights_in, 4 * 16)
            act.activation(wqkv_hi[:, :, :], wqkv_raw, ACT.Copy).then_inc(wqkv_split_hi, 1)
            act.activation(wo_hi[:, :, :, :], wo_raw[:, :, :, :], ACT.Copy).then_inc(wqkv_split_hi, 1)
            act.activation(router_hi[:, :, :], router_raw[:, :, :], ACT.Copy).then_inc(wqkv_split_hi, 1)
            act.wait_ge(constants_set, 14)

            def step1(i):
                t = i.back(3)
                if t.live:
                    pr = probs[t.slot(2)]
                    wait_tile(act, first["probs_masked"], t)
                    act.activation(pr[:, :], pr[:, :], ACT.Square).then_inc(first["probs_squared"], 1)
                    wait_tile(act, first["probs_squared"], t)
                    act.activation(pr[:, :], pr[:, :], ACT.Square).then_inc(first["probs_set"], 1)
                t = i
                if t.live:
                    act.wait_ge(xt_loaded[t.slot(4)], 4 * (t.n - t.slot(4)) + 16)
                    wait_tile(act, proj_v_done, t, 2)
                    act.activation(xt_hi[t.slot(2)][:, :, :], xt_raw[t.slot(4)][:, :, :], ACT.Copy).then_inc(xt_hi_set, 1)
                t = i.back(2)
                if t.live:
                    act_move_qk(act, first, t, scale_sb[:, 0:1], bias_sb[:, 0:1])
                t = i.back(4)
                if t.live:
                    wait_tile(act, first["mv_done"], t)
                    wait_tile(act, first["norm_done"], t, 1)
                    act.activation(y_std[:, :], y_mv[:, 1:2], ACT.Sqrt, bias=eps_sb[:, 0:1]).then_inc(first["std_done"], 1)
                t = i.back(1)
                if t.live:
                    wait_tile(act, proj_v_done, t)
                    wait_tile(act, first["av_done"], t, 2)
                    for q in range(2):
                        vals = bank_v[64 * q:64 * q + 64, 0:E].rearrange("p (j o d) -> p j o d", o=2, d=D)
                        for o in range(2):
                            last = act.activation(v_pair[t.slot(2)][q][64 * o:64 * o + 64, :, VW * o:VW * o + D],
                                                  vals[:, :, o, :], ACT.Copy)
                    last.then_inc(first["v_set"], 1)
                    wait_tile(act, centred_done, t)
                    wait_tile(act, head_var_done, t, 1)
                    act.activation(centred_sq[:, :, :], centred[:, :, :], ACT.Square).then_inc(centred_sq_done, 1)
                t = i.back(3)
                if t.live:
                    act_o_high(act, first, t)
                t = i.back(1)
                if t.live:
                    wait_tile(act, head_var_done, t)
                    wait_tile(act, head_inv_done, t, 1)
                    act.activation(head_std[:, :], head_var[:, :], ACT.Sqrt, bias=eps_sb[:, 0:1],
                                   scale=1.0 / D).then_inc(head_std_done, 1)

            over_tiles(act, step1, 4)

            after_first(act)
            act.dma_start(ctx_sb[:, :, :], ctx.rearrange("(t p) n -> p t n", p=P)).then_inc(ctx_in, 16)
            act.wait_ge(ffn_in, 48)
            act.activation(ffn_hi[:, :, :, :], ffn_raw[:, :, :, :], ACT.Copy).then_inc(ffn_hi_set, 1)
            act.wait_ge(ctx_in, 16)

            def step2(i):
                t = i
                if t.live:
                    alone(act)
                    wait_tile(act, rms_in_done, t, 1)
                    act.activation(square_out[:, :], x_sb[:, t.n, :], ACT.Square, scale=E ** -0.5,
                                   accum_out=mean_sq[:, 0:1]).then_inc(squares_q, 1)
                    alone(act)
                    wait_tile(act, squares_q, t)
                    act.activation(square_out[:, 0:CTX], ctx_sb[:, t.n, :], ACT.Square, scale=CTX ** -0.5,
                                   accum_out=mean_sq[:, 1:2]).then_inc(mean_sq_done, 1)
                t = i.back(1)
                if t.live:
                    alone(act)
                    wait_tile(act, second["av_done"], t, 2)
                    for q in range(2):
                        vals = ctx_sb[64 * q:64 * q + 64, t.n, :].rearrange("p (g d) -> p g d", d=D)
                        for o in range(2):
                            last = act.activation(v_pair[t.slot(2)][q][64 * o:64 * o + 64, 0:KV_HEADS, VW * o:VW * o + D],
                                                  vals, ACT.Copy)
                    last.then_inc(second["v_set"], 1)
                    act_move_qk(act, second, t, 1.0, 0.0)
                t = i.back(2)
                if t.live:
                    pr = probs[t.slot(2)]
                    wait_tile(act, shifted_done, t)
                    act.activation(pr[:, :], pr[:, :], ACT.Exp, scale=D ** -0.5).then_inc(second["probs_set"], 1)
                    wait_tile(act, second["probs_turned"], t)
                    wait_tile(act, second["av_done"], t, 1)
                    for n, b in enumerate((bank_qk, bank_v)):
                        last = act.activation(probs_t[:, 4 * n:4 * n + 4, :].rearrange("p j q -> p (j q)"), b[:, :], ACT.Copy)
                    last.then_inc(second["probs_turned_moved"], 1)
                    act_o_high(act, second, t)

            over_tiles(act, step2, 3)
            after_second(act)

            def move_group(g):
                wait_turn(act, x_turned, g)
                for k, b in enumerate((bank_ot, bank_out)):
                    last = act.activation(xg_hi[g.parity][:, k, :], b[:, :], ACT.Copy)
                last.then_inc(xg_hi_set, 1)

            def move_logits(g):
                wait_turn(act, logits_t_done, g)
                wait_turn(act, logits_done, g, 1)
                act.activation(logits_t[:, :], bank_ot[0:EXPERTS, :], ACT.Copy).then_inc(logits_t_moved, 1)

            def exp_logits(g):
                wait_turn(act, shifted3_done, g)
                act.activation(expd[:, :, :], shifted[:, :, :], ACT.Exp).then_inc(exp_done, 1)

            move_group(Turn(0))
            move_logits(Turn(0))
            exp_logits(Turn(0))

            def step3(i, g, e):
                if not_last(i):
                    wait_turn(act, gate_up_done, i)
                    wait_turn(act, h_done, i, 2)
                    act.activation(silu_sb[e % 2][:, :], bank_gate[e % 2][:, :], ACT.Silu).then_inc(silu_done, 1)
                    wait_turn(act, h_done, i)
                    wait_turn(act, down_done, i, 2)
                    act.activation(h_hi[e % 2][:, :], h_sb[e % 2][:, :], ACT.Copy).then_inc(h_hi_done, 1)
                if more(g):
                    if e == 3:
                        move_group(g.back(-1))
                    if e == 4:
                        move_logits(g.back(-1))
                    if e == 5:
                        exp_logits(g.back(-1))

            over_experts(act, step3)

        @block.vector
        def _(dve):
            dve.wait_ge(tables_in, TABLES * 16)
            dve.wait_ge(weights_in, 4 * 16)
            dve.wait_ge(wqkv_split_hi, 1)
            dve.tensor_tensor(wqkv_lo[:, :, :], wqkv_raw, wqkv_hi[:, :, :].bitcast(f32), ALU.subtract).then_inc(weights_split, 1)
            dve.wait_ge(wqkv_split_hi, 3)
            dve.tensor_tensor(wo_lo[:, :, :, :], wo_raw[:, :, :, :], wo_hi[:, :, :, :].bitcast(f32), ALU.subtract).then_inc(weights_split, 1)
            dve.tensor_tensor(router_lo[:, :, :], router_raw[:, :, :], router_hi[:, :, :].bitcast(f32), ALU.subtract).then_inc(weights_split, 1)
            for w, w_cos, w_sin, heads in ((qw_sb, q_cos, q_sin, HEADS), (kw_sb, k_cos, k_sin, KV_HEADS)):
                wv = w[:, :].rearrange("p (h d) -> p h d", d=D)
                dve.tensor_tensor(w_cos[:, :, :], wv, cos_sb[:, :].unsqueeze(1).broadcast_to([P, heads, D]), ALU.mult).then_inc(qk_tables_set, 1)
                for lo, hi in ((0, D // 2), (D // 2, 0)):
                    dve.tensor_tensor(w_sin[:, :, lo:lo + 8], wv[:, :, hi:hi + 8],
                                      sin_sb[:, lo:lo + 8].unsqueeze(1).broadcast_to([P, heads, 8]), ALU.mult).then_inc(qk_tables_set, 1)
            dve.wait_ge(x_in, 64)

            def step1(i):
                t = i.back(3)
                if t.live:
                    wait_tile(dve, first["scores_done"], t)
                    wait_tile(dve, first["av_done"], t, 2)
                    for b in range(2):
                        last = dve.tensor_tensor(
                            probs[t.slot(2)][:, 512 * b:512 * b + 512].rearrange("p (n q) -> p n q", q=SEQ),
                            bank_s[b][:, :].rearrange("p (n q) -> p n q", q=SEQ),
                            keep_sb[:, :].unsqueeze(1).broadcast_to([P, 8, SEQ]), ALU.mult)
                    last.then_inc(first["probs_masked"], 1)
                t = i.back(4)
                if t.live:
                    dve_residual(dve, first, t)
                t = i.back(1)
                if t.live:
                    wait_tile(dve, proj_qk_done, t)
                    wait_tile(dve, rope_sum_done, t, 1)
                    qk = bank_qk[:, :].rearrange("p (h d) -> p h d", d=D)
                    dve.tensor_tensor(rot_cos[:, :, :], qk, cos_sb[:, :].unsqueeze(1).broadcast_to([P, 32, D]), ALU.mult).then_inc(rope_cos_done, 1)
                    for lo, hi in ((0, D // 2), (D // 2, 0)):
                        last = dve.tensor_tensor(rot_sin[:, :, lo:lo + 8], qk[:, :, hi:hi + 8],
                                                 sin_sb[:, lo:lo + 8].unsqueeze(1).broadcast_to([P, 32, 8]), ALU.mult)
                    last.then_inc(rope_sin_done, 1)
                t = i.back(4)
                if t.live:
                    wait_tile(dve, first["std_done"], t)
                    dve.reciprocal(y_inv[:, :], y_std[:, :]).then_inc(first["inv_done"], 1)
                t = i.back(2)
                if t.live:
                    dve_split_qk(dve, first, t)
                t = i.back(4)
                if t.live:
                    wait_tile(dve, first["inv_done"], t)
                    dve_normalise(dve, first, t)
                t = i.back(1)
                if t.live:
                    wait_tile(dve, rope_sum_done, t)
                    dve.reduce_sum(head_sum[:, :], rot[:, :, :], axis=AX.X).then_inc(head_sum_done, 1)
                    wait_tile(dve, head_sum_done, t)
                    wait_tile(dve, centred_done, t, 1)
                    dve.tensor_scalar(head_mean[:, :], head_sum[:, :], 1.0 / D, None, ALU.mult).then_inc(head_mean_done, 1)
                t = i.back(3)
                if t.live:
                    dve_o_norm(dve, first, t)
                t = i.back(1)
                if t.live:
                    wait_tile(dve, centred_sq_done, t)
                    wait_tile(dve, head_std_done, t, 1)
                    dve.reduce_sum(head_var[:, :], centred_sq[:, :, :], axis=AX.X).then_inc(head_var_done, 1)
                t = i.back(3)
                if t.live:
                    dve_o_low(dve, first, t)
                t = i.back(1)
                if t.live:
                    wait_tile(dve, head_std_done, t)
                    dve.reciprocal(head_inv[:, :], head_std[:, :]).then_inc(head_inv_done, 1)
                    wait_tile(dve, head_inv_done, t)
                    wait_tile(dve, first["qk_turned"], t, 2)
                    dve.tensor_tensor(qk_norm[t.slot(2)][:, :, :], centred[:, :, :],
                                      head_inv[:, :].unsqueeze(2).broadcast_to([P, 32, D]), ALU.mult).then_inc(qk_norm_done, 1)

            over_tiles(dve, step1, 4)

            after_first(dve)
            dve.wait_ge(ffn_hi_set, 1)
            dve.tensor_tensor(ffn_lo[:, :, :, :], ffn_raw[:, :, :, :], ffn_hi[:, :, :, :].bitcast(f32), ALU.subtract).then_inc(ffn_split, 1)
            dve.wait_ge(qk_tables_set, 6)

            def step2(i):
                t = i.back(2)
                if t.live:
                    pr = probs[t.slot(2)]
                    rows = pr[:, :].rearrange("p (n q) -> p n q", q=SEQ)
                    wait_tile(dve, second["scores_done"], t)
                    wait_tile(dve, second["probs_turned"], t, 2)
                    for b in range(2):
                        last = dve.tensor_tensor(rows[:, 8 * b:8 * b + 8, :],
                                                 bank_s[b][:, :].rearrange("p (n q) -> p n q", q=SEQ),
                                                 causal_sb[:, :].unsqueeze(1).broadcast_to([P, 8, SEQ]), ALU.add)
                    last.then_inc(second["probs_masked"], 1)
                    wait_tile(dve, second["probs_masked"], t)
                    dve.reduce_max(row_max[:, :], rows, axis=AX.X).then_inc(row_max_done, 1)
                    wait_tile(dve, row_max_done, t)
                    dve.tensor_tensor(rows, rows, row_max[:, :].unsqueeze(2).broadcast_to([P, HEADS, SEQ]),
                                      ALU.subtract).then_inc(shifted_done, 1)
                t = i.back(1)
                if t.live:
                    dve_split_qk(dve, second, t)
                t = i.back(3)
                if t.live:
                    dve_residual(dve, second, t)
                t = i
                if t.live:
                    wait_tile(dve, rms_inv_done, t)
                    wait_tile(dve, cross_rot_done, t, 1)
                    xv = x_sb[:, t.n, :].rearrange("p (h d) -> p h d", d=D)
                    cv = ctx_sb[:, t.n, :].rearrange("p (h d) -> p h d", d=D)
                    for src, inv, w_cos, h0, heads in ((xv, rms_inv[:, 0:1], q_cos, 0, HEADS),
                                                       (cv, rms_inv[:, 1:2], k_cos, HEADS, KV_HEADS)):
                        last = dve.scalar_tensor_tensor(cross_cos[:, h0:h0 + heads, :], src, inv, w_cos[:, :, :],
                                                        ALU.mult, ALU.mult)
                    last.then_inc(cross_cos_done, 1)
                    for src, inv, w_sin, h0, heads in ((xv, rms_inv[:, 0:1], q_sin, 0, HEADS),
                                                       (cv, rms_inv[:, 1:2], k_sin, HEADS, KV_HEADS)):
                        for lo, hi in ((0, D // 2), (D // 2, 0)):
                            last = dve.scalar_tensor_tensor(cross_sin[:, h0:h0 + heads, lo:lo + 8], src[:, :, hi:hi + 8], inv,
                                                            w_sin[:, :, lo:lo + 8], ALU.mult, ALU.mult)
                    last.then_inc(cross_sin_done, 1)
                t = i.back(3)
                if t.live:
                    wait_tile(dve, second["inv_done"], t)
                    dve_normalise(dve, second, t)
                t = i.back(2)
                if t.live:
                    dve_o_norm(dve, second, t)
                    dve_o_low(dve, second, t)

            over_tiles(dve, step2, 3)
            after_second(dve)

            def split_group(g):
                wait_turn(dve, xg_hi_set, g)
                for k, b in enumerate((bank_ot, bank_out)):
                    last = dve.tensor_tensor(xg_lo[g.parity][:, k, :], b[:, :], xg_hi[g.parity][:, k, :].bitcast(f32), ALU.subtract)
                last.then_inc(xg_split, 1)

            def shift_logits(g):
                wait_turn(dve, logits_done, g)
                logits = bank_out[:, 0:GROUP_TILES * EXPERTS].rearrange("p (t e) -> p t e", e=EXPERTS)
                dve.reduce_max(top_logit[:, :], logits, axis=AX.X).then_inc(top_logit_done, 1)
                wait_turn(dve, top_logit_done, g)
                wait_turn(dve, exp_done, g, 1)
                dve.tensor_tensor(shifted[:, :, :], logits,
                                  top_logit[:, :].unsqueeze(2).broadcast_to([P, GROUP_TILES, EXPERTS]), ALU.subtract).then_inc(shifted3_done, 1)

            def combine_weights(g):
                alone(dve)
                wait_turn(dve, exp_done, g)
                for j in range(GROUP_TILES):
                    last = dve.max(best[:, j, :], expd[:, j, :])
                last.then_inc(best_done, 1)
                wait_turn(dve, best_done, g)
                dve.tensor_tensor(pair_sum[:, :], best[:, :, 0], best[:, :, 1], ALU.add).then_inc(pair_sum_done, 1)
                for j in range(GROUP_TILES):
                    last = dve.max_index(best_at[:, j, :], best[:, j, :], expd[:, j, :])
                last.then_inc(best_at_done, 1)
                wait_turn(dve, pair_sum_done, g)
                dve.reciprocal(pair_inv[:, :], pair_sum[:, :]).then_inc(pair_inv_done, 1)
                wait_turn(dve, best_at_done, g)
                dve.tensor_copy(best_at_f[:, :, :], best_at[:, :, :]).then_inc(best_f_done, 1)
                wait_turn(dve, pair_inv_done, g)
                dve.tensor_tensor(pair_w[:, :, :], best[:, :, 0:2], pair_inv[:, :].unsqueeze(2).broadcast_to([P, GROUP_TILES, 2]),
                                  ALU.mult).then_inc(pair_w_done, 1)
                wait_turn(dve, best_f_done, g)
                wait_turn(dve, pair_w_done, g)
                for j in range(GROUP_TILES):
                    for r in range(2):
                        last = dve.tensor_scalar(picked[r][:, j, :], iota_sb[:, :], best_at_f[:, j, r:r + 1],
                                                 pair_w[:, j, r:r + 1], ALU.is_equal, ALU.mult)
                last.then_inc(picked_done, 1)
                wait_turn(dve, picked_done, g)
                dve.tensor_tensor(combine[g.parity][:, :, :], picked[0][:, :, :], picked[1][:, :, :], ALU.add).then_inc(combine_done, 1)

            split_group(Turn(0))
            shift_logits(Turn(0))
            combine_weights(Turn(0))

            def weigh(i, g, e):
                wait_turn(dve, down_done, i)
                wait_turn(dve, weighed, i, 1)
                if e == 0:
                    wait_turn(dve, combine_done, g)
                    wait_turn(dve, out_set, g, 1)
                for j in range(GROUP_TILES):
                    onto = x_sb[:, g.n * GROUP_TILES + j, :] if e == 0 else acc[:, j, :]
                    last = dve.scalar_tensor_tensor(acc[:, j, :], bank_down[j // 2][:, j % 2 * E:j % 2 * E + E],
                                                    combine[g.parity][:, j, e:e + 1], onto, ALU.mult, ALU.add)
                last.then_inc(weighed, 1)

            def step3(i, g, e):
                if not_last(i):
                    wait_turn(dve, silu_done, i)
                    wait_turn(dve, h_split, i, 2)
                    dve.tensor_tensor(h_sb[e % 2][:, :], bank_up[e % 2][:, :], silu_sb[e % 2][:, :], ALU.mult).then_inc(h_done, 1)
                if e > 0:
                    weigh(i.back(1), g, e - 1)
                elif later(g):
                    weigh(i.back(1), g.back(1), EXPERTS - 1)
                if not_last(i):
                    wait_turn(dve, h_hi_done, i)
                    wait_turn(dve, down_done, i, 2)
                    dve.tensor_tensor(h_lo[e % 2][:, :], h_sb[e % 2][:, :], h_hi[e % 2][:, :].bitcast(f32), ALU.subtract).then_inc(h_split, 1)
                if e == 0 and later(g):
                    b = g.back(1)
                    wait_turn(dve, weighed, i.back(1))
                    for j in range(GROUP_TILES):
                        last = dve.bn_stats(g_stats[:, j, :], acc[:, j, :])
                    last.then_inc(g_stats_done, 1)
                    alone(dve)
                    wait_turn(dve, g_stats_done, b)
                    for j in range(GROUP_TILES):
                        last = dve.bn_aggr(g_mv[:, j, :], g_stats[:, j, :])
                    last.then_inc(g_mv_done, 1)
                    wait_turn(dve, g_inv_done, b)
                    wait_stores(dve, b, 1)
                    for j in range(GROUP_TILES):
                        last = dve.tensor_scalar(out_sb[:, j, :], acc[:, j, :], g_mv[:, j, 0:1], g_inv[:, j:j + 1],
                                                 ALU.subtract, ALU.mult)
                    last.then_inc(out_set, 1)
                if more(g):
                    if e == 3:
                        split_group(g.back(-1))
                    if e == 5:
                        shift_logits(g.back(-1))
                    if e == 6:
                        combine_weights(g.back(-1))

            over_experts(dve, step3)

        @block.tensor
        def _(pe):
            pe.wait_ge(tables_in, TABLES * 16)
            pe.wait_ge(weights_split, 3)

            def step1(i):
                t = i.back(4)
                if t.live:
                    pe_project(pe, first, t, 0)
                t = i.back(1)
                if t.live:
                    wait_tile(pe, xt_split, t)
                    wait_tile(pe, rope_sin_done, t, 1)
                    hi, lo = xt_hi[t.slot(2)], xt_lo[t.slot(2)]
                    passes = [(l, w, c) for l, w in ((hi, wqkv_hi), (hi, wqkv_lo), (lo, wqkv_hi)) for c in range(KC)]
                    for n, (l, w, c) in enumerate(passes):
                        last = pe.matmul(bank_qk[:, :], l[:, c, :], w[:, c, 0:512], start=n == 0, stop=n == 5)
                    last.then_inc(proj_qk_done, 1)
                    wait_tile(pe, first["v_set"], t, 1)
                    for n, (l, w, c) in enumerate(passes):
                        last = pe.matmul(bank_v[:, 0:E], l[:, c, :], w[:, c, 512:768], start=n == 0, stop=n == 5)
                    last.then_inc(proj_v_done, 1)
                t = i.back(2)
                if t.live:
                    wait_tile(pe, qk_norm_done, t)
                    wait_tile(pe, first["qk_moved"], t, 1)
                    flat = qk_norm[t.slot(2)][:, :, :].rearrange("p h d -> p (h d)")
                    pe_turn(pe, first, t, lambda n: flat[:, n * P:(n + 1) * P])
                t = i.back(3)
                if t.live:
                    wait_tile(pe, first["probs_set"], t)
                    wait_tile(pe, first["v_set"], t)
                    wait_tile(pe, first["o_done"], t, 1)
                    pr = probs[t.slot(2)][:, :].rearrange("p (b q c m n) -> p b q c m n", b=2, q=2, c=2, m=2)
                    for j in range(PAIRS):
                        c, b, m = j // 4, j // 2 % 2, j % 2
                        for q in range(2):
                            last = pe.matmul(bank_av[64 * q:64 * q + 64, 2 * VW * j:2 * VW * (j + 1)],
                                             pr[:, b, q, c, m, :], v_pair[t.slot(2)][q][:, j, :], start=True, stop=True)
                    last.then_inc(first["av_done"], 1)
                t = i.back(2)
                if t.live:
                    wait_tile(pe, first["keys_set"], t)
                    wait_tile(pe, first["probs_masked"], t, 1)
                    for j in range(PAIRS):
                        c, b, m = j // 4, j // 2 % 2, j % 2
                        rows = slice(64 * b, 64 * b + 64)
                        for q in range(2):
                            at = ((q * 2 + c) * 2 + m) * SEQ
                            cols = slice(c * P + q * 64, c * P + q * 64 + 64)
                            for n, (part, kq) in enumerate(((0, kq_hi), (0, kq_lo), (1, kq_hi))):
                                last = pe.matmul(
                                    bank_s[b][:, at:at + SEQ],
                                    k_one[rows, part, c, q, 2 * m:2 * m + 2, :].rearrange("p m n -> p (m n)"),
                                    kq[rows, cols], start=n == 0, stop=n == 2)
                    last.then_inc(first["scores_done"], 1)
                t = i.back(3)
                if t.live:
                    pe_turn_o(pe, first, t)

            over_tiles(pe, step1, 4)

            after_first(pe)

            def step2(i):
                t = i.back(3)
                if t.live:
                    pe_project(pe, second, t, 1)
                t = i.back(1)
                if t.live:
                    wait_tile(pe, cross_rot_done, t)
                    wait_tile(pe, second["qk_moved"], t, 1)
                    flat = cross_rot[t.slot(2)][:, :, :].rearrange("p h d -> p (h d)")
                    pe_turn(pe, second, t, lambda n: flat[:, n * P:(n + 1) * P])
                    alone(pe)
                    wait_tile(pe, second["keys_set"], t)
                    wait_tile(pe, second["probs_masked"], t, 1)
                    for c in range(KC):
                        for q in range(2):
                            cols = slice(c * P + q * 64, c * P + q * 64 + 64)
                            for b in range(2):
                                rows = slice(64 * b, 64 * b + 64)
                                for n, (kq, part) in enumerate(((kq_hi, 0), (kq_hi, 1), (kq_lo, 0))):
                                    last = pe.matmul(bank_s[b][64 * q:64 * q + 64, 256 * c:256 * c + 256],
                                                     kq[rows, cols],
                                                     k_one[rows, part, c, q, :, :].rearrange("p m n -> p (m n)"),
                                                     start=n == 0, stop=n == 2)
                    last.then_inc(second["scores_done"], 1)
                t = i.back(2)
                if t.live:
                    wait_tile(pe, second["probs_set"], t)
                    wait_tile(pe, second["probs_turned_moved"], t, 1)
                    pr = probs[t.slot(2)][:, :].rearrange("p (b c m n) -> p b c m n", b=2, c=2, m=4)
                    for j in range(PAIRS):
                        c, b, m = j // 4, j // 2 % 2, j % 2
                        last = pe.transpose((bank_qk, bank_v)[j // 4][:, j % 4 * P:j % 4 * P + P],
                                            pr[:, b, c, 2 * m:2 * m + 2, :].rearrange("p m n -> p (m n)"), ident[:, :])
                    last.then_inc(second["probs_turned"], 1)
                    wait_tile(pe, second["probs_turned_moved"], t)
                    wait_tile(pe, second["v_set"], t)
                    wait_tile(pe, second["o_done"], t, 1)
                    for j in range(PAIRS):
                        for q in range(2):
                            last = pe.matmul(bank_av[64 * q:64 * q + 64, 2 * VW * j:2 * VW * (j + 1)],
                                             probs_t[:, j, 64 * q:64 * q + 64], v_pair[t.slot(2)][q][:, j // 2, :],
                                             start=True, stop=True)
                    last.then_inc(second["av_done"], 1)
                    pe_turn_o(pe, second, t)

            over_tiles(pe, step2, 3)
            after_second(pe)
            pe.wait_ge(ffn_split, 1)

            def turn_group(g):
                wait_turn(pe, x_copied, g)
                if later(g):
                    wait_turn(pe, shifted3_done, g, 1)
                for k, b in enumerate((bank_ot, bank_out)):
                    for j in range(GROUP_TILES):
                        last = pe.transpose(b[:, j * P:j * P + P], x_group[:, j, k * P:k * P + P], ident[:, :])
                last.then_inc(x_turned, 1)

            def score_group(g):
                wait_turn(pe, xg_split, g)
                hi, lo = xg_hi[g.parity], xg_lo[g.parity]
                passes = [(w, v, k) for w, v in ((router_hi, hi), (router_lo, hi), (router_hi, lo)) for k in range(KC)]
                for n, (w, v, k) in enumerate(passes):
                    last = pe.matmul(bank_ot[0:EXPERTS, :], w[:, k, :], v[:, k, :], start=n == 0, stop=n == 5)
                last.then_inc(logits_t_done, 1)

            def turn_logits(g):
                alone(pe)
                wait_turn(pe, logits_t_moved, g)
                for j in range(GROUP_TILES):
                    last = pe.transpose(bank_out[:, j * EXPERTS:(j + 1) * EXPERTS], logits_t[:, j * P:j * P + P],
                                        ident[0:EXPERTS, 0:EXPERTS])
                last.then_inc(logits_done, 1)

            turn_group(Turn(0))
            score_group(Turn(0))
            turn_logits(Turn(0))

            def down(i, g, e):
                wait_turn(pe, h_split, i)
                wait_turn(pe, weighed, i, 1)
                for j in range(GROUP_TILES):
                    cols = slice(j * P, j * P + P)
                    for n, (h, w) in enumerate(((h_hi, ffn_hi), (h_hi, ffn_lo), (h_lo, ffn_hi))):
                        last = pe.matmul(bank_down[j // 2][:, j % 2 * E:j % 2 * E + E], h[e % 2][:, cols], w[:, 2, e, :],
                                         start=n == 0, stop=n == 2)
                last.then_inc(down_done, 1)

            def step3(i, g, e):
                if not_last(i):
                    wait_turn(pe, h_done, i, 2)
                    hi, lo = xg_hi[g.parity], xg_lo[g.parity]
                    for m, b in enumerate((bank_gate[e % 2], bank_up[e % 2])):
                        passes = [(w, v, k) for w, v in ((ffn_hi, hi), (ffn_lo, hi), (ffn_hi, lo)) for k in range(KC)]
                        for n, (w, v, k) in enumerate(passes):
                            last = pe.matmul(b[:, :], w[:, m, e, k * F:(k + 1) * F], v[:, k, :], start=n == 0, stop=n == 5)
                    last.then_inc(gate_up_done, 1)
                if e > 0:
                    down(i.back(1), g, e - 1)
                elif later(g):
                    down(i.back(1), g.back(1), EXPERTS - 1)
                if more(g):
                    if e == 2:
                        turn_group(g.back(-1))
                    if e == 3:
                        score_group(g.back(-1))
                    if e == 4:
                        turn_logits(g.back(-1))

            over_experts(pe, step3)


def rotary_tables():
    inv = (1.0 / np.float32(10000.0) ** (np.arange(0, D, 2, dtype=np.float32) / np.float32(D))).astype(np.float32)
    angle = np.arange(SEQ, dtype=np.float32)[:, None] * inv[None, :]
    cos, sin = np.cos(angle).astype(np.float32), np.sin(angle).astype(np.float32)
    return np.tile(np.concatenate([cos, cos], 1), (2, 1)), np.tile(np.concatenate([-sin, sin], 1), (2, 1))


def kernel(x, ctx_512, L0_attn_w_qkv, L0_attn_w_out, L0_attn_ln_scale, L0_attn_ln_bias, L0_xattn_q_norm_w,
           L0_xattn_k_norm_w, L0_xattn_w_out, L0_ffn_router_w, L0_ffn_gate_proj, L0_ffn_up_proj, L0_ffn_down_proj):
    import concourse.bacc as bacc
    from concourse.bass_utils import run_bass_kernel_spmd

    flat = np.asarray(x).reshape(TOKENS, E)
    cos, sin = rotary_tables()
    pos = np.arange(P) % SEQ
    keep = (pos[:, None] <= np.arange(SEQ)[None, :]).astype(np.float32)
    causal = np.where(np.arange(SEQ)[None, :] <= pos[:, None], 0.0, -1e30).astype(np.float32)
    quarter = (np.arange(P)[:, None] % 64 // D == np.arange(4)[None, :]).astype(np.float32)
    arrays = {
        "x": flat,
        "x_t": np.ascontiguousarray(flat.T),
        "ctx": np.asarray(ctx_512).reshape(TOKENS, CTX),
        "w_qkv": np.asarray(L0_attn_w_qkv),
        "w_out1": np.asarray(L0_attn_w_out),
        "ln_scale": np.ascontiguousarray(np.tile(np.asarray(L0_attn_ln_scale), P // D).reshape(P, 1)),
        "ln_bias": np.ascontiguousarray(np.tile(np.asarray(L0_attn_ln_bias), P // D).reshape(P, 1)),
        "q_w": np.asarray(L0_xattn_q_norm_w),
        "k_w": np.asarray(L0_xattn_k_norm_w),
        "w_out2_t": np.ascontiguousarray(np.asarray(L0_xattn_w_out).T),
        "router": np.asarray(L0_ffn_router_w),
        "gate_w": np.asarray(L0_ffn_gate_proj),
        "up_w": np.asarray(L0_ffn_up_proj),
        "down_w": np.asarray(L0_ffn_down_proj),
        "cos_t": cos,
        "sin_t": sin,
        "keep_t": keep,
        "causal_add": causal,
        "quarter": quarter,
        "identity": np.eye(P, dtype=np.float32),
        "experts_iota": np.tile(np.arange(EXPERTS, dtype=np.float32), (P, 1)),
    }
    nc = bacc.Bacc("TRN2", target_bir_lowering=False, num_devices=1)
    args = {n: nc.dram_tensor(n, a.shape, mybir.dt.from_np(a.dtype), kind="ExternalInput").ap()
            for n, a in arrays.items()}
    out = nc.dram_tensor("out", (TOKENS, E), mybir.dt.float32, kind="ExternalOutput").ap()
    build_decoder(nc, out=out, **args)
    result = run_bass_kernel_spmd(nc, [arrays], core_ids=[0])
    return result.results[0]["out"].reshape(SEQS, SEQ, E)
```

```python
from contextlib import ExitStack

import numpy as np

import concourse.bass as bass
from concourse import mybir

P = 128
SEQS, SEQ, E = 64, 64, 256
TOKENS = SEQS * SEQ
T = TOKENS // P
CTX = 64
HEADS, D = 16, 16
KV_HEADS = 4
PAIRS = HEADS // 2
EXPERTS, F = 8, 128
KC = E // P
UNROLL = 4
TABLES = 11
LAG1, LAG2, HANDOVER = 6, 6, 1
GROUP_TILES = 4
TAIL = 5
GROUP = GROUP_TILES * P
GROUPS = T // GROUP_TILES
EPS = 1e-5
VW = D + 1


class Tile:

    def __init__(self, n, rest):
        self.n, self.rest = n, rest % UNROLL

    def back(self, k):
        return Tile(self.n - k, self.rest - k)

    def slot(self, slots):
        return self.rest % slots

    @property
    def live(self):
        return not isinstance(self.n, int) or 0 <= self.n < T

    @property
    def first(self):
        return isinstance(self.n, int) and self.n == 0


class Turn:

    def __init__(self, n, parity=0):
        self.n, self.parity = n, parity % 2

    def back(self, k):
        return Turn(self.n - k, self.parity - k)


def over_tiles(eng, first_step, second_step):
    head1, head2 = (-(-lag // UNROLL) * UNROLL for lag in (LAG1, LAG2))
    for i in range(head1):
        first_step(Tile(i, i))
    with eng.Fori(head1, T - UNROLL + 1, UNROLL) as base:
        for u in range(UNROLL):
            first_step(Tile(base + u, u))
    for k in range(HANDOVER + head2):
        if k < LAG1:
            first_step(Tile(T + k, k))
        if k >= HANDOVER:
            second_step(Tile(k - HANDOVER, k - HANDOVER))
    with eng.Fori(head2, T - UNROLL + 1, UNROLL) as base:
        for u in range(UNROLL):
            second_step(Tile(base + u, u))
    for i in range(T, T + LAG2):
        second_step(Tile(i, i))


def at(i, lag, step):
    tile = i.back(lag)
    if tile.live:
        step(tile)


def wait_tile(eng, sem, tile, back=0):
    count = tile.n + 1 - back
    if isinstance(count, int) and count <= 0:
        return
    eng.wait_ge(sem, count)


def build_decoder(nc, x, x_t, ctx, w_qkv, w_out1, ln_scale, ln_bias, q_w, k_w, w_out2_t, router,
                  gate_w, up_w, down_w, cos_t, sin_t, keep_t, causal_add, quarter, identity, experts_iota, out):
    f32, f16, f32r = mybir.dt.float32, mybir.dt.float16, mybir.dt.float32r
    ALU, ACT, AX = mybir.AluOpType, mybir.ActivationFunctionType, mybir.AxisListType

    stack = ExitStack()
    with stack:
        def sb(name, shape, dt=f32):
            return stack.enter_context(nc.sbuf_tensor(name, shape, dt))

        def sem(name):
            return stack.enter_context(nc.semaphore(name))

        def bank(name):
            return stack.enter_context(nc.psum_tensor(name, [P, 512], f32))

        x_sb = sb("x_sb", [P, T, E])
        ffn_raw = sb("ffn_raw", [P, 3, EXPERTS, E])
        wqkv_raw = ffn_raw[:, 0, :, :].rearrange("p e n -> p (e n)")[:, 0:KC * 3 * E].rearrange(
            "p (k n) -> p k n", k=KC)
        router_raw = sb("router_raw", [P, KC, EXPERTS])
        router_hi, router_lo = sb("router_hi", [P, KC, EXPERTS], f32r), sb("router_lo", [P, KC, EXPERTS], f32r)
        cos_sb, sin_sb = sb("cos_sb", [P, D]), sb("sin_sb", [P, D])
        ident = sb("ident", [P, P])
        iota_sb = sb("iota_sb", [P, EXPERTS])
        eps_sb, minus_half = sb("eps_sb", [P, GROUP_TILES]), sb("minus_half", [P, GROUP_TILES])
        attention_memory = ExitStack()
        stack2 = attention_memory

        def sb(name, shape, dt=f32):
            return stack2.enter_context(nc.sbuf_tensor(name, shape, dt))

        wo_raw = sb("wo_raw", [P, 2, KC, E])
        wo_hi, wo_lo = sb("wo_hi", [P, 2, KC, E], f32r), sb("wo_lo", [P, 2, KC, E], f32r)
        keep_sb, causal_sb = sb("keep_sb", [P, SEQ]), sb("causal_sb", [P, SEQ])
        quarter_sb = sb("quarter_sb", [P, 4])
        scale_sb, bias_sb = sb("scale_sb", [P, 1]), sb("bias_sb", [P, 1])
        qw_sb, kw_sb = sb("qw_sb", [P, E]), sb("kw_sb", [P, CTX])
        q_cos, q_sin = sb("q_cos", [P, HEADS, D]), sb("q_sin", [P, HEADS, D])
        k_cos, k_sin = sb("k_cos", [P, KV_HEADS, D]), sb("k_sin", [P, KV_HEADS, D])

        bank_qk, bank_v, bank_tr, bank_s0, bank_s1, bank_av, bank_ot, bank_out = (
            bank(n) for n in ("bank_qk", "bank_v", "bank_tr", "bank_s0", "bank_s1", "bank_av", "bank_ot", "bank_out"))
        bank_s = (bank_s0, bank_s1)

        block_names = ("weights_in", "tables_in", "x_in", "constants_set", "wqkv_split_hi", "weights_split",
                       "qk_tables_set")
        s = {n: sem(n) for n in block_names}
        weights_in, tables_in, x_in, constants_set, wqkv_split_hi, weights_split, qk_tables_set = (
            s[n] for n in block_names)
        ffn_in, ffn_hi_set, ffn_split = sem("ffn_in"), sem("ffn_hi_set"), sem("ffn_split")

        kq32 = sb("kq32", [P, 512])
        kq_parts = [sb(f"kq_parts{n}", [P, 2, 512], f16) for n in range(2)]
        k_one = [sb(f"k_one{n}", [P, 2, KC, 2, 4, SEQ], f16) for n in range(2)]
        probs = [sb(f"probs{n}", [P, 1024]) for n in range(2)]
        v_pair = [[sb(f"v_pair{n}{q}", [P, PAIRS, 2 * VW]) for q in range(2)] for n in range(4)]
        o_inv, o_sb = sb("o_inv", [P, HEADS]), sb("o_sb", [P, HEADS, D])
        o_hi, o_lo = sb("o_hi", [P, KC, P], f32r), sb("o_lo", [P, KC, P], f32r)
        y_sb = sb("y_sb", [P, E])
        y_stats, y_mv, y_inv = sb("y_stats", [P, 6]), sb("y_mv", [P, 2]), sb("y_inv", [P, 1])
        y_std = sb("y_std", [P, 1])

        NH = HEADS + KV_HEADS
        ctx_sb = sb("ctx_sb", [P, T, CTX])
        square_out = sb("square_out", [P, E])
        mean_sq, rms_in, rms_inv = sb("mean_sq", [P, 2]), sb("rms_in", [P, 2]), sb("rms_inv", [P, 2])
        cross_cos, cross_sin = sb("cross_cos", [P, NH, D]), sb("cross_sin", [P, NH, D])
        cross_rot = [sb(f"cross_rot{n}", [P, 2 * HEADS, D]) for n in range(2)]
        probs_t = sb("probs_t", [P, PAIRS, P])
        row_max = sb("row_max", [P, HEADS])
        y_var = sb("y_var", [P, 1])

        phase1 = ExitStack()

        def sb1(name, shape, dt=f32):
            return phase1.enter_context(nc.sbuf_tensor(name, shape, dt))

        xt_raw = [sb1(f"xt_raw{n}", [P, KC, P]) for n in range(4)]
        wqkv_hi, wqkv_lo = sb1("wqkv_hi", [P, KC, 3 * E], f32r), sb1("wqkv_lo", [P, KC, 3 * E], f32r)
        xt_hi = [sb1(f"xt_hi{n}", [P, KC, P], f32r) for n in range(4)]
        xt_lo = [sb1(f"xt_lo{n}", [P, KC, P], f32r) for n in range(4)]
        rot_cos, rot_sin = sb1("rot_cos", [P, 32, D]), sb1("rot_sin", [P, 32, D])
        rot = [sb1(f"rot{n}", [P, 32, D]) for n in range(2)]
        centred, centred_sq = sb1("centred", [P, 32, D]), sb1("centred_sq", [P, 32, D])
        head_sum, head_var = sb1("head_sum", [P, 32]), sb1("head_var", [P, 32])
        head_mean = [sb1(f"head_mean{n}", [P, 32]) for n in range(2)]
        head_std, head_inv = sb1("head_std", [P, 32]), sb1("head_inv", [P, 32])
        qk_norm = [sb1(f"qk_norm{n}", [P, 32, D]) for n in range(2)]
        phase1.close()
        attention_memory.close()

        xt_loaded = [sem(f"xt_loaded{n}") for n in range(4)]
        names1 = ["xt_hi_set", "xt_split", "proj_qk_done", "proj_v_done", "rope_cos_done", "rope_sin_done",
                  "rope_sum_done", "head_sum_done", "head_mean_done", "centred_done", "centred_sq_done",
                  "head_var_done", "head_std_done", "head_inv_done", "qk_norm_done"]
        (xt_hi_set, xt_split, proj_qk_done, proj_v_done, rope_cos_done, rope_sin_done, rope_sum_done,
         head_sum_done, head_mean_done, centred_done, centred_sq_done, head_var_done, head_std_done,
         head_inv_done, qk_norm_done) = (sem(n) for n in names1)

        def attention_sems(layer):
            return {n: sem(f"{n}{layer}") for n in (
                "qk_turned", "qk_hi_set", "qk_lo_set", "keys_set", "scores_done", "probs_masked",
                "probs_squared", "probs_set", "probs_turned", "probs_turned_moved", "v_set", "av_done",
                "o_inv_done", "o_done", "o_turned", "o_hi_set", "o_split", "out_done", "residual_done",
                "stats_done", "mv_done", "std_done", "inv_done", "norm_done")}

        first, second = attention_sems(1), attention_sems(2)

        squares_q = sem("squares_q")
        (ctx_in, mean_sq_done, rms_in_done, rms_inv_done, cross_cos_done, cross_sin_done, cross_rot_done,
         row_max_done, shifted_done, y_var_done) = (sem(n) for n in (
             "ctx_in", "mean_sq_done", "rms_in_done", "rms_inv_done", "cross_cos_done", "cross_sin_done",
             "cross_rot_done", "row_max_done", "shifted_done", "y_var_done"))

        phase3 = ExitStack()

        def sb3(name, shape, dt=f32):
            return phase3.enter_context(nc.sbuf_tensor(name, shape, dt))

        ffn_hi, ffn_lo = sb3("ffn_hi", [P, 3, EXPERTS, E], f32r), sb3("ffn_lo", [P, 3, EXPERTS, E], f32r)
        x_group = sb3("x_group", [P, GROUP_TILES, E])
        xg_hi = [sb3(f"xg_hi{n}", [P, KC, GROUP], f32r) for n in range(2)]
        xg_lo = [sb3(f"xg_lo{n}", [P, KC, GROUP], f32r) for n in range(2)]
        silu_sb = [sb3(f"silu_sb{n}", [P, GROUP]) for n in range(2)]
        h_sb = [sb3(f"h_sb{n}", [P, GROUP]) for n in range(2)]
        h_hi = [sb3(f"h_hi{n}", [P, GROUP], f32r) for n in range(2)]
        h_lo = [sb3(f"h_lo{n}", [P, GROUP], f32r) for n in range(2)]
        acc = [sb3(f"acc{n}", [P, GROUP_TILES, E]) for n in range(2)]
        out_sb = sb3("out_sb", [P, GROUP_TILES, E])
        logits_t = sb3("logits_t", [EXPERTS, GROUP])
        top_logit = sb3("top_logit", [P, GROUP_TILES])
        shifted = sb3("shifted", [P, GROUP_TILES, EXPERTS])
        expd = sb3("expd", [P, GROUP_TILES, EXPERTS])
        best = sb3("best", [P, GROUP_TILES, 8])
        best_at = sb3("best_at", [P, GROUP_TILES, 8], mybir.dt.uint32)
        best_at_f = sb3("best_at_f", [P, GROUP_TILES, 8])
        pair_sum, pair_inv = sb3("pair_sum", [P, GROUP_TILES]), sb3("pair_inv", [P, GROUP_TILES])
        pair_w = sb3("pair_w", [P, GROUP_TILES, 2])
        chosen = [sb3(f"chosen{n}", [P, GROUP_TILES, EXPERTS]) for n in range(2)]
        picked = [sb3(f"picked{n}", [P, GROUP_TILES, EXPERTS]) for n in range(2)]
        combine = [sb3(f"combine{n}", [P, GROUP_TILES, EXPERTS]) for n in range(2)]
        g_stats, g_mv = sb3("g_stats", [P, GROUP_TILES, 6]), sb3("g_mv", [P, GROUP_TILES, 2])
        g_var, g_inv = sb3("g_var", [P, GROUP_TILES]), sb3("g_inv", [P, GROUP_TILES])
        phase3.close()
        (x_copied, x_turned, xg_hi_set, xg_split, logits_t_done, logits_t_moved, logits_done, top_logit_done,
         shifted3_done, exp_done, best_done, best_at_done, best_f_done, pair_sum_done, pair_inv_done,
         pair_w_done, picked_done, combine_done, acc_done, g_stats_done, g_mv_done, g_var_done, g_inv_done,
         out_set, out_stored) = (sem(n) for n in (
             "x_copied", "x_turned", "xg_hi_set", "xg_split", "logits_t_done", "logits_t_moved", "logits_done",
             "top_logit_done", "shifted3_done", "exp_done", "best_done", "best_at_done", "best_f_done",
             "pair_sum_done", "pair_inv_done", "pair_w_done", "picked_done", "combine_done", "acc_done",
             "g_stats_done", "g_mv_done", "g_var_done", "g_inv_done", "out_set", "out_stored"))
        chosen_done = sem("chosen_done")
        gate_done, up_done, silu_done, h_done, h_hi_done, h_split, down_done, weighed = (sem(n) for n in (
            "gate_done", "up_done", "silu_done", "h_done", "h_hi_done", "h_split", "down_done", "weighed"))
        bank_gate, bank_up = bank_qk, bank_v
        bank_down = ((bank_s1, bank_av), (bank_tr, bank_s0))

        def wait_turn(eng, sem, turn, back=0):
            count = turn.n + 1 - back
            if isinstance(count, int) and count <= 0:
                return
            eng.wait_ge(sem, count)

        def wait_stores(eng, turn, back):
            count = 16 * (turn.n + 1 - back)
            if isinstance(count, int) and count <= 0:
                return
            eng.wait_ge(out_stored, count)

        def more(g):
            return not isinstance(g.n, int) or g.n + 1 < GROUPS

        def later(g):
            return not isinstance(g.n, int) or g.n > 0

        def first_group(g):
            return isinstance(g.n, int) and g.n == 0

        def not_last(i):
            return not isinstance(i.n, int) or i.n < GROUPS * EXPERTS

        def after_second(eng):
            eng.wait_ge(second["norm_done"], T)

        def over_experts(eng, step):
            def groups(first_n):
                for u in range(2):
                    for e in range(EXPERTS):
                        step(Turn((first_n + u) * EXPERTS + e), Turn(first_n + u, u), e)
            groups(0)
            with eng.Fori(2, GROUPS - 3, 2) as base:
                groups(base)
            groups(GROUPS - 2)
            for e in range(TAIL):
                step(Turn(GROUPS * EXPERTS + e), Turn(GROUPS, 0), e)


        def alone(eng):
            eng.wait_ge(tables_in, TABLES * 16)

        def wait_before(eng, name, a, t, back=1):
            if a is second and isinstance(t.n, int) and t.n < back:
                eng.wait_ge(first[name], T + t.n + 1 - back)
            else:
                wait_tile(eng, a[name], t, back)

        def low_qk(eng, a, t):
            parts = kq_parts[t.slot(2)]
            wait_tile(eng, a["qk_hi_set"], t)
            wait_before(eng, "scores_done", a, t, 2)
            eng.tensor_tensor(parts[:, 1, :], kq32[:, :], parts[:, 0, :], ALU.subtract).then_inc(a["qk_lo_set"], 1)

        def dve_set_keys(dve, a, t):
            wait_tile(dve, a["qk_lo_set"], t)
            wait_before(dve, "scores_done", a, t, 2)
            for m in range(4):
                last = dve.tensor_scalar(
                    k_one[t.slot(2)][:, :, :, :, m, :].rearrange("p w c s n -> p w (c s) n"),
                    kq_parts[t.slot(2)][:, :, 256:512].rearrange("p w (cs n) -> p w cs n", n=SEQ),
                    quarter_sb[:, m:m + 1], None, ALU.mult)
            last.then_inc(a["keys_set"], 1)

        def dve_o_inverse(dve, a, t):
            wait_tile(dve, a["av_done"], t)
            wait_before(dve, "o_done", a, t)
            av = bank_av[:, 0:HEADS * VW].rearrange("p (h v) -> p h v", v=VW)
            dve.reciprocal(o_inv[:, :], av[:, :, D]).then_inc(a["o_inv_done"], 1)

        def dve_o_norm(dve, a, t):
            wait_tile(dve, a["o_inv_done"], t)
            wait_before(dve, "o_turned", a, t)
            av = bank_av[:, 0:HEADS * VW].rearrange("p (h v) -> p h v", v=VW)
            dve.tensor_tensor(o_sb[:, :, :], av[:, :, 0:D],
                              o_inv[:, :].unsqueeze(2).broadcast_to([P, HEADS, D]), ALU.mult).then_inc(a["o_done"], 1)

        def dve_o_low(dve, a, t):
            wait_tile(dve, a["o_hi_set"], t)
            wait_before(dve, "out_done", a, t)
            dve.tensor_tensor(o_lo[:, :, :], bank_ot[:, 0:E].rearrange("p (k n) -> p k n", k=KC),
                              o_hi[:, :, :].bitcast(f32), ALU.subtract).then_inc(a["o_split"], 1)

        def dve_residual(dve, a, t):
            wait_tile(dve, a["out_done"], t)
            wait_before(dve, "norm_done", a, t)
            dve.tensor_tensor(y_sb[:, :], bank_out[:, 0:E], x_sb[:, t.n, :], ALU.add).then_inc(a["residual_done"], 1)

        def dve_statistics(dve, a, t):
            wait_tile(dve, a["residual_done"], t)
            dve.bn_stats(y_stats[:, :], y_sb[:, :]).then_inc(a["stats_done"], 1)

        def dve_variance(dve, a, t):
            alone(dve)
            wait_tile(dve, a["stats_done"], t)
            dve.bn_aggr(y_mv[:, :], y_stats[:, :]).then_inc(a["mv_done"], 1)

        def dve_normalise(dve, a, t):
            wait_tile(dve, a["inv_done"], t)
            dve.tensor_scalar(x_sb[:, t.n, :], y_sb[:, :], y_mv[:, 0:1], y_inv[:, 0:1],
                              ALU.subtract, ALU.mult).then_inc(a["norm_done"], 1)

        def act_move_qk(act, a, t, scale, bias):
            wait_tile(act, a["qk_turned"], t)
            wait_before(act, "qk_lo_set", a, t)
            act.activation(kq32[:, :], bank_tr[:, :], ACT.Identity, bias=bias, scale=scale)
            wait_before(act, "scores_done", a, t, 2)
            act.activation(kq_parts[t.slot(2)][:, 0, :], bank_tr[:, :], ACT.Identity, bias=bias,
                           scale=scale).then_inc(a["qk_hi_set"], 1)

        def act_o_high(act, a, t):
            wait_tile(act, a["o_turned"], t)
            wait_before(act, "out_done", a, t)
            act.activation(o_hi[:, :, :], bank_ot[:, 0:E].rearrange("p (k n) -> p k n", k=KC),
                           ACT.Copy).then_inc(a["o_hi_set"], 1)

        def pe_turn(pe, a, t, source):
            for n in range(4):
                last = pe.transpose(bank_tr[:, n * P:(n + 1) * P], source(n), ident[:, :])
            last.then_inc(a["qk_turned"], 1)

        def pe_turn_o(pe, a, t):
            wait_tile(pe, a["o_done"], t)
            wait_before(pe, "o_split", a, t)
            flat = o_sb[:, :, :].rearrange("p h d -> p (h d)")
            for c in range(KC):
                last = pe.transpose(bank_ot[:, c * P:(c + 1) * P], flat[:, c * P:(c + 1) * P], ident[:, :])
            last.then_inc(a["o_turned"], 1)

        def pe_project(pe, a, t, layer):
            wait_tile(pe, a["o_split"], t)
            wait_before(pe, "residual_done", a, t)
            passes = [(l, w, c) for l, w in ((o_hi, wo_hi), (o_hi, wo_lo), (o_lo, wo_hi)) for c in range(KC)]
            for n, (l, w, c) in enumerate(passes):
                last = pe.matmul(bank_out[:, 0:E], l[:, c, :], w[:, layer, c, :], start=n == 0,
                                 stop=n == len(passes) - 1)
            last.then_inc(a["out_done"], 1)

        block = stack.enter_context(nc.Block())

        @block.sync
        def _(sp):
            sp.dma_start(wqkv_raw, w_qkv.rearrange("(k p) n -> p k n", p=P)).then_inc(weights_in, 16)
            sp.dma_start(wo_raw[:, 0, :, :], w_out1.rearrange("(k p) n -> p k n", p=P)).then_inc(weights_in, 16)
            sp.dma_start(wo_raw[:, 1, :, :], w_out2_t.rearrange("(k p) n -> p k n", p=P)).then_inc(weights_in, 16)
            sp.dma_start(router_raw[:, :, :], router.rearrange("(k p) n -> p k n", p=P)).then_inc(weights_in, 16)
            for dst, src in ((qw_sb, q_w), (kw_sb, k_w)):
                sp.dma_start(dst[:, :], src.partition_broadcast(P)).then_inc(tables_in, 16)

            def load_xt(t):
                if not t.live:
                    return
                wait_tile(sp, xt_split, t, 4)
                sp.dma_start(xt_raw[t.slot(4)][:, :, :],
                             x_t[:, bass.ds(t.n * P, P)].rearrange("(k p) n -> p k n", p=P)
                             ).then_inc(xt_loaded[t.slot(4)], 16)

            over_tiles(sp, load_xt, lambda t: None)
            sp.wait_ge(weights_split, 1)
            for n, w in enumerate((gate_w, up_w)):
                sp.dma_start(ffn_raw[:, n, :, :].rearrange("p e (k f) -> p e k f", k=KC),
                             w.rearrange("e (k p) f -> p e k f", p=P)).then_inc(ffn_in, 16)
            sp.dma_start(ffn_raw[:, 2, :, :], down_w.rearrange("e f n -> f e n")).then_inc(ffn_in, 16)

            outs = out.rearrange("(t p) n -> p t n", p=P)

            def store(i, g, e):
                if e == 4 and later(g):
                    b = g.back(1)
                    wait_turn(sp, out_set, b)
                    sp.dma_start(outs[:, bass.ds(b.n * GROUP_TILES, GROUP_TILES), :], out_sb[:, :, :]).then_inc(out_stored, 16)

            over_experts(sp, store)
            sp.wait_ge(out_stored, 16 * GROUPS)

        @block.gpsimd
        def _(pool):
            pool.memset(eps_sb[:, :], EPS).then_inc(constants_set, 1)
            pool.memset(minus_half[:, :], -0.5).then_inc(constants_set, 1)
            n = 2
            for pair in v_pair:
                for v in pair:
                    pool.memset(v[:, :, :], 0.0).then_inc(constants_set, 1)
                    n += 1
            pool.wait_ge(constants_set, n)
            for pair in v_pair:
                for v in pair:
                    pool.memset(v[0:64, :, D:D + 1], 1.0).then_inc(constants_set, 1)
                    pool.memset(v[64:128, :, VW + D:VW + D + 1], 1.0).then_inc(constants_set, 1)

            def low_xt(t):
                wait_tile(pool, xt_hi_set, t)
                wait_tile(pool, proj_v_done, t, 4)
                pool.tensor_tensor(xt_lo[t.slot(4)][:, :, :], xt_raw[t.slot(4)][:, :, :],
                                   xt_hi[t.slot(4)][:, :, :].bitcast(f32), ALU.subtract).then_inc(xt_split, 1)

            def add_rotary(t):
                wait_tile(pool, rope_sin_done, t)
                wait_tile(pool, centred_done, t, 2)
                wait_tile(pool, head_sum_done, t, 2)
                pool.tensor_tensor(rot[t.slot(2)][:, :, :], rot_cos[:, :, :], rot_sin[:, :, :], ALU.add).then_inc(rope_sum_done, 1)

            def centre(t):
                wait_tile(pool, head_mean_done, t)
                wait_tile(pool, qk_norm_done, t, 1)
                pool.tensor_tensor(centred[:, :, :], rot[t.slot(2)][:, :, :],
                                   head_mean[t.slot(2)][:, :].unsqueeze(2).broadcast_to([P, 32, D]), ALU.subtract
                                   ).then_inc(centred_done, 1)

            def scale_heads(t):
                wait_tile(pool, head_inv_done, t)
                wait_tile(pool, first["qk_turned"], t, 2)
                pool.tensor_tensor(qk_norm[t.slot(2)][:, :, :], centred[:, :, :],
                                   head_inv[:, :].unsqueeze(2).broadcast_to([P, 32, D]), ALU.mult).then_inc(qk_norm_done, 1)

            def mask(t):
                pr = probs[t.slot(2)][:, :].rearrange("p (n q) -> p n q", q=SEQ)
                wait_tile(pool, first["probs_squared"], t)
                pool.tensor_tensor(pr, pr, keep_sb[:, :].unsqueeze(1).broadcast_to([P, HEADS, SEQ]),
                                   ALU.mult).then_inc(first["probs_masked"], 1)

            def step1(i):
                at(i, 0, low_xt)
                at(i, 1, centre)
                at(i, 4, mask)
                at(i, 0, add_rotary)
                at(i, 1, scale_heads)

            def rms_sum(t):
                wait_tile(pool, mean_sq_done, t)
                wait_tile(pool, rms_inv_done, t, 1)
                pool.tensor_tensor(rms_in[:, :], mean_sq[:, :], eps_sb[:, 0:2], ALU.add).then_inc(rms_in_done, 1)

            def rms_root(t):
                wait_tile(pool, rms_in_done, t)
                wait_tile(pool, cross_sin_done, t, 1)
                pool.tensor_tensor(rms_inv[:, :], rms_in[:, :], minus_half[:, 0:2], ALU.pow).then_inc(rms_inv_done, 1)

            def add_cross_rotary(t):
                wait_tile(pool, cross_sin_done, t)
                wait_tile(pool, second["qk_turned"], t, 2)
                rot_t = cross_rot[t.slot(2)]
                pool.tensor_tensor(rot_t[:, 0:HEADS, :], cross_cos[:, 0:HEADS, :], cross_sin[:, 0:HEADS, :], ALU.add)
                k_c, k_s = (v[:, HEADS:NH, :].unsqueeze(2).broadcast_to([P, KV_HEADS, HEADS // KV_HEADS, D])
                            for v in (cross_cos, cross_sin))
                pool.tensor_tensor(rot_t[:, HEADS:2 * HEADS, :].rearrange("p (g r) d -> p g r d", g=KV_HEADS),
                                   k_c, k_s, ALU.add).then_inc(cross_rot_done, 1)

            def shift(t):
                rows = probs[t.slot(2)][:, :].rearrange("p (n q) -> p n q", q=SEQ)
                wait_tile(pool, row_max_done, t)
                pool.tensor_tensor(rows, rows, row_max[:, :].unsqueeze(2).broadcast_to([P, HEADS, SEQ]),
                                   ALU.subtract).then_inc(shifted_done, 1)

            def variance(t):
                wait_tile(pool, second["mv_done"], t)
                wait_tile(pool, second["inv_done"], t, 1)
                pool.tensor_tensor(y_var[:, :], y_mv[:, 1:2], eps_sb[:, 0:1], ALU.add).then_inc(y_var_done, 1)

            def inverse_std(t):
                wait_tile(pool, y_var_done, t)
                wait_before(pool, "norm_done", second, t)
                pool.tensor_tensor(y_inv[:, :], y_var[:, :], minus_half[:, 0:1], ALU.pow).then_inc(second["inv_done"], 1)

            def step2(i):
                at(i, 0, rms_sum)
                at(i, 0, rms_root)
                at(i, 3, shift)
                at(i, 0, add_cross_rotary)
                at(i, 1, lambda t: low_qk(pool, second, t))
                at(i, 5, variance)
                at(i, 5, inverse_std)

            over_tiles(pool, step1, step2)
            after_second(pool)

            def copy_group(g):
                wait_turn(pool, x_turned, g, 1)
                pool.tensor_copy(x_group[:, :, :], x_sb[:, bass.ds(g.n * GROUP_TILES, GROUP_TILES), :]).then_inc(x_copied, 1)

            copy_group(Turn(0))

            def step3(i, g, e):
                if e == 0 and more(g):
                    copy_group(g.back(-1))
                if e == 2 and later(g):
                    b = g.back(1)
                    wait_turn(pool, g_mv_done, b)
                    wait_turn(pool, g_inv_done, b, 1)
                    pool.tensor_tensor(g_var[:, :], g_mv[:, :, 1], eps_sb[:, :], ALU.add).then_inc(g_var_done, 1)
                    wait_turn(pool, g_var_done, b)
                    wait_turn(pool, out_set, b, 1)
                    pool.tensor_tensor(g_inv[:, :], g_var[:, :], minus_half[:, :], ALU.pow).then_inc(g_inv_done, 1)

            over_experts(pool, step3)

        @block.scalar
        def _(act):
            for dst, src in ((cos_sb, cos_t), (sin_sb, sin_t), (keep_sb, keep_t), (causal_sb, causal_add),
                             (quarter_sb, quarter), (ident, identity), (iota_sb, experts_iota),
                             (scale_sb, ln_scale), (bias_sb, ln_bias)):
                act.dma_start(dst[:, :], src).then_inc(tables_in, 16)
            xs = x.rearrange("(t p) n -> p t n", p=P)
            for n in range(4):
                act.dma_start(x_sb[:, 8 * n:8 * n + 8, :], xs[:, 8 * n:8 * n + 8, :]).then_inc(x_in, 16)
            act.wait_ge(tables_in, TABLES * 16)
            act.wait_ge(weights_in, 4 * 16)
            act.activation(wqkv_hi[:, :, :], wqkv_raw, ACT.Copy).then_inc(wqkv_split_hi, 1)
            act.activation(wo_hi[:, :, :, :], wo_raw[:, :, :, :], ACT.Copy).then_inc(wqkv_split_hi, 1)
            act.activation(router_hi[:, :, :], router_raw[:, :, :], ACT.Copy).then_inc(wqkv_split_hi, 1)
            act.wait_ge(constants_set, 26)

            act.dma_start(ctx_sb[:, :, :], ctx.rearrange("(t p) n -> p t n", p=P)).then_inc(ctx_in, 16)

            def high_xt(t):
                act.wait_ge(xt_loaded[t.slot(4)], 4 * (t.n - t.slot(4)) + 16)
                wait_tile(act, proj_v_done, t, 4)
                act.activation(xt_hi[t.slot(4)][:, :, :], xt_raw[t.slot(4)][:, :, :], ACT.Copy).then_inc(xt_hi_set, 1)

            def square_centred(t):
                wait_tile(act, centred_done, t)
                wait_tile(act, head_var_done, t, 1)
                act.activation(centred_sq[:, :, :], centred[:, :, :], ACT.Square).then_inc(centred_sq_done, 1)

            def head_std_root(t):
                wait_tile(act, head_var_done, t)
                wait_tile(act, head_inv_done, t, 1)
                act.activation(head_std[:, :], head_var[:, :], ACT.Sqrt, bias=eps_sb[:, 0:1],
                               scale=1.0 / D).then_inc(head_std_done, 1)

            def set_values(t):
                wait_tile(act, proj_v_done, t)
                wait_tile(act, first["av_done"], t, 4)
                for q in range(2):
                    vals = bank_v[64 * q:64 * q + 64, 0:E].rearrange("p (j o d) -> p j o d", o=2, d=D)
                    for o in range(2):
                        last = act.activation(v_pair[t.slot(4)][q][64 * o:64 * o + 64, :, VW * o:VW * o + D],
                                              vals[:, :, o, :], ACT.Copy)
                last.then_inc(first["v_set"], 1)

            def square_scores(t):
                wait_tile(act, first["scores_done"], t)
                wait_tile(act, first["av_done"], t, 2)
                for b in range(2):
                    last = act.activation(probs[t.slot(2)][:, 512 * b:512 * b + 512], bank_s[b][:, :], ACT.Square)
                last.then_inc(first["probs_squared"], 1)

            def square_masked(t):
                pr = probs[t.slot(2)]
                wait_tile(act, first["probs_masked"], t)
                act.activation(pr[:, :], pr[:, :], ACT.Square).then_inc(first["probs_set"], 1)

            def y_root(t):
                wait_tile(act, first["mv_done"], t)
                wait_tile(act, first["inv_done"], t, 1)
                act.activation(y_std[:, :], y_mv[:, 1:2], ACT.Sqrt, bias=eps_sb[:, 0:1]).then_inc(first["std_done"], 1)

            def step1(i):
                at(i, 0, high_xt)
                at(i, 1, set_values)
                at(i, 2, lambda t: act_move_qk(act, first, t, scale_sb[:, 0:1], bias_sb[:, 0:1]))
                at(i, 1, square_centred)
                at(i, 6, y_root)
                at(i, 5, lambda t: act_o_high(act, first, t))
                at(i, 4, square_masked)
                at(i, 1, head_std_root)
                at(i, 3, square_scores)

            def square_inputs(t):
                if t.first:
                    act.wait_ge(ctx_in, 16)
                act.wait_ge(first["norm_done"], t.n + 1 if isinstance(t.n, int) else T)
                wait_tile(act, rms_in_done, t, 1)
                act.activation(square_out[:, :], x_sb[:, t.n, :], ACT.Square, scale=E ** -0.5,
                               accum_out=mean_sq[:, 0:1]).then_inc(squares_q, 1)
                alone(act)
                wait_tile(act, squares_q, t)
                act.activation(square_out[:, 0:CTX], ctx_sb[:, t.n, :], ACT.Square, scale=CTX ** -0.5,
                               accum_out=mean_sq[:, 1:2]).then_inc(mean_sq_done, 1)

            def set_context_values(t):
                alone(act)
                wait_before(act, "av_done", second, t, 4)
                for q in range(2):
                    vals = ctx_sb[64 * q:64 * q + 64, t.n, :].rearrange("p (g d) -> p g d", d=D)
                    for o in range(2):
                        last = act.activation(v_pair[t.slot(4)][q][64 * o:64 * o + 64, 0:KV_HEADS, VW * o:VW * o + D],
                                              vals, ACT.Copy)
                last.then_inc(second["v_set"], 1)

            def move_probs(t):
                wait_tile(act, second["probs_turned"], t)
                wait_tile(act, second["av_done"], t, 1)
                for n, b in enumerate((bank_qk, bank_v)):
                    last = act.activation(probs_t[:, 4 * n:4 * n + 4, :].rearrange("p j q -> p (j q)"), b[:, :], ACT.Copy)
                last.then_inc(second["probs_turned_moved"], 1)

            def exponentials(t):
                pr = probs[t.slot(2)]
                wait_tile(act, shifted_done, t)
                act.activation(pr[:, :], pr[:, :], ACT.Exp, scale=D ** -0.5).then_inc(second["probs_set"], 1)

            def step2(i):
                at(i, 0, square_inputs)
                at(i, 1, lambda t: act_move_qk(act, second, t, 1.0, 0.0))
                at(i, 3, exponentials)
                at(i, 3, move_probs)
                at(i, 0, set_context_values)
                at(i, 4, lambda t: act_o_high(act, second, t))

            over_tiles(act, step1, step2)
            after_second(act)
            act.wait_ge(ffn_in, 48)

            def split_expert(e):
                act.activation(ffn_hi[:, :, e, :], ffn_raw[:, :, e, :], ACT.Copy).then_inc(ffn_hi_set, 1)

            def move_group(g):
                wait_turn(act, x_turned, g)
                for k, b in enumerate((bank_ot, bank_out)):
                    last = act.activation(xg_hi[g.parity][:, k, :], b[:, :], ACT.Copy)
                last.then_inc(xg_hi_set, 1)

            def move_logits(g):
                wait_turn(act, logits_t_done, g)
                wait_turn(act, logits_done, g, 1)
                act.activation(logits_t[:, :], bank_ot[0:EXPERTS, :], ACT.Copy).then_inc(logits_t_moved, 1)

            def exp_logits(g):
                wait_turn(act, shifted3_done, g)
                act.activation(expd[:, :, :], shifted[:, :, :], ACT.Exp).then_inc(exp_done, 1)

            split_expert(0)
            move_group(Turn(0))
            move_logits(Turn(0))
            exp_logits(Turn(0))

            def step3(i, g, e):
                if first_group(g) and e + 1 < EXPERTS:
                    split_expert(e + 1)
                if not_last(i):
                    wait_turn(act, gate_done, i)
                    wait_turn(act, h_done, i, 2)
                    act.activation(silu_sb[e % 2][:, :], bank_gate[:, :], ACT.Silu).then_inc(silu_done, 1)
                    wait_turn(act, h_done, i)
                    wait_turn(act, down_done, i, 2)
                    act.activation(h_hi[e % 2][:, :], h_sb[e % 2][:, :], ACT.Copy).then_inc(h_hi_done, 1)
                if more(g):
                    if e == 2:
                        move_group(g.back(-1))
                    if e == 4:
                        move_logits(g.back(-1))
                    if e == 6:
                        exp_logits(g.back(-1))

            over_experts(act, step3)

        @block.vector
        def _(dve):
            dve.wait_ge(tables_in, TABLES * 16)
            dve.wait_ge(weights_in, 4 * 16)
            dve.wait_ge(wqkv_split_hi, 1)
            dve.tensor_tensor(wqkv_lo[:, :, :], wqkv_raw, wqkv_hi[:, :, :].bitcast(f32), ALU.subtract).then_inc(weights_split, 1)
            dve.wait_ge(wqkv_split_hi, 3)
            dve.tensor_tensor(wo_lo[:, :, :, :], wo_raw[:, :, :, :], wo_hi[:, :, :, :].bitcast(f32), ALU.subtract).then_inc(weights_split, 1)
            dve.tensor_tensor(router_lo[:, :, :], router_raw[:, :, :], router_hi[:, :, :].bitcast(f32), ALU.subtract).then_inc(weights_split, 1)
            for w, w_cos, w_sin, heads in ((qw_sb, q_cos, q_sin, HEADS), (kw_sb, k_cos, k_sin, KV_HEADS)):
                wv = w[:, :].rearrange("p (h d) -> p h d", d=D)
                dve.tensor_tensor(w_cos[:, :, :], wv, cos_sb[:, :].unsqueeze(1).broadcast_to([P, heads, D]), ALU.mult).then_inc(qk_tables_set, 1)
                for lo, hi in ((0, D // 2), (D // 2, 0)):
                    dve.tensor_tensor(w_sin[:, :, lo:lo + 8], wv[:, :, hi:hi + 8],
                                      sin_sb[:, lo:lo + 8].unsqueeze(1).broadcast_to([P, heads, 8]), ALU.mult).then_inc(qk_tables_set, 1)
            dve.wait_ge(x_in, 64)

            dve.wait_ge(qk_tables_set, 6)

            def rotate(t):
                wait_tile(dve, proj_qk_done, t)
                wait_tile(dve, rope_sum_done, t, 1)
                qk = bank_qk[:, :].rearrange("p (h d) -> p h d", d=D)
                dve.tensor_tensor(rot_cos[:, :, :], qk, cos_sb[:, :].unsqueeze(1).broadcast_to([P, 32, D]), ALU.mult)
                for lo, hi in ((0, D // 2), (D // 2, 0)):
                    last = dve.tensor_tensor(rot_sin[:, :, lo:lo + 8], qk[:, :, hi:hi + 8],
                                             sin_sb[:, lo:lo + 8].unsqueeze(1).broadcast_to([P, 32, 8]), ALU.mult)
                last.then_inc(rope_sin_done, 1)

            def sum_heads(t):
                wait_tile(dve, rope_sum_done, t)
                dve.reduce_sum(head_sum[:, :], rot[t.slot(2)][:, :, :], axis=AX.X).then_inc(head_sum_done, 1)

            def mean_heads(t):
                wait_tile(dve, head_sum_done, t)
                wait_tile(dve, centred_done, t, 2)
                dve.tensor_scalar(head_mean[t.slot(2)][:, :], head_sum[:, :], 1.0 / D, None, ALU.mult).then_inc(head_mean_done, 1)

            def sum_squares(t):
                wait_tile(dve, centred_sq_done, t)
                wait_tile(dve, head_std_done, t, 1)
                dve.reduce_sum(head_var[:, :], centred_sq[:, :, :], axis=AX.X).then_inc(head_var_done, 1)

            def invert_head_std(t):
                wait_tile(dve, head_std_done, t)
                wait_tile(dve, qk_norm_done, t, 1)
                dve.reciprocal(head_inv[:, :], head_std[:, :]).then_inc(head_inv_done, 1)

            def invert_y_std(t):
                wait_tile(dve, first["std_done"], t)
                wait_tile(dve, first["norm_done"], t, 1)
                dve.reciprocal(y_inv[:, :], y_std[:, :]).then_inc(first["inv_done"], 1)

            def step1(i):
                at(i, 5, lambda t: dve_o_inverse(dve, first, t))
                at(i, 1, mean_heads)
                at(i, 3, lambda t: dve_set_keys(dve, first, t))
                at(i, 5, lambda t: dve_o_norm(dve, first, t))
                at(i, 6, lambda t: dve_residual(dve, first, t))
                at(i, 6, lambda t: dve_statistics(dve, first, t))
                at(i, 6, lambda t: dve_variance(dve, first, t))
                at(i, 0, rotate)
                at(i, 1, sum_squares)
                at(i, 2, lambda t: low_qk(dve, first, t))
                at(i, 6, invert_y_std)
                at(i, 1, invert_head_std)
                at(i, 6, lambda t: dve_normalise(dve, first, t))
                at(i, 5, lambda t: dve_o_low(dve, first, t))
                at(i, 0, sum_heads)

            def rotate_cross(t):
                wait_tile(dve, rms_inv_done, t)
                wait_tile(dve, cross_rot_done, t, 1)
                xv = x_sb[:, t.n, :].rearrange("p (h d) -> p h d", d=D)
                cv = ctx_sb[:, t.n, :].rearrange("p (h d) -> p h d", d=D)
                for src, inv, w_cos, h0, heads in ((xv, rms_inv[:, 0:1], q_cos, 0, HEADS),
                                                   (cv, rms_inv[:, 1:2], k_cos, HEADS, KV_HEADS)):
                    dve.scalar_tensor_tensor(cross_cos[:, h0:h0 + heads, :], src, inv, w_cos[:, :, :],
                                             ALU.mult, ALU.mult)
                for src, inv, w_sin, h0, heads in ((xv, rms_inv[:, 0:1], q_sin, 0, HEADS),
                                                   (cv, rms_inv[:, 1:2], k_sin, HEADS, KV_HEADS)):
                    for lo, hi in ((0, D // 2), (D // 2, 0)):
                        last = dve.scalar_tensor_tensor(cross_sin[:, h0:h0 + heads, lo:lo + 8], src[:, :, hi:hi + 8], inv,
                                                        w_sin[:, :, lo:lo + 8], ALU.mult, ALU.mult)
                last.then_inc(cross_sin_done, 1)

            def mask_scores(t):
                rows = probs[t.slot(2)][:, :].rearrange("p (n q) -> p n q", q=SEQ)
                wait_tile(dve, second["scores_done"], t)
                wait_tile(dve, second["probs_turned"], t, 2)
                if isinstance(t.n, int) and t.n < 2:
                    dve.wait_ge(first["av_done"], T - 1 + t.n)
                for b in range(2):
                    last = dve.tensor_tensor(rows[:, 8 * b:8 * b + 8, :],
                                             bank_s[b][:, :].rearrange("p (n q) -> p n q", q=SEQ),
                                             causal_sb[:, :].unsqueeze(1).broadcast_to([P, 8, SEQ]), ALU.add)
                last.then_inc(second["probs_masked"], 1)

            def row_maximum(t):
                rows = probs[t.slot(2)][:, :].rearrange("p (n q) -> p n q", q=SEQ)
                wait_tile(dve, second["probs_masked"], t)
                wait_tile(dve, shifted_done, t, 1)
                dve.reduce_max(row_max[:, :], rows, axis=AX.X).then_inc(row_max_done, 1)

            def step2(i):
                at(i, 5, lambda t: dve_o_low(dve, second, t))
                at(i, 6, lambda t: dve_normalise(dve, second, t))
                at(i, 0, rotate_cross)
                at(i, 4, lambda t: dve_o_inverse(dve, second, t))
                at(i, 5, lambda t: dve_residual(dve, second, t))
                at(i, 5, lambda t: dve_statistics(dve, second, t))
                at(i, 2, mask_scores)
                at(i, 4, lambda t: dve_o_norm(dve, second, t))
                at(i, 5, lambda t: dve_variance(dve, second, t))
                at(i, 1, lambda t: dve_set_keys(dve, second, t))
                at(i, 2, row_maximum)

            over_tiles(dve, step1, step2)
            after_second(dve)

            def split_expert(e):
                dve.wait_ge(ffn_hi_set, e + 1)
                dve.tensor_tensor(ffn_lo[:, :, e, :], ffn_raw[:, :, e, :], ffn_hi[:, :, e, :].bitcast(f32),
                                  ALU.subtract).then_inc(ffn_split, 1)

            def split_group(g):
                wait_turn(dve, xg_hi_set, g)
                for k, b in enumerate((bank_ot, bank_out)):
                    last = dve.tensor_tensor(xg_lo[g.parity][:, k, :], b[:, :], xg_hi[g.parity][:, k, :].bitcast(f32), ALU.subtract)
                last.then_inc(xg_split, 1)

            def shift_logits(g):
                wait_turn(dve, logits_done, g)
                logits = bank_out[:, 0:GROUP_TILES * EXPERTS].rearrange("p (t e) -> p t e", e=EXPERTS)
                dve.reduce_max(top_logit[:, :], logits, axis=AX.X).then_inc(top_logit_done, 1)
                wait_turn(dve, top_logit_done, g)
                wait_turn(dve, exp_done, g, 1)
                dve.tensor_tensor(shifted[:, :, :], logits,
                                  top_logit[:, :].unsqueeze(2).broadcast_to([P, GROUP_TILES, EXPERTS]), ALU.subtract).then_inc(shifted3_done, 1)

            def pick_best(g):
                alone(dve)
                wait_turn(dve, exp_done, g)
                for j in range(GROUP_TILES):
                    last = dve.max(best[:, j, :], expd[:, j, :])
                last.then_inc(best_done, 1)
                wait_turn(dve, best_done, g)
                dve.tensor_tensor(pair_sum[:, :], best[:, :, 0], best[:, :, 1], ALU.add).then_inc(pair_sum_done, 1)
                for j in range(GROUP_TILES):
                    last = dve.max_index(best_at[:, j, :], best[:, j, :], expd[:, j, :])
                last.then_inc(best_at_done, 1)
                wait_turn(dve, pair_sum_done, g)
                dve.reciprocal(pair_inv[:, :], pair_sum[:, :]).then_inc(pair_inv_done, 1)
                wait_turn(dve, best_at_done, g)
                dve.tensor_copy(best_at_f[:, :, :], best_at[:, :, :]).then_inc(best_f_done, 1)
                wait_turn(dve, pair_inv_done, g)
                dve.tensor_tensor(pair_w[:, :, :], best[:, :, 0:2], pair_inv[:, :].unsqueeze(2).broadcast_to([P, GROUP_TILES, 2]),
                                  ALU.mult).then_inc(pair_w_done, 1)

            def combine_weights(g):
                iota = iota_sb[:, :].unsqueeze(1).broadcast_to([P, GROUP_TILES, EXPERTS])
                wait_turn(dve, best_f_done, g)
                wait_turn(dve, pair_w_done, g)
                for r in range(2):
                    at_r = best_at_f[:, :, r:r + 1].broadcast_to([P, GROUP_TILES, EXPERTS])
                    last = dve.tensor_tensor(chosen[r][:, :, :], iota, at_r, ALU.is_equal)
                last.then_inc(chosen_done, 1)
                wait_turn(dve, chosen_done, g)
                for r in range(2):
                    w_r = pair_w[:, :, r:r + 1].broadcast_to([P, GROUP_TILES, EXPERTS])
                    last = dve.tensor_tensor(picked[r][:, :, :], chosen[r][:, :, :], w_r, ALU.mult)
                last.then_inc(picked_done, 1)
                wait_turn(dve, picked_done, g)
                dve.tensor_tensor(combine[g.parity][:, :, :], picked[0][:, :, :], picked[1][:, :, :], ALU.add).then_inc(combine_done, 1)

            split_expert(0)
            split_group(Turn(0))
            shift_logits(Turn(0))
            pick_best(Turn(0))
            combine_weights(Turn(0))

            def weigh(i, g, e):
                wait_turn(dve, down_done, i)
                wait_turn(dve, weighed, i, 1)
                if e == 0:
                    wait_turn(dve, combine_done, g)
                    wait_turn(dve, out_set, g, 2)
                sums, banks = acc[g.parity], bank_down[e % 2]
                for j in range(GROUP_TILES):
                    onto = x_sb[:, g.n * GROUP_TILES + j, :] if e == 0 else sums[:, j, :]
                    last = dve.scalar_tensor_tensor(sums[:, j, :], banks[j // 2][:, j % 2 * E:j % 2 * E + E],
                                                    combine[g.parity][:, j, e:e + 1], onto, ALU.mult, ALU.add)
                last.then_inc(weighed, 1)

            def finish_group(g, e):
                sums = acc[g.parity]
                if e == 1:
                    wait_turn(dve, weighed, Turn((g.n + 1) * EXPERTS - 1))
                    for j in range(GROUP_TILES):
                        last = dve.bn_stats(g_stats[:, j, :], sums[:, j, :])
                    last.then_inc(g_stats_done, 1)
                if e == 2:
                    alone(dve)
                    wait_turn(dve, g_stats_done, g)
                    for j in range(GROUP_TILES):
                        last = dve.bn_aggr(g_mv[:, j, :], g_stats[:, j, :])
                    last.then_inc(g_mv_done, 1)
                if e == 4:
                    wait_turn(dve, g_inv_done, g)
                    wait_stores(dve, g, 1)
                    for j in range(GROUP_TILES):
                        last = dve.tensor_scalar(out_sb[:, j, :], sums[:, j, :], g_mv[:, j, 0:1], g_inv[:, j:j + 1],
                                                 ALU.subtract, ALU.mult)
                    last.then_inc(out_set, 1)

            def step3(i, g, e):
                if first_group(g) and e + 1 < EXPERTS:
                    split_expert(e + 1)
                if not_last(i):
                    wait_turn(dve, up_done, i)
                    wait_turn(dve, silu_done, i)
                    wait_turn(dve, h_split, i, 2)
                    dve.tensor_tensor(h_sb[e % 2][:, :], bank_up[:, :], silu_sb[e % 2][:, :], ALU.mult).then_inc(h_done, 1)
                    wait_turn(dve, h_hi_done, i)
                    wait_turn(dve, down_done, i, 2)
                    dve.tensor_tensor(h_lo[e % 2][:, :], h_sb[e % 2][:, :], h_hi[e % 2][:, :].bitcast(f32), ALU.subtract).then_inc(h_split, 1)
                if e > 0 and not_last(i):
                    weigh(i.back(1), g, e - 1)
                elif e == 0 and later(g):
                    weigh(i.back(1), g.back(1), EXPERTS - 1)
                if later(g):
                    finish_group(g.back(1), e)
                if more(g):
                    if e == 3:
                        split_group(g.back(-1))
                    if e == 5:
                        shift_logits(g.back(-1))
                    if e == 6:
                        pick_best(g.back(-1))
                    if e == 7:
                        combine_weights(g.back(-1))

            over_experts(dve, step3)

        @block.tensor
        def _(pe):
            pe.wait_ge(tables_in, TABLES * 16)
            pe.wait_ge(weights_split, 3)

            def project(bank, t, first_col, cols):
                hi, lo = xt_hi[t.slot(4)], xt_lo[t.slot(4)]
                passes = [(l, w, c) for l, w in ((hi, wqkv_hi), (hi, wqkv_lo), (lo, wqkv_hi)) for c in range(KC)]
                for n, (l, w, c) in enumerate(passes):
                    last = pe.matmul(bank[:, 0:cols], l[:, c, :], w[:, c, first_col:first_col + cols],
                                     start=n == 0, stop=n == len(passes) - 1)
                return last

            def project_qk(t):
                wait_tile(pe, xt_split, t)
                wait_tile(pe, rope_sin_done, t, 1)
                project(bank_qk, t, 0, 2 * E).then_inc(proj_qk_done, 1)

            def project_v(t):
                wait_tile(pe, first["v_set"], t, 1)
                project(bank_v, t, 2 * E, E).then_inc(proj_v_done, 1)

            def turn_qk(t):
                wait_tile(pe, qk_norm_done, t)
                wait_tile(pe, first["qk_hi_set"], t, 1)
                flat = qk_norm[t.slot(2)][:, :, :].rearrange("p h d -> p (h d)")
                pe_turn(pe, first, t, lambda n: flat[:, n * P:(n + 1) * P])

            def score(t):
                wait_tile(pe, first["keys_set"], t)
                wait_tile(pe, first["probs_squared"], t, 1)
                keys, kq = k_one[t.slot(2)], kq_parts[t.slot(2)]
                for j in range(PAIRS):
                    c, b, m = j // 4, j // 2 % 2, j % 2
                    rows = slice(64 * b, 64 * b + 64)
                    for q in range(2):
                        at_col = ((q * 2 + c) * 2 + m) * SEQ
                        cols = slice(c * P + q * 64, c * P + q * 64 + 64)
                        for n, (part, q_part) in enumerate(((0, 0), (0, 1), (1, 0))):
                            last = pe.matmul(
                                bank_s[b][:, at_col:at_col + SEQ],
                                keys[rows, part, c, q, 2 * m:2 * m + 2, :].rearrange("p m n -> p (m n)"),
                                kq[rows, q_part, cols], start=n == 0, stop=n == 2)
                last.then_inc(first["scores_done"], 1)

            def weigh_values(t):
                wait_tile(pe, first["probs_set"], t)
                wait_tile(pe, first["v_set"], t)
                wait_tile(pe, first["o_done"], t, 1)
                pr = probs[t.slot(2)][:, :].rearrange("p (b q c m n) -> p b q c m n", b=2, q=2, c=2, m=2)
                for j in range(PAIRS):
                    c, b, m = j // 4, j // 2 % 2, j % 2
                    for q in range(2):
                        last = pe.matmul(bank_av[64 * q:64 * q + 64, 2 * VW * j:2 * VW * (j + 1)],
                                         pr[:, b, q, c, m, :], v_pair[t.slot(4)][q][:, j, :], start=True, stop=True)
                last.then_inc(first["av_done"], 1)

            def step1(i):
                at(i, 2, turn_qk)
                at(i, 6, lambda t: pe_project(pe, first, t, 0))
                at(i, 0, project_qk)
                at(i, 0, project_v)
                at(i, 5, lambda t: pe_turn_o(pe, first, t))
                at(i, 3, score)
                at(i, 4, weigh_values)

            def turn_cross_qk(t):
                wait_tile(pe, cross_rot_done, t)
                wait_before(pe, "qk_hi_set", second, t)
                flat = cross_rot[t.slot(2)][:, :, :].rearrange("p h d -> p (h d)")
                pe_turn(pe, second, t, lambda n: flat[:, n * P:(n + 1) * P])

            def score_cross(t):
                alone(pe)
                wait_tile(pe, second["keys_set"], t)
                if t.first:
                    pe.wait_ge(first["probs_squared"], T)
                wait_tile(pe, second["probs_masked"], t, 1)
                keys, kq = k_one[t.slot(2)], kq_parts[t.slot(2)]
                for c in range(KC):
                    for q in range(2):
                        cols = slice(c * P + q * 64, c * P + q * 64 + 64)
                        for b in range(2):
                            rows = slice(64 * b, 64 * b + 64)
                            for n, (q_part, part) in enumerate(((0, 0), (0, 1), (1, 0))):
                                last = pe.matmul(bank_s[b][64 * q:64 * q + 64, 256 * c:256 * c + 256],
                                                 kq[rows, q_part, cols],
                                                 keys[rows, part, c, q, :, :].rearrange("p m n -> p (m n)"),
                                                 start=n == 0, stop=n == 2)
                last.then_inc(second["scores_done"], 1)

            def turn_probs(t):
                wait_tile(pe, second["probs_set"], t)
                if t.first:
                    pe.wait_ge(rope_sin_done, T)
                    pe.wait_ge(first["v_set"], T)
                wait_tile(pe, second["probs_turned_moved"], t, 1)
                pr = probs[t.slot(2)][:, :].rearrange("p (b c m n) -> p b c m n", b=2, c=2, m=4)
                for j in range(PAIRS):
                    c, b, m = j // 4, j // 2 % 2, j % 2
                    last = pe.transpose((bank_qk, bank_v)[j // 4][:, j % 4 * P:j % 4 * P + P],
                                        pr[:, b, c, 2 * m:2 * m + 2, :].rearrange("p m n -> p (m n)"), ident[:, :])
                last.then_inc(second["probs_turned"], 1)

            def weigh_context(t):
                wait_tile(pe, second["probs_turned_moved"], t)
                wait_tile(pe, second["v_set"], t)
                wait_before(pe, "o_done", second, t)
                for j in range(PAIRS):
                    for q in range(2):
                        last = pe.matmul(bank_av[64 * q:64 * q + 64, 2 * VW * j:2 * VW * (j + 1)],
                                         probs_t[:, j, 64 * q:64 * q + 64], v_pair[t.slot(4)][q][:, j // 2, :],
                                         start=True, stop=True)
                last.then_inc(second["av_done"], 1)

            def step2(i):
                if not isinstance(i.n, int):
                    pe.wait_ge(second["qk_turned"], i.n - 1)
                    pe.wait_ge(second["qk_turned"], i.n - 2)
                at(i, 5, lambda t: pe_project(pe, second, t, 1))
                at(i, 2, score_cross)
                at(i, 3, turn_probs)
                at(i, 0, turn_cross_qk)
                at(i, 4, lambda t: pe_turn_o(pe, second, t))
                at(i, 3, weigh_context)

            over_tiles(pe, step1, step2)
            after_second(pe)

            def turn_group(g):
                wait_turn(pe, x_copied, g)
                if later(g):
                    wait_turn(pe, shifted3_done, g, 1)
                for k, b in enumerate((bank_ot, bank_out)):
                    for j in range(GROUP_TILES):
                        last = pe.transpose(b[:, j * P:j * P + P], x_group[:, j, k * P:k * P + P], ident[:, :])
                last.then_inc(x_turned, 1)

            def score_group(g):
                wait_turn(pe, xg_split, g)
                hi, lo = xg_hi[g.parity], xg_lo[g.parity]
                passes = [(w, v, k) for w, v in ((router_hi, hi), (router_lo, hi), (router_hi, lo)) for k in range(KC)]
                for n, (w, v, k) in enumerate(passes):
                    last = pe.matmul(bank_ot[0:EXPERTS, :], w[:, k, :], v[:, k, :], start=n == 0, stop=n == 5)
                last.then_inc(logits_t_done, 1)

            def turn_logits(g):
                alone(pe)
                wait_turn(pe, logits_t_moved, g)
                for j in range(GROUP_TILES):
                    last = pe.transpose(bank_out[:, j * EXPERTS:(j + 1) * EXPERTS], logits_t[:, j * P:j * P + P],
                                        ident[0:EXPERTS, 0:EXPERTS])
                last.then_inc(logits_done, 1)

            turn_group(Turn(0))
            score_group(Turn(0))
            turn_logits(Turn(0))

            def down(i, g, e):
                wait_turn(pe, h_split, i)
                wait_turn(pe, weighed, i, 2)
                banks = bank_down[e % 2]
                for j in range(GROUP_TILES):
                    cols = slice(j * P, j * P + P)
                    for n, (h, w) in enumerate(((h_hi, ffn_hi), (h_hi, ffn_lo), (h_lo, ffn_hi))):
                        last = pe.matmul(banks[j // 2][:, j % 2 * E:j % 2 * E + E], h[e % 2][:, cols], w[:, 2, e, :],
                                         start=n == 0, stop=n == 2)
                last.then_inc(down_done, 1)

            def gate_or_up(bank, m, g, e):
                hi, lo = xg_hi[g.parity], xg_lo[g.parity]
                passes = [(w, v, k) for w, v in ((ffn_hi, hi), (ffn_lo, hi), (ffn_hi, lo)) for k in range(KC)]
                for n, (w, v, k) in enumerate(passes):
                    last = pe.matmul(bank[:, :], w[:, m, e, k * F:(k + 1) * F], v[:, k, :], start=n == 0, stop=n == 5)
                return last

            def step3(i, g, e):
                if not_last(i):
                    if first_group(g):
                        pe.wait_ge(ffn_split, e + 1)
                    wait_turn(pe, silu_done, i, 1)
                    gate_or_up(bank_gate, 0, g, e).then_inc(gate_done, 1)
                    wait_turn(pe, h_done, i, 1)
                    gate_or_up(bank_up, 1, g, e).then_inc(up_done, 1)
                if e > 0 and not_last(i):
                    down(i.back(1), g, e - 1)
                elif e == 0 and later(g):
                    down(i.back(1), g.back(1), EXPERTS - 1)
                if more(g):
                    if e == 2:
                        turn_group(g.back(-1))
                    if e == 4:
                        score_group(g.back(-1))
                    if e == 5:
                        turn_logits(g.back(-1))

            over_experts(pe, step3)


def rotary_tables():
    inv = (1.0 / np.float32(10000.0) ** (np.arange(0, D, 2, dtype=np.float32) / np.float32(D))).astype(np.float32)
    angle = np.arange(SEQ, dtype=np.float32)[:, None] * inv[None, :]
    cos, sin = np.cos(angle).astype(np.float32), np.sin(angle).astype(np.float32)
    return np.tile(np.concatenate([cos, cos], 1), (2, 1)), np.tile(np.concatenate([-sin, sin], 1), (2, 1))


def kernel(x, ctx_512, L0_attn_w_qkv, L0_attn_w_out, L0_attn_ln_scale, L0_attn_ln_bias, L0_xattn_q_norm_w,
           L0_xattn_k_norm_w, L0_xattn_w_out, L0_ffn_router_w, L0_ffn_gate_proj, L0_ffn_up_proj, L0_ffn_down_proj):
    import concourse.bacc as bacc
    from concourse.bass_utils import run_bass_kernel_spmd

    flat = np.asarray(x).reshape(TOKENS, E)
    cos, sin = rotary_tables()
    pos = np.arange(P) % SEQ
    keep = (pos[:, None] <= np.arange(SEQ)[None, :]).astype(np.float32)
    causal = np.where(np.arange(SEQ)[None, :] <= pos[:, None], 0.0, -1e30).astype(np.float32)
    quarter = (np.arange(P)[:, None] % 64 // D == np.arange(4)[None, :]).astype(np.float32)
    arrays = {
        "x": flat,
        "x_t": np.ascontiguousarray(flat.T),
        "ctx": np.asarray(ctx_512).reshape(TOKENS, CTX),
        "w_qkv": np.asarray(L0_attn_w_qkv),
        "w_out1": np.asarray(L0_attn_w_out),
        "ln_scale": np.ascontiguousarray(np.tile(np.asarray(L0_attn_ln_scale), P // D).reshape(P, 1)),
        "ln_bias": np.ascontiguousarray(np.tile(np.asarray(L0_attn_ln_bias), P // D).reshape(P, 1)),
        "q_w": np.asarray(L0_xattn_q_norm_w),
        "k_w": np.asarray(L0_xattn_k_norm_w),
        "w_out2_t": np.ascontiguousarray(np.asarray(L0_xattn_w_out).T),
        "router": np.asarray(L0_ffn_router_w),
        "gate_w": np.asarray(L0_ffn_gate_proj),
        "up_w": np.asarray(L0_ffn_up_proj),
        "down_w": np.asarray(L0_ffn_down_proj),
        "cos_t": cos,
        "sin_t": sin,
        "keep_t": keep,
        "causal_add": causal,
        "quarter": quarter,
        "identity": np.eye(P, dtype=np.float32),
        "experts_iota": np.tile(np.arange(EXPERTS, dtype=np.float32), (P, 1)),
    }
    nc = bacc.Bacc("TRN2", target_bir_lowering=False, num_devices=1)
    args = {n: nc.dram_tensor(n, a.shape, mybir.dt.from_np(a.dtype), kind="ExternalInput").ap()
            for n, a in arrays.items()}
    out = nc.dram_tensor("out", (TOKENS, E), mybir.dt.float32, kind="ExternalOutput").ap()
    build_decoder(nc, out=out, **args)
    result = run_bass_kernel_spmd(nc, [arrays], core_ids=[0])
    return result.results[0]["out"].reshape(SEQS, SEQ, E)
```

```python
from contextlib import ExitStack

import numpy as np

import concourse.bass as bass
from concourse import mybir

P = 128
SEQS, SEQ, E = 64, 64, 256
TOKENS = SEQS * SEQ
T = TOKENS // P
CTX = 64
HEADS, D = 16, 16
KV_HEADS = 4
PAIRS = HEADS // 2
EXPERTS, F = 8, 128
KC = E // P
UNROLL = 4
TABLES = 4
LAG1, LAG2, HANDOVER = 6, 7, 2
GROUP_TILES = 4
TAIL = 5
GROUP = GROUP_TILES * P
GROUPS = T // GROUP_TILES
EPS = 1e-5
VW = D + 1


class Tile:

    def __init__(self, n, rest):
        self.n, self.rest = n, rest % UNROLL

    def back(self, k):
        return Tile(self.n - k, self.rest - k)

    def slot(self, slots):
        return self.rest % slots

    @property
    def live(self):
        return not isinstance(self.n, int) or 0 <= self.n < T

    @property
    def first(self):
        return isinstance(self.n, int) and self.n == 0


class Turn:

    def __init__(self, n, parity=0):
        self.n, self.parity = n, parity % 2

    def back(self, k):
        return Turn(self.n - k, self.parity - k)


def over_tiles(eng, first_step, second_step):
    head1, head2 = (-(-lag // UNROLL) * UNROLL for lag in (LAG1, LAG2))
    for i in range(head1):
        first_step(Tile(i, i))
    with eng.Fori(head1, T - UNROLL + 1, UNROLL) as base:
        for u in range(UNROLL):
            first_step(Tile(base + u, u))
    for k in range(HANDOVER + head2):
        if k < LAG1:
            first_step(Tile(T + k, k))
        if k >= HANDOVER:
            second_step(Tile(k - HANDOVER, k - HANDOVER))
    with eng.Fori(head2, T - UNROLL + 1, UNROLL) as base:
        for u in range(UNROLL):
            second_step(Tile(base + u, u))
    for i in range(T, T + LAG2):
        second_step(Tile(i, i))


def at(i, lag, step):
    tile = i.back(lag)
    if tile.live:
        step(tile)


def wait_tile(eng, sem, tile, back=0):
    count = tile.n + 1 - back
    if isinstance(count, int) and count <= 0:
        return
    eng.wait_ge(sem, count)


def table_columns():
    first = 0
    for cols in (P, D, D, SEQ, SEQ, 4, EXPERTS):
        yield first, cols
        first += cols


TABLE_COLS = P + 2 * D + 2 * SEQ + 4 + EXPERTS


def build_decoder(nc, x, x_t, ctx, w_qkv, w_out1, ln_pair, q_w, k_w, w_out2_t, router,
                  gate_w, up_w, down_w, tables, out):
    f32, f16, bf16, f32r = mybir.dt.float32, mybir.dt.float16, mybir.dt.bfloat16, mybir.dt.float32r
    ALU, ACT, AX = mybir.AluOpType, mybir.ActivationFunctionType, mybir.AxisListType

    stack = ExitStack()
    with stack:
        def sb(name, shape, dt=f32):
            return stack.enter_context(nc.sbuf_tensor(name, shape, dt))

        def sem(name):
            return stack.enter_context(nc.semaphore(name))

        def bank(name):
            return stack.enter_context(nc.psum_tensor(name, [P, 512], f32))

        x_sb = sb("x_sb", [P, T, E])
        ffn_raw = sb("ffn_raw", [P, 3, EXPERTS, E])
        wqkv_raw = ffn_raw[:, 0, :, :].rearrange("p e n -> p (e n)")[:, 0:KC * 3 * E].rearrange(
            "p (k n) -> p k n", k=KC)
        router_raw = sb("router_raw", [P, KC, EXPERTS])
        router_hi, router_lo = sb("router_hi", [P, KC, EXPERTS], f32r), sb("router_lo", [P, KC, EXPERTS], f32r)
        tables_sb = sb("tables_sb", [P, TABLE_COLS])
        ident, cos_sb, sin_sb, keep_sb, causal_sb, quarter_sb, iota_sb = (
            tables_sb[:, first:first + cols] for first, cols in table_columns())
        eps_sb, minus_half = sb("eps_sb", [P, GROUP_TILES]), sb("minus_half", [P, GROUP_TILES])
        phase1 = ExitStack()

        def sb1(name, shape, dt=f32):
            return phase1.enter_context(nc.sbuf_tensor(name, shape, dt))

        xt_raw = [sb1(f"xt_raw{n}", [P, KC, P]) for n in range(4)]
        wqkv_hi, wqkv_lo = sb1("wqkv_hi", [P, KC, 3 * E], f32r), sb1("wqkv_lo", [P, KC, 3 * E], f32r)
        xt_hi = [sb1(f"xt_hi{n}", [P, KC, P], f32r) for n in range(4)]
        xt_lo = [sb1(f"xt_lo{n}", [P, KC, P], f32r) for n in range(4)]
        rot_cos, rot_sin = sb1("rot_cos", [P, 32, D]), sb1("rot_sin", [P, 32, D])
        rot = [sb1(f"rot{n}", [P, 32, D]) for n in range(2)]
        centred, centred_sq = sb1("centred", [P, 32, D]), sb1("centred_sq", [P, 32, D])
        head_sum, head_var = sb1("head_sum", [P, 32]), sb1("head_var", [P, 32])
        head_mean = [sb1(f"head_mean{n}", [P, 32]) for n in range(2)]
        head_std, head_inv = sb1("head_std", [P, 32]), sb1("head_inv", [P, 32])
        qk_norm = [sb1(f"qk_norm{n}", [P, 32, D]) for n in range(2)]
        phase1.close()

        phase3 = ExitStack()

        def sb3(name, shape, dt=f32):
            return phase3.enter_context(nc.sbuf_tensor(name, shape, dt))

        ffn_hi, ffn_lo = sb3("ffn_hi", [P, 3, EXPERTS, E], f32r), sb3("ffn_lo", [P, 3, EXPERTS, E], f32r)
        xg_hi, xg_lo = [sb3("xg_hi0", [P, KC, GROUP], f32r)], [sb3("xg_lo0", [P, KC, GROUP], f32r)]
        logits_t = sb3("logits_t", [EXPERTS, GROUP])
        top_logit = sb3("top_logit", [P, GROUP_TILES])
        shifted = sb3("shifted", [P, GROUP_TILES, EXPERTS])
        expd = sb3("expd", [P, GROUP_TILES, EXPERTS])
        attention_memory = ExitStack()
        stack2 = attention_memory

        def sb(name, shape, dt=f32):
            return stack2.enter_context(nc.sbuf_tensor(name, shape, dt))

        wo_raw = sb("wo_raw", [P, 2, KC, E])
        wo_hi, wo_lo = sb("wo_hi", [P, 2, KC, E], f32r), sb("wo_lo", [P, 2, KC, E], f32r)
        causal_16, ident_16 = sb("causal_16", [P, 4, SEQ], bf16), sb("ident_16", [P, P], bf16)
        ln_sb = sb("ln_sb", [P, 2])
        scale_sb, bias_sb = ln_sb[:, 0:1], ln_sb[:, 1:2]
        qw_sb, kw_sb = sb("qw_sb", [P, E]), sb("kw_sb", [P, CTX])
        q_cos, q_sin = sb("q_cos", [P, HEADS, D]), sb("q_sin", [P, HEADS, D])
        k_cos, k_sin = sb("k_cos", [P, KV_HEADS, D]), sb("k_sin", [P, KV_HEADS, D])

        bank_qk, bank_v, bank_tr, bank_s0, bank_s1, bank_av, bank_ot, bank_out = (
            bank(n) for n in ("bank_qk", "bank_v", "bank_tr", "bank_s0", "bank_s1", "bank_av", "bank_ot", "bank_out"))
        bank_s = (bank_s0, bank_s1)

        block_names = ("wqkv_in", "weights_in", "tables_in", "x_in", "constants_set", "wqkv_split_hi", "weights_split",
                       "qk_tables_set")
        s = {n: sem(n) for n in block_names}
        wqkv_in, weights_in, tables_in, x_in, constants_set, wqkv_split_hi, weights_split, qk_tables_set = (
            s[n] for n in block_names)
        ffn_in, ffn_hi_set, ffn_split = sem("ffn_in"), sem("ffn_hi_set"), sem("ffn_split")

        kq32 = sb("kq32", [P, 512])
        kq_parts = [sb(f"kq_parts{n}", [P, 2, 512], f16) for n in range(2)]
        k_one = [sb(f"k_one{n}", [P, 2, KC, 2, 4, SEQ], f16) for n in range(2)]
        probs = [sb(f"probs{n}", [P, 1024]) for n in range(2)]
        v_pair = [[sb(f"v_pair{n}{q}", [P, PAIRS, 2 * VW]) for q in range(2)] for n in range(4)]
        o_inv, o_sb = sb("o_inv", [P, HEADS]), sb("o_sb", [P, HEADS, D])
        o_hi, o_lo = sb("o_hi", [P, KC, P], f32r), sb("o_lo", [P, KC, P], f32r)
        y_sb = sb("y_sb", [P, E])
        y_stats, y_mv, y_inv = sb("y_stats", [P, 6]), sb("y_mv", [P, 2]), sb("y_inv", [P, 1])
        y_std = sb("y_std", [P, 1])

        NH = HEADS + KV_HEADS
        ctx_sb = sb("ctx_sb", [P, T, CTX])
        square_out = sb("square_out", [P, E])
        mean_sq, rms_in, rms_inv = sb("mean_sq", [P, 2]), sb("rms_in", [P, 2]), sb("rms_inv", [P, 2])
        cross_cos, cross_sin = sb("cross_cos", [P, NH, D]), sb("cross_sin", [P, NH, D])
        cross_rot = [sb(f"cross_rot{n}", [P, 2 * HEADS, D]) for n in range(2)]
        cross_sum = [sb(f"cross_sum{n}", [P, NH, D]) for n in range(2)]
        probs_t = sb("probs_t", [P, PAIRS, P])
        row_max = sb("row_max", [P, HEADS])
        y_var = sb("y_var", [P, 1])

        attention_memory.close()

        xt_loaded = [sem(f"xt_loaded{n}") for n in range(4)]
        names1 = ["xt_hi_set", "xt_split", "proj_qk_done", "proj_v_done", "rope_cos_done", "rope_sin_done",
                  "rope_sum_done", "head_sum_done", "head_mean_done", "centred_done", "centred_sq_done",
                  "head_var_done", "head_std_done", "head_inv_done", "qk_norm_done"]
        (xt_hi_set, xt_split, proj_qk_done, proj_v_done, rope_cos_done, rope_sin_done, rope_sum_done,
         head_sum_done, head_mean_done, centred_done, centred_sq_done, head_var_done, head_std_done,
         head_inv_done, qk_norm_done) = (sem(n) for n in names1)

        def attention_sems(layer):
            return {n: sem(f"{n}{layer}") for n in (
                "qk_turned", "qk_hi_set", "qk_lo_set", "keys_set", "scores_done", "probs_masked",
                "probs_squared", "probs_set", "probs_turned", "probs_turned_moved", "v_set", "av_done",
                "o_inv_done", "o_done", "o_turned", "o_hi_set", "o_split", "out_done", "residual_done",
                "stats_done", "mv_done", "std_done", "inv_done", "norm_done")}

        first, second = attention_sems(1), attention_sems(2)

        squares_q = sem("squares_q")
        (ctx_in, mean_sq_done, rms_in_done, rms_inv_done, cross_scaled, cross_sin_done, cross_sum_done,
         row_max_done, shifted_done, y_var_done) = (sem(n) for n in (
             "ctx_in", "mean_sq_done", "rms_in_done", "rms_inv_done", "cross_scaled", "cross_sin_done",
             "cross_sum_done", "row_max_done", "shifted_done", "y_var_done"))

        x_group = sb3("x_group", [P, GROUP_TILES, E])
        xg_hi.append(sb3("xg_hi1", [P, KC, GROUP], f32r))
        xg_lo.append(sb3("xg_lo1", [P, KC, GROUP], f32r))
        silu_sb = [sb3(f"silu_sb{n}", [P, GROUP]) for n in range(2)]
        h_sb = [sb3(f"h_sb{n}", [P, GROUP]) for n in range(2)]
        h_hi = [sb3(f"h_hi{n}", [P, GROUP], f32r) for n in range(2)]
        h_lo = [sb3(f"h_lo{n}", [P, GROUP], f32r) for n in range(2)]
        acc = [sb3(f"acc{n}", [P, GROUP_TILES, E]) for n in range(2)]
        out_sb = sb3("out_sb", [P, GROUP_TILES, E])
        best = sb3("best", [P, GROUP_TILES, 8])
        best_at = sb3("best_at", [P, GROUP_TILES, 8], mybir.dt.uint32)
        best_at_f = sb3("best_at_f", [P, GROUP_TILES, 8])
        pair_sum, pair_inv = sb3("pair_sum", [P, GROUP_TILES]), sb3("pair_inv", [P, GROUP_TILES])
        pair_w = sb3("pair_w", [P, GROUP_TILES, 2])
        chosen = [sb3(f"chosen{n}", [P, GROUP_TILES, EXPERTS]) for n in range(2)]
        picked = [sb3(f"picked{n}", [P, GROUP_TILES, EXPERTS]) for n in range(2)]
        combine = [sb3(f"combine{n}", [P, GROUP_TILES, EXPERTS]) for n in range(2)]
        g_stats, g_mv = sb3("g_stats", [P, GROUP_TILES, 6]), sb3("g_mv", [P, GROUP_TILES, 2])
        g_var, g_inv = sb3("g_var", [P, GROUP_TILES]), sb3("g_inv", [P, GROUP_TILES])
        phase3.close()
        (x_copied, x_turned, xg_hi_set, xg_split, logits_t_done, logits_t_moved, logits_done, top_logit_done,
         shifted3_done, exp_done, best_done, best_at_done, best_f_done, pair_sum_done, pair_inv_done,
         pair_w_done, picked_done, combine_done, acc_done, g_stats_done, g_mv_done, g_var_done, g_inv_done,
         out_set, out_stored) = (sem(n) for n in (
             "x_copied", "x_turned", "xg_hi_set", "xg_split", "logits_t_done", "logits_t_moved", "logits_done",
             "top_logit_done", "shifted3_done", "exp_done", "best_done", "best_at_done", "best_f_done",
             "pair_sum_done", "pair_inv_done", "pair_w_done", "picked_done", "combine_done", "acc_done",
             "g_stats_done", "g_mv_done", "g_var_done", "g_inv_done", "out_set", "out_stored"))
        chosen_done = sem("chosen_done")
        gate_done, up_done, silu_done, h_done, h_hi_done, h_split, down_done, weighed = (sem(n) for n in (
            "gate_done", "up_done", "silu_done", "h_done", "h_hi_done", "h_split", "down_done", "weighed"))
        bank_gate, bank_up = bank_qk, bank_v
        bank_down = ((bank_s1, bank_av), (bank_tr, bank_s0))

        def turn_banks(g):
            return (bank_s0, bank_s1) if first_group(g) else (bank_ot, bank_out)

        def logits_t_bank(g):
            return bank_tr if first_group(g) else bank_ot

        def logits_bank(g):
            return bank_s0 if first_group(g) else bank_out

        def ending(i):
            return i.n - T if isinstance(i.n, int) and i.n >= T else None

        def wait_turn(eng, sem, turn, back=0):
            count = turn.n + 1 - back
            if isinstance(count, int) and count <= 0:
                return
            eng.wait_ge(sem, count)

        def wait_stores(eng, turn, back):
            count = 16 * (turn.n + 1 - back)
            if isinstance(count, int) and count <= 0:
                return
            eng.wait_ge(out_stored, count)

        def more(g):
            return not isinstance(g.n, int) or g.n + 1 < GROUPS

        def later(g):
            return not isinstance(g.n, int) or g.n > 0

        def first_group(g):
            return isinstance(g.n, int) and g.n == 0

        def not_last(i):
            return not isinstance(i.n, int) or i.n < GROUPS * EXPERTS

        def after_second(eng):
            eng.wait_ge(second["norm_done"], T)

        def over_experts(eng, step):
            def groups(first_n):
                for u in range(2):
                    for e in range(EXPERTS):
                        step(Turn((first_n + u) * EXPERTS + e), Turn(first_n + u, u), e)
            groups(0)
            with eng.Fori(2, GROUPS - 3, 2) as base:
                groups(base)
            groups(GROUPS - 2)
            for e in range(TAIL):
                step(Turn(GROUPS * EXPERTS + e), Turn(GROUPS, 0), e)


        def alone(eng):
            eng.wait_ge(tables_in, TABLES * 16)

        def wait_before(eng, name, a, t, back=1):
            if a is second and isinstance(t.n, int) and t.n < back:
                eng.wait_ge(first[name], T + t.n + 1 - back)
            else:
                wait_tile(eng, a[name], t, back)

        def low_qk(eng, a, t):
            parts = kq_parts[t.slot(2)]
            wait_tile(eng, a["qk_hi_set"], t)
            wait_before(eng, "scores_done", a, t, 2)
            eng.tensor_tensor(parts[:, 1, :], kq32[:, :], parts[:, 0, :], ALU.subtract).then_inc(a["qk_lo_set"], 1)

        def dve_set_keys(dve, a, t):
            wait_tile(dve, a["qk_lo_set"], t)
            wait_before(dve, "scores_done", a, t, 2)
            for m in range(4):
                last = dve.tensor_scalar(
                    k_one[t.slot(2)][:, :, :, :, m, :].rearrange("p w c s n -> p w (c s) n"),
                    kq_parts[t.slot(2)][:, :, 256:512].rearrange("p w (cs n) -> p w cs n", n=SEQ),
                    quarter_sb[:, m:m + 1], None, ALU.mult)
            last.then_inc(a["keys_set"], 1)

        def dve_o_inverse(dve, a, t):
            wait_tile(dve, a["av_done"], t)
            wait_before(dve, "o_done", a, t)
            av = bank_av[:, 0:HEADS * VW].rearrange("p (h v) -> p h v", v=VW)
            dve.reciprocal(o_inv[:, :], av[:, :, D]).then_inc(a["o_inv_done"], 1)

        def dve_o_norm(dve, a, t):
            wait_tile(dve, a["o_inv_done"], t)
            wait_before(dve, "o_turned", a, t)
            av = bank_av[:, 0:HEADS * VW].rearrange("p (h v) -> p h v", v=VW)
            dve.tensor_tensor(o_sb[:, :, :], av[:, :, 0:D],
                              o_inv[:, :].unsqueeze(2).broadcast_to([P, HEADS, D]), ALU.mult).then_inc(a["o_done"], 1)

        def dve_o_low(dve, a, t):
            wait_tile(dve, a["o_hi_set"], t)
            wait_before(dve, "out_done", a, t)
            dve.tensor_tensor(o_lo[:, :, :], bank_ot[:, 0:E].rearrange("p (k n) -> p k n", k=KC),
                              o_hi[:, :, :].bitcast(f32), ALU.subtract).then_inc(a["o_split"], 1)

        def dve_residual(dve, a, t):
            if t.first and a is first:
                dve.wait_ge(x_in, 4 * 16)
            wait_tile(dve, a["out_done"], t)
            wait_before(dve, "norm_done", a, t)
            dve.tensor_tensor(y_sb[:, :], bank_out[:, 0:E], x_sb[:, t.n, :], ALU.add).then_inc(a["residual_done"], 1)

        def dve_statistics(dve, a, t):
            wait_tile(dve, a["residual_done"], t)
            dve.bn_stats(y_stats[:, :], y_sb[:, :]).then_inc(a["stats_done"], 1)

        def dve_variance(dve, a, t):
            alone(dve)
            wait_tile(dve, a["stats_done"], t)
            dve.bn_aggr(y_mv[:, :], y_stats[:, :]).then_inc(a["mv_done"], 1)

        def dve_normalise(dve, a, t):
            wait_tile(dve, a["inv_done"], t)
            dve.tensor_scalar(x_sb[:, t.n, :], y_sb[:, :], y_mv[:, 0:1], y_inv[:, 0:1],
                              ALU.subtract, ALU.mult).then_inc(a["norm_done"], 1)

        def act_move_qk(act, a, t, scale, bias):
            wait_tile(act, a["qk_turned"], t)
            wait_before(act, "qk_lo_set", a, t)
            act.activation(kq32[:, :], bank_tr[:, :], ACT.Identity, bias=bias, scale=scale)
            wait_before(act, "scores_done", a, t, 2)
            act.activation(kq_parts[t.slot(2)][:, 0, :], bank_tr[:, :], ACT.Identity, bias=bias,
                           scale=scale).then_inc(a["qk_hi_set"], 1)

        def act_o_high(act, a, t):
            wait_tile(act, a["o_turned"], t)
            wait_before(act, "out_done", a, t)
            act.activation(o_hi[:, :, :], bank_ot[:, 0:E].rearrange("p (k n) -> p k n", k=KC),
                           ACT.Copy).then_inc(a["o_hi_set"], 1)

        def pe_turn(pe, a, t, source):
            for n in range(4):
                last = pe.transpose(bank_tr[:, n * P:(n + 1) * P], source(n), ident[:, :])
            last.then_inc(a["qk_turned"], 1)

        def pe_turn_o(pe, a, t):
            wait_tile(pe, a["o_done"], t)
            wait_before(pe, "o_split", a, t)
            flat = o_sb[:, :, :].rearrange("p h d -> p (h d)")
            for c in range(KC):
                last = pe.transpose(bank_ot[:, c * P:(c + 1) * P], flat[:, c * P:(c + 1) * P], ident[:, :])
            last.then_inc(a["o_turned"], 1)

        def pe_project(pe, a, t, layer):
            if t.first and a is first:
                pe.wait_ge(weights_split, KC + 2)
            wait_tile(pe, a["o_split"], t)
            wait_before(pe, "residual_done", a, t)
            passes = [(l, w, c) for l, w in ((o_hi, wo_hi), (o_hi, wo_lo), (o_lo, wo_hi)) for c in range(KC)]
            for n, (l, w, c) in enumerate(passes):
                last = pe.matmul(bank_out[:, 0:E], l[:, c, :], w[:, layer, c, :], start=n == 0,
                                 stop=n == len(passes) - 1)
            last.then_inc(a["out_done"], 1)

        block = stack.enter_context(nc.Block())

        @block.sync
        def _(sp):
            for k in range(KC):
                sp.dma_start(wqkv_raw[:, k, :], w_qkv[k * P:(k + 1) * P, :]).then_inc(wqkv_in, 16)
            sp.dma_start(wo_raw[:, 0, :, :], w_out1.rearrange("(k p) n -> p k n", p=P)).then_inc(weights_in, 16)
            sp.dma_start(wo_raw[:, 1, :, :], w_out2_t.rearrange("(k p) n -> p k n", p=P)).then_inc(weights_in, 16)
            sp.dma_start(router_raw[:, :, :], router.rearrange("(k p) n -> p k n", p=P)).then_inc(weights_in, 16)
            for dst, src in ((qw_sb, q_w), (kw_sb, k_w)):
                sp.dma_start(dst[:, :], src.partition_broadcast(P)).then_inc(tables_in, 16)

            def load_xt(t):
                if not t.live:
                    return
                wait_tile(sp, xt_split, t, 4)
                sp.dma_start(xt_raw[t.slot(4)][:, :, :],
                             x_t[:, bass.ds(t.n * P, P)].rearrange("(k p) n -> p k n", p=P)
                             ).then_inc(xt_loaded[t.slot(4)], 16)

            over_tiles(sp, load_xt, lambda t: None)
            sp.wait_ge(weights_split, KC)
            for n, w in enumerate((gate_w, up_w)):
                sp.dma_start(ffn_raw[:, n, :, :].rearrange("p e (k f) -> p e k f", k=KC),
                             w.rearrange("e (k p) f -> p e k f", p=P)).then_inc(ffn_in, 16)
            sp.dma_start(ffn_raw[:, 2, :, :], down_w.rearrange("e f n -> f e n")).then_inc(ffn_in, 16)

            outs = out.rearrange("(t p) n -> p t n", p=P)

            def store(i, g, e):
                if e == 4 and later(g):
                    b = g.back(1)
                    wait_turn(sp, out_set, b)
                    sp.dma_start(outs[:, bass.ds(b.n * GROUP_TILES, GROUP_TILES), :], out_sb[:, :, :]).then_inc(out_stored, 16)

            over_experts(sp, store)
            sp.wait_ge(out_stored, 16 * GROUPS)

        @block.gpsimd
        def _(pool):
            pool.memset(eps_sb[:, :], EPS).then_inc(constants_set, 1)
            pool.memset(minus_half[:, :], -0.5).then_inc(constants_set, 1)
            n = 2
            for pair in v_pair:
                for v in pair:
                    pool.memset(v[:, :, :], 0.0).then_inc(constants_set, 1)
                    n += 1
            pool.wait_ge(constants_set, n)
            for pair in v_pair:
                for v in pair:
                    pool.memset(v[0:64, :, D:D + 1], 1.0).then_inc(constants_set, 1)
                    pool.memset(v[64:128, :, VW + D:VW + D + 1], 1.0).then_inc(constants_set, 1)

            def low_xt(t):
                wait_tile(pool, xt_hi_set, t)
                wait_tile(pool, proj_v_done, t, 4)
                pool.tensor_tensor(xt_lo[t.slot(4)][:, :, :], xt_raw[t.slot(4)][:, :, :],
                                   xt_hi[t.slot(4)][:, :, :].bitcast(f32), ALU.subtract).then_inc(xt_split, 1)

            def add_rotary(t):
                wait_tile(pool, rope_sin_done, t)
                wait_tile(pool, centred_done, t, 2)
                wait_tile(pool, head_sum_done, t, 2)
                pool.tensor_tensor(rot[t.slot(2)][:, :, :], rot_cos[:, :, :], rot_sin[:, :, :], ALU.add).then_inc(rope_sum_done, 1)

            def centre(t):
                wait_tile(pool, head_mean_done, t)
                wait_tile(pool, qk_norm_done, t, 1)
                pool.tensor_tensor(centred[:, :, :], rot[t.slot(2)][:, :, :],
                                   head_mean[t.slot(2)][:, :].unsqueeze(2).broadcast_to([P, 32, D]), ALU.subtract
                                   ).then_inc(centred_done, 1)

            def scale_heads(t):
                wait_tile(pool, head_inv_done, t)
                wait_tile(pool, first["qk_turned"], t, 2)
                pool.tensor_tensor(qk_norm[t.slot(2)][:, :, :], centred[:, :, :],
                                   head_inv[:, :].unsqueeze(2).broadcast_to([P, 32, D]), ALU.mult).then_inc(qk_norm_done, 1)

            def mask(t):
                pr = probs[t.slot(2)][:, :].rearrange("p (n q) -> p n q", q=SEQ)
                wait_tile(pool, first["probs_squared"], t)
                pool.tensor_tensor(pr, pr, keep_sb[:, :].unsqueeze(1).broadcast_to([P, HEADS, SEQ]),
                                   ALU.mult).then_inc(first["probs_masked"], 1)

            def step1(i):
                at(i, 0, low_xt)
                at(i, 1, centre)
                at(i, 4, mask)
                at(i, 0, add_rotary)
                at(i, 1, scale_heads)

            def rms_sum(t):
                wait_tile(pool, mean_sq_done, t)
                wait_tile(pool, rms_inv_done, t, 1)
                pool.tensor_tensor(rms_in[:, :], mean_sq[:, :], eps_sb[:, 0:2], ALU.add).then_inc(rms_in_done, 1)

            def rms_root(t):
                wait_tile(pool, rms_in_done, t)
                wait_tile(pool, cross_scaled, t, 1)
                pool.tensor_tensor(rms_inv[:, :], rms_in[:, :], minus_half[:, 0:2], ALU.pow).then_inc(rms_inv_done, 1)

            def rotate_cross(t):
                if t.first:
                    pool.wait_ge(ctx_in, 16)
                    pool.wait_ge(qk_tables_set, 7)
                wait_tile(pool, cross_sum_done, t, 1)
                pool.wait_ge(first["norm_done"], t.n + 1 if isinstance(t.n, int) else T)
                xv = x_sb[:, t.n, :].rearrange("p (h d) -> p h d", d=D)
                cv = ctx_sb[:, t.n, :].rearrange("p (h d) -> p h d", d=D)
                for src, w_cos, w_sin, heads in ((xv, q_cos, q_sin, slice(0, HEADS)), (cv, k_cos, k_sin, slice(HEADS, NH))):
                    pool.tensor_tensor(cross_cos[:, heads, :], src, w_cos[:, :, :], ALU.mult)
                    for lo, hi in ((0, D // 2), (D // 2, 0)):
                        last = pool.tensor_tensor(cross_sin[:, heads, lo:lo + 8], src[:, :, hi:hi + 8],
                                                  w_sin[:, :, lo:lo + 8], ALU.mult)
                last.then_inc(cross_sin_done, 1)

            def add_cross_rotary(t):
                wait_tile(pool, cross_sin_done, t)
                wait_tile(pool, cross_scaled, t, 2)
                pool.tensor_tensor(cross_sum[t.slot(2)][:, :, :], cross_cos[:, :, :], cross_sin[:, :, :],
                                   ALU.add).then_inc(cross_sum_done, 1)

            def variance(t):
                wait_tile(pool, second["mv_done"], t)
                wait_tile(pool, second["inv_done"], t, 1)
                pool.tensor_tensor(y_var[:, :], y_mv[:, 1:2], eps_sb[:, 0:1], ALU.add).then_inc(y_var_done, 1)

            def inverse_std(t):
                wait_tile(pool, y_var_done, t)
                wait_before(pool, "norm_done", second, t)
                pool.tensor_tensor(y_inv[:, :], y_var[:, :], minus_half[:, 0:1], ALU.pow).then_inc(second["inv_done"], 1)

            def step2(i):
                at(i, 0, rotate_cross)
                at(i, 0, rms_sum)
                at(i, 0, add_cross_rotary)
                at(i, 0, rms_root)
                at(i, 1, lambda t: low_qk(pool, second, t))
                at(i, 6, variance)
                at(i, 6, inverse_std)

            over_tiles(pool, step1, step2)
            after_second(pool)

            def copy_group(g):
                wait_turn(pool, x_turned, g, 1)
                pool.tensor_copy(x_group[:, :, :], x_sb[:, bass.ds(g.n * GROUP_TILES, GROUP_TILES), :]).then_inc(x_copied, 1)

            def step3(i, g, e):
                if e == 0 and more(g):
                    copy_group(g.back(-1))
                if e == 2 and later(g):
                    b = g.back(1)
                    wait_turn(pool, g_mv_done, b)
                    wait_turn(pool, g_inv_done, b, 1)
                    pool.tensor_tensor(g_var[:, :], g_mv[:, :, 1], eps_sb[:, :], ALU.add).then_inc(g_var_done, 1)
                    wait_turn(pool, g_var_done, b)
                    wait_turn(pool, out_set, b, 1)
                    pool.tensor_tensor(g_inv[:, :], g_var[:, :], minus_half[:, :], ALU.pow).then_inc(g_inv_done, 1)

            over_experts(pool, step3)

        @block.scalar
        def _(act):
            for dst, src in ((tables_sb, tables), (ln_sb, ln_pair)):
                act.dma_start(dst[:, :], src).then_inc(tables_in, 16)
            act.wait_ge(wqkv_in, KC * 16)
            for k in range(KC):
                act.activation(wqkv_hi[:, k, :], wqkv_raw[:, k, :], ACT.Copy).then_inc(wqkv_split_hi, 1)
            act.wait_ge(tables_in, TABLES * 16)
            act.wait_ge(weights_in, 3 * 16)
            act.activation(wo_hi[:, :, :, :], wo_raw[:, :, :, :], ACT.Copy).then_inc(wqkv_split_hi, 1)
            act.activation(router_hi[:, :, :], router_raw[:, :, :], ACT.Copy).then_inc(wqkv_split_hi, 1)
            xs = x.rearrange("(t p) n -> p t n", p=P)
            for n in range(4):
                act.dma_start(x_sb[:, 8 * n:8 * n + 8, :], xs[:, 8 * n:8 * n + 8, :]).then_inc(x_in, 16)
            act.wait_ge(constants_set, 26)

            act.dma_start(ctx_sb[:, :, :], ctx.rearrange("(t p) n -> p t n", p=P)).then_inc(ctx_in, 16)

            def high_xt(t):
                act.wait_ge(xt_loaded[t.slot(4)], 4 * (t.n - t.slot(4)) + 16)
                wait_tile(act, proj_v_done, t, 4)
                act.activation(xt_hi[t.slot(4)][:, :, :], xt_raw[t.slot(4)][:, :, :], ACT.Copy).then_inc(xt_hi_set, 1)

            def square_centred(t):
                wait_tile(act, centred_done, t)
                wait_tile(act, head_var_done, t, 1)
                act.activation(centred_sq[:, :, :], centred[:, :, :], ACT.Square).then_inc(centred_sq_done, 1)

            def head_std_root(t):
                wait_tile(act, head_var_done, t)
                wait_tile(act, head_inv_done, t, 1)
                act.activation(head_std[:, :], head_var[:, :], ACT.Sqrt, bias=eps_sb[:, 0:1],
                               scale=1.0 / D).then_inc(head_std_done, 1)

            def set_values(t):
                wait_tile(act, proj_v_done, t)
                wait_tile(act, first["av_done"], t, 4)
                for q in range(2):
                    vals = bank_v[64 * q:64 * q + 64, 0:E].rearrange("p (j o d) -> p j o d", o=2, d=D)
                    for o in range(2):
                        last = act.activation(v_pair[t.slot(4)][q][64 * o:64 * o + 64, :, VW * o:VW * o + D],
                                              vals[:, :, o, :], ACT.Copy)
                last.then_inc(first["v_set"], 1)

            def square_scores(t):
                wait_tile(act, first["scores_done"], t)
                wait_tile(act, first["av_done"], t, 2)
                for b in range(2):
                    last = act.activation(probs[t.slot(2)][:, 512 * b:512 * b + 512], bank_s[b][:, :], ACT.Square)
                last.then_inc(first["probs_squared"], 1)

            def square_masked(t):
                pr = probs[t.slot(2)]
                wait_tile(act, first["probs_masked"], t)
                act.activation(pr[:, :], pr[:, :], ACT.Square).then_inc(first["probs_set"], 1)

            def y_root(t):
                wait_tile(act, first["mv_done"], t)
                wait_tile(act, first["inv_done"], t, 1)
                act.activation(y_std[:, :], y_mv[:, 1:2], ACT.Sqrt, bias=eps_sb[:, 0:1]).then_inc(first["std_done"], 1)

            def step1(i):
                at(i, 0, high_xt)
                at(i, 1, set_values)
                at(i, 2, lambda t: act_move_qk(act, first, t, scale_sb[:, 0:1], bias_sb[:, 0:1]))
                at(i, 1, square_centred)
                at(i, 6, y_root)
                at(i, 5, lambda t: act_o_high(act, first, t))
                at(i, 4, square_masked)
                at(i, 1, head_std_root)
                at(i, 3, square_scores)

            def square_inputs(t):
                if t.first:
                    act.wait_ge(ctx_in, 16)
                act.wait_ge(first["norm_done"], t.n + 1 if isinstance(t.n, int) else T)
                wait_tile(act, rms_in_done, t, 1)
                act.activation(square_out[:, :], x_sb[:, t.n, :], ACT.Square, scale=E ** -0.5,
                               accum_out=mean_sq[:, 0:1]).then_inc(squares_q, 1)
                alone(act)
                wait_tile(act, squares_q, t)
                act.activation(square_out[:, 0:CTX], ctx_sb[:, t.n, :], ACT.Square, scale=CTX ** -0.5,
                               accum_out=mean_sq[:, 1:2]).then_inc(mean_sq_done, 1)

            def set_context_values(t):
                alone(act)
                wait_before(act, "av_done", second, t, 4)
                for q in range(2):
                    vals = ctx_sb[64 * q:64 * q + 64, t.n, :].rearrange("p (g d) -> p g d", d=D)
                    for o in range(2):
                        last = act.activation(v_pair[t.slot(4)][q][64 * o:64 * o + 64, 0:KV_HEADS, VW * o:VW * o + D],
                                              vals, ACT.Copy)
                last.then_inc(second["v_set"], 1)

            def move_probs(t):
                wait_tile(act, second["probs_turned"], t)
                wait_tile(act, second["av_done"], t, 1)
                for n, b in enumerate((bank_qk, bank_v)):
                    last = act.activation(probs_t[:, 4 * n:4 * n + 4, :].rearrange("p j q -> p (j q)"), b[:, :], ACT.Copy)
                last.then_inc(second["probs_turned_moved"], 1)

            def scale_cross(t):
                wait_tile(act, rms_inv_done, t)
                wait_tile(act, cross_sum_done, t)
                wait_tile(act, second["qk_turned"], t, 2)
                rot_t, total = cross_rot[t.slot(2)], cross_sum[t.slot(2)]
                act.activation(rot_t[:, 0:HEADS, :], total[:, 0:HEADS, :], ACT.Copy, scale=rms_inv[:, 0:1])
                act.activation(rot_t[:, HEADS:2 * HEADS, :].rearrange("p (g r) d -> p g r d", g=KV_HEADS),
                               total[:, HEADS:NH, :].unsqueeze(2).broadcast_to([P, KV_HEADS, HEADS // KV_HEADS, D]),
                               ACT.Copy, scale=rms_inv[:, 1:2]).then_inc(cross_scaled, 1)

            def exponentials(t):
                pr = probs[t.slot(2)]
                wait_tile(act, shifted_done, t)
                act.activation(pr[:, :], pr[:, :], ACT.Exp, scale=D ** -0.5).then_inc(second["probs_set"], 1)

            def split_expert(e):
                act.activation(ffn_hi[:, :, e, :], ffn_raw[:, :, e, :], ACT.Copy).then_inc(ffn_hi_set, 1)

            def move_group(g):
                wait_turn(act, x_turned, g)
                for k, b in enumerate(turn_banks(g)):
                    last = act.activation(xg_hi[g.parity][:, k, :], b[:, :], ACT.Copy)
                last.then_inc(xg_hi_set, 1)

            def move_logits(g):
                wait_turn(act, logits_t_done, g)
                wait_turn(act, logits_done, g, 1)
                act.activation(logits_t[:, :], logits_t_bank(g)[0:EXPERTS, :], ACT.Copy).then_inc(logits_t_moved, 1)

            def exp_logits(g):
                wait_turn(act, shifted3_done, g)
                act.activation(expd[:, :, :], shifted[:, :, :], ACT.Exp).then_inc(exp_done, 1)

            def prepare_experts(k):
                if k == 0:
                    act.wait_ge(first["norm_done"], T)
                    act.wait_ge(ffn_in, 48)
                split_expert(k)
                if k == 3:
                    move_group(Turn(0))
                if k == 5:
                    move_logits(Turn(0))
                if k == 6:
                    exp_logits(Turn(0))

            def step2(i):
                at(i, 0, square_inputs)
                at(i, 5, lambda t: act_o_high(act, second, t))
                at(i, 3, exponentials)
                at(i, 0, scale_cross)
                at(i, 3, move_probs)
                at(i, 0, set_context_values)
                at(i, 0, lambda t: act_move_qk(act, second, t, 1.0, 0.0))
                if ending(i) is not None:
                    prepare_experts(ending(i))

            over_tiles(act, step1, step2)
            split_expert(EXPERTS - 1)
            after_second(act)

            def step3(i, g, e):
                if not_last(i):
                    wait_turn(act, gate_done, i)
                    wait_turn(act, h_done, i, 2)
                    act.activation(silu_sb[e % 2][:, :], bank_gate[:, :], ACT.Silu).then_inc(silu_done, 1)
                    wait_turn(act, h_done, i)
                    wait_turn(act, down_done, i, 2)
                    act.activation(h_hi[e % 2][:, :], h_sb[e % 2][:, :], ACT.Copy).then_inc(h_hi_done, 1)
                if more(g):
                    if e == 2:
                        move_group(g.back(-1))
                    if e == 4:
                        move_logits(g.back(-1))
                    if e == 6:
                        exp_logits(g.back(-1))

            over_experts(act, step3)

        @block.vector
        def _(dve):
            for k in range(KC):
                dve.wait_ge(wqkv_split_hi, k + 1)
                dve.tensor_tensor(wqkv_lo[:, k, :], wqkv_raw[:, k, :], wqkv_hi[:, k, :].bitcast(f32),
                                  ALU.subtract).then_inc(weights_split, 1)
            dve.wait_ge(tables_in, TABLES * 16)
            dve.wait_ge(wqkv_split_hi, KC + 2)
            dve.tensor_tensor(wo_lo[:, :, :, :], wo_raw[:, :, :, :], wo_hi[:, :, :, :].bitcast(f32), ALU.subtract).then_inc(weights_split, 1)
            dve.tensor_tensor(router_lo[:, :, :], router_raw[:, :, :], router_hi[:, :, :].bitcast(f32), ALU.subtract).then_inc(weights_split, 1)
            for w, w_cos, w_sin, heads in ((qw_sb, q_cos, q_sin, HEADS), (kw_sb, k_cos, k_sin, KV_HEADS)):
                wv = w[:, :].rearrange("p (h d) -> p h d", d=D)
                dve.tensor_tensor(w_cos[:, :, :], wv, cos_sb[:, :].unsqueeze(1).broadcast_to([P, heads, D]), ALU.mult).then_inc(qk_tables_set, 1)
                for lo, hi in ((0, D // 2), (D // 2, 0)):
                    dve.tensor_tensor(w_sin[:, :, lo:lo + 8], wv[:, :, hi:hi + 8],
                                      sin_sb[:, lo:lo + 8].unsqueeze(1).broadcast_to([P, heads, 8]), ALU.mult).then_inc(qk_tables_set, 1)
            dve.tensor_copy(causal_16[:, :, :], causal_sb[:, :].unsqueeze(1).broadcast_to([P, 4, SEQ]))
            dve.tensor_copy(ident_16[:, :], ident[:, :]).then_inc(qk_tables_set, 1)

            def rotate(t):
                wait_tile(dve, proj_qk_done, t)
                wait_tile(dve, rope_sum_done, t, 1)
                qk = bank_qk[:, :].rearrange("p (h d) -> p h d", d=D)
                dve.tensor_tensor(rot_cos[:, :, :], qk, cos_sb[:, :].unsqueeze(1).broadcast_to([P, 32, D]), ALU.mult)
                for lo, hi in ((0, D // 2), (D // 2, 0)):
                    last = dve.tensor_tensor(rot_sin[:, :, lo:lo + 8], qk[:, :, hi:hi + 8],
                                             sin_sb[:, lo:lo + 8].unsqueeze(1).broadcast_to([P, 32, 8]), ALU.mult)
                last.then_inc(rope_sin_done, 1)

            def sum_heads(t):
                wait_tile(dve, rope_sum_done, t)
                dve.reduce_sum(head_sum[:, :], rot[t.slot(2)][:, :, :], axis=AX.X).then_inc(head_sum_done, 1)

            def mean_heads(t):
                wait_tile(dve, head_sum_done, t)
                wait_tile(dve, centred_done, t, 2)
                dve.tensor_scalar(head_mean[t.slot(2)][:, :], head_sum[:, :], 1.0 / D, None, ALU.mult).then_inc(head_mean_done, 1)

            def sum_squares(t):
                wait_tile(dve, centred_sq_done, t)
                wait_tile(dve, head_std_done, t, 1)
                dve.reduce_sum(head_var[:, :], centred_sq[:, :, :], axis=AX.X).then_inc(head_var_done, 1)

            def invert_head_std(t):
                wait_tile(dve, head_std_done, t)
                wait_tile(dve, qk_norm_done, t, 1)
                dve.reciprocal(head_inv[:, :], head_std[:, :]).then_inc(head_inv_done, 1)

            def invert_y_std(t):
                wait_tile(dve, first["std_done"], t)
                wait_tile(dve, first["norm_done"], t, 1)
                dve.reciprocal(y_inv[:, :], y_std[:, :]).then_inc(first["inv_done"], 1)

            def step1(i):
                at(i, 5, lambda t: dve_o_inverse(dve, first, t))
                at(i, 1, mean_heads)
                at(i, 3, lambda t: dve_set_keys(dve, first, t))
                at(i, 5, lambda t: dve_o_norm(dve, first, t))
                at(i, 6, lambda t: dve_residual(dve, first, t))
                at(i, 6, lambda t: dve_statistics(dve, first, t))
                at(i, 6, lambda t: dve_variance(dve, first, t))
                at(i, 0, rotate)
                at(i, 1, sum_squares)
                at(i, 2, lambda t: low_qk(dve, first, t))
                at(i, 6, invert_y_std)
                at(i, 1, invert_head_std)
                at(i, 6, lambda t: dve_normalise(dve, first, t))
                at(i, 5, lambda t: dve_o_low(dve, first, t))
                at(i, 0, sum_heads)

            def row_maximum(t):
                wait_tile(dve, second["scores_done"], t)
                wait_tile(dve, shifted_done, t, 1)
                for b in range(2):
                    last = dve.reduce_max(row_max[:, 8 * b:8 * b + 8],
                                          bank_s[b][:, :].rearrange("p (n q) -> p n q", q=SEQ), axis=AX.X)
                last.then_inc(row_max_done, 1)

            def shift(t):
                rows = probs[t.slot(2)][:, :].rearrange("p (n q) -> p n q", q=SEQ)
                wait_tile(dve, row_max_done, t)
                wait_tile(dve, second["probs_turned"], t, 2)
                if isinstance(t.n, int) and t.n < 2:
                    dve.wait_ge(first["av_done"], T - 1 + t.n)
                for b in range(2):
                    last = dve.tensor_tensor(rows[:, 8 * b:8 * b + 8, :],
                                             bank_s[b][:, :].rearrange("p (n q) -> p n q", q=SEQ),
                                             row_max[:, 8 * b:8 * b + 8].unsqueeze(2).broadcast_to([P, 8, SEQ]),
                                             ALU.subtract)
                last.then_inc(shifted_done, 1)

            def split_expert(e):
                dve.wait_ge(ffn_hi_set, e + 1)
                dve.tensor_tensor(ffn_lo[:, :, e, :], ffn_raw[:, :, e, :], ffn_hi[:, :, e, :].bitcast(f32),
                                  ALU.subtract).then_inc(ffn_split, 1)

            def split_group(g):
                wait_turn(dve, xg_hi_set, g)
                for k, b in enumerate(turn_banks(g)):
                    last = dve.tensor_tensor(xg_lo[g.parity][:, k, :], b[:, :], xg_hi[g.parity][:, k, :].bitcast(f32), ALU.subtract)
                last.then_inc(xg_split, 1)

            def shift_logits(g):
                wait_turn(dve, logits_done, g)
                logits = logits_bank(g)[:, 0:GROUP_TILES * EXPERTS].rearrange("p (t e) -> p t e", e=EXPERTS)
                dve.reduce_max(top_logit[:, :], logits, axis=AX.X).then_inc(top_logit_done, 1)
                wait_turn(dve, top_logit_done, g)
                wait_turn(dve, exp_done, g, 1)
                dve.tensor_tensor(shifted[:, :, :], logits,
                                  top_logit[:, :].unsqueeze(2).broadcast_to([P, GROUP_TILES, EXPERTS]), ALU.subtract).then_inc(shifted3_done, 1)

            def pick_best(g):
                alone(dve)
                wait_turn(dve, exp_done, g)
                for j in range(GROUP_TILES):
                    last = dve.max(best[:, j, :], expd[:, j, :])
                last.then_inc(best_done, 1)
                wait_turn(dve, best_done, g)
                dve.tensor_tensor(pair_sum[:, :], best[:, :, 0], best[:, :, 1], ALU.add).then_inc(pair_sum_done, 1)
                for j in range(GROUP_TILES):
                    last = dve.max_index(best_at[:, j, :], best[:, j, :], expd[:, j, :])
                last.then_inc(best_at_done, 1)
                wait_turn(dve, pair_sum_done, g)
                dve.reciprocal(pair_inv[:, :], pair_sum[:, :]).then_inc(pair_inv_done, 1)
                wait_turn(dve, best_at_done, g)
                dve.tensor_copy(best_at_f[:, :, :], best_at[:, :, :]).then_inc(best_f_done, 1)
                wait_turn(dve, pair_inv_done, g)
                dve.tensor_tensor(pair_w[:, :, :], best[:, :, 0:2], pair_inv[:, :].unsqueeze(2).broadcast_to([P, GROUP_TILES, 2]),
                                  ALU.mult).then_inc(pair_w_done, 1)

            def combine_weights(g):
                iota = iota_sb[:, :].unsqueeze(1).broadcast_to([P, GROUP_TILES, EXPERTS])
                wait_turn(dve, best_f_done, g)
                wait_turn(dve, pair_w_done, g)
                for r in range(2):
                    at_r = best_at_f[:, :, r:r + 1].broadcast_to([P, GROUP_TILES, EXPERTS])
                    last = dve.tensor_tensor(chosen[r][:, :, :], iota, at_r, ALU.is_equal)
                last.then_inc(chosen_done, 1)
                wait_turn(dve, chosen_done, g)
                for r in range(2):
                    w_r = pair_w[:, :, r:r + 1].broadcast_to([P, GROUP_TILES, EXPERTS])
                    last = dve.tensor_tensor(picked[r][:, :, :], chosen[r][:, :, :], w_r, ALU.mult)
                last.then_inc(picked_done, 1)
                wait_turn(dve, picked_done, g)
                dve.tensor_tensor(combine[g.parity][:, :, :], picked[0][:, :, :], picked[1][:, :, :], ALU.add).then_inc(combine_done, 1)

            def prepare_experts(k):
                split_expert(k)
                if k == 3:
                    split_group(Turn(0))
                if k == 6:
                    shift_logits(Turn(0))

            def step2(i):
                at(i, 4, lambda t: dve_o_inverse(dve, second, t))
                at(i, 7, lambda t: dve_normalise(dve, second, t))
                at(i, 4, lambda t: dve_o_norm(dve, second, t))
                at(i, 5, lambda t: dve_o_low(dve, second, t))
                at(i, 6, lambda t: dve_residual(dve, second, t))
                at(i, 6, lambda t: dve_statistics(dve, second, t))
                at(i, 2, row_maximum)
                at(i, 6, lambda t: dve_variance(dve, second, t))
                at(i, 1, lambda t: dve_set_keys(dve, second, t))
                at(i, 2, shift)
                if ending(i) is not None:
                    prepare_experts(ending(i))

            over_tiles(dve, step1, step2)
            split_expert(EXPERTS - 1)
            after_second(dve)
            pick_best(Turn(0))
            combine_weights(Turn(0))

            def weigh(i, g, e):
                wait_turn(dve, down_done, i)
                wait_turn(dve, weighed, i, 1)
                if e == 0:
                    wait_turn(dve, combine_done, g)
                    wait_turn(dve, out_set, g, 2)
                sums, banks = acc[g.parity], bank_down[e % 2]
                for j in range(GROUP_TILES):
                    onto = x_sb[:, g.n * GROUP_TILES + j, :] if e == 0 else sums[:, j, :]
                    last = dve.scalar_tensor_tensor(sums[:, j, :], banks[j // 2][:, j % 2 * E:j % 2 * E + E],
                                                    combine[g.parity][:, j, e:e + 1], onto, ALU.mult, ALU.add)
                last.then_inc(weighed, 1)

            def finish_group(g, e):
                sums = acc[g.parity]
                if e == 1:
                    wait_turn(dve, weighed, Turn((g.n + 1) * EXPERTS - 1))
                    for j in range(GROUP_TILES):
                        last = dve.bn_stats(g_stats[:, j, :], sums[:, j, :])
                    last.then_inc(g_stats_done, 1)
                if e == 2:
                    alone(dve)
                    wait_turn(dve, g_stats_done, g)
                    for j in range(GROUP_TILES):
                        last = dve.bn_aggr(g_mv[:, j, :], g_stats[:, j, :])
                    last.then_inc(g_mv_done, 1)
                if e == 4:
                    wait_turn(dve, g_inv_done, g)
                    wait_stores(dve, g, 1)
                    for j in range(GROUP_TILES):
                        last = dve.tensor_scalar(out_sb[:, j, :], sums[:, j, :], g_mv[:, j, 0:1], g_inv[:, j:j + 1],
                                                 ALU.subtract, ALU.mult)
                    last.then_inc(out_set, 1)

            def step3(i, g, e):
                if not_last(i):
                    wait_turn(dve, up_done, i)
                    wait_turn(dve, silu_done, i)
                    wait_turn(dve, h_split, i, 2)
                    dve.tensor_tensor(h_sb[e % 2][:, :], bank_up[:, :], silu_sb[e % 2][:, :], ALU.mult).then_inc(h_done, 1)
                    wait_turn(dve, h_hi_done, i)
                    wait_turn(dve, down_done, i, 2)
                    dve.tensor_tensor(h_lo[e % 2][:, :], h_sb[e % 2][:, :], h_hi[e % 2][:, :].bitcast(f32), ALU.subtract).then_inc(h_split, 1)
                if e > 0 and not_last(i):
                    weigh(i.back(1), g, e - 1)
                elif e == 0 and later(g):
                    weigh(i.back(1), g.back(1), EXPERTS - 1)
                if later(g):
                    finish_group(g.back(1), e)
                if more(g):
                    if e == 3:
                        split_group(g.back(-1))
                    if e == 5:
                        shift_logits(g.back(-1))
                    if e == 6:
                        pick_best(g.back(-1))
                    if e == 7:
                        combine_weights(g.back(-1))

            over_experts(dve, step3)

        @block.tensor
        def _(pe):
            pe.wait_ge(tables_in, TABLES * 16)
            pe.wait_ge(weights_split, KC)

            def project(bank, t, first_col, cols):
                hi, lo = xt_hi[t.slot(4)], xt_lo[t.slot(4)]
                passes = [(l, w, c) for l, w in ((hi, wqkv_hi), (hi, wqkv_lo), (lo, wqkv_hi)) for c in range(KC)]
                for n, (l, w, c) in enumerate(passes):
                    last = pe.matmul(bank[:, 0:cols], l[:, c, :], w[:, c, first_col:first_col + cols],
                                     start=n == 0, stop=n == len(passes) - 1)
                return last

            def project_qk(t):
                wait_tile(pe, xt_split, t)
                wait_tile(pe, rope_sin_done, t, 1)
                project(bank_qk, t, 0, 2 * E).then_inc(proj_qk_done, 1)

            def project_v(t):
                wait_tile(pe, first["v_set"], t, 1)
                project(bank_v, t, 2 * E, E).then_inc(proj_v_done, 1)

            def turn_qk(t):
                wait_tile(pe, qk_norm_done, t)
                wait_tile(pe, first["qk_hi_set"], t, 1)
                flat = qk_norm[t.slot(2)][:, :, :].rearrange("p h d -> p (h d)")
                pe_turn(pe, first, t, lambda n: flat[:, n * P:(n + 1) * P])

            def score(t):
                wait_tile(pe, first["keys_set"], t)
                wait_tile(pe, first["probs_squared"], t, 1)
                keys, kq = k_one[t.slot(2)], kq_parts[t.slot(2)]
                for j in range(PAIRS):
                    c, b, m = j // 4, j // 2 % 2, j % 2
                    rows = slice(64 * b, 64 * b + 64)
                    for q in range(2):
                        at_col = ((q * 2 + c) * 2 + m) * SEQ
                        cols = slice(c * P + q * 64, c * P + q * 64 + 64)
                        for n, (part, q_part) in enumerate(((0, 0), (0, 1), (1, 0))):
                            last = pe.matmul(
                                bank_s[b][:, at_col:at_col + SEQ],
                                keys[rows, part, c, q, 2 * m:2 * m + 2, :].rearrange("p m n -> p (m n)"),
                                kq[rows, q_part, cols], start=n == 0, stop=n == 2)
                last.then_inc(first["scores_done"], 1)

            def weigh_values(t):
                wait_tile(pe, first["probs_set"], t)
                wait_tile(pe, first["v_set"], t)
                wait_tile(pe, first["o_done"], t, 1)
                pr = probs[t.slot(2)][:, :].rearrange("p (b q c m n) -> p b q c m n", b=2, q=2, c=2, m=2)
                for j in range(PAIRS):
                    c, b, m = j // 4, j // 2 % 2, j % 2
                    for q in range(2):
                        last = pe.matmul(bank_av[64 * q:64 * q + 64, 2 * VW * j:2 * VW * (j + 1)],
                                         pr[:, b, q, c, m, :], v_pair[t.slot(4)][q][:, j, :], start=True, stop=True)
                last.then_inc(first["av_done"], 1)

            def step1(i):
                at(i, 2, turn_qk)
                at(i, 6, lambda t: pe_project(pe, first, t, 0))
                at(i, 0, project_qk)
                at(i, 0, project_v)
                at(i, 5, lambda t: pe_turn_o(pe, first, t))
                at(i, 3, score)
                at(i, 4, weigh_values)

            def turn_cross_qk(t):
                wait_tile(pe, cross_scaled, t)
                wait_before(pe, "qk_hi_set", second, t)
                flat = cross_rot[t.slot(2)][:, :, :].rearrange("p h d -> p (h d)")
                pe_turn(pe, second, t, lambda n: flat[:, n * P:(n + 1) * P])

            def score_cross(t):
                alone(pe)
                wait_tile(pe, second["keys_set"], t)
                if t.first:
                    pe.wait_ge(qk_tables_set, 7)
                    pe.wait_ge(first["probs_squared"], T)
                wait_tile(pe, shifted_done, t, 1)
                keys, kq = k_one[t.slot(2)], kq_parts[t.slot(2)]
                for c in range(KC):
                    for q in range(2):
                        cols = slice(c * P + q * 64, c * P + q * 64 + 64)
                        for b in range(2):
                            rows = slice(64 * b, 64 * b + 64)
                            pe.matmul(bank_s[b][64 * q:64 * q + 64, 256 * c:256 * c + 256], ident_16[rows, rows],
                                      causal_16[rows, :, :].rearrange("p m n -> p (m n)"), start=True, stop=False)
                            for n, (q_part, part) in enumerate(((0, 0), (0, 1), (1, 0))):
                                last = pe.matmul(bank_s[b][64 * q:64 * q + 64, 256 * c:256 * c + 256],
                                                 kq[rows, q_part, cols],
                                                 keys[rows, part, c, q, :, :].rearrange("p m n -> p (m n)"),
                                                 start=False, stop=n == 2)
                last.then_inc(second["scores_done"], 1)

            def turn_probs(t):
                wait_tile(pe, second["probs_set"], t)
                if t.first:
                    pe.wait_ge(rope_sin_done, T)
                    pe.wait_ge(first["v_set"], T)
                wait_tile(pe, second["probs_turned_moved"], t, 1)
                pr = probs[t.slot(2)][:, :].rearrange("p (b c m n) -> p b c m n", b=2, c=2, m=4)
                for j in range(PAIRS):
                    c, b, m = j // 4, j // 2 % 2, j % 2
                    last = pe.transpose((bank_qk, bank_v)[j // 4][:, j % 4 * P:j % 4 * P + P],
                                        pr[:, b, c, 2 * m:2 * m + 2, :].rearrange("p m n -> p (m n)"), ident[:, :])
                last.then_inc(second["probs_turned"], 1)

            def weigh_context(t):
                wait_tile(pe, second["probs_turned_moved"], t)
                wait_tile(pe, second["v_set"], t)
                wait_before(pe, "o_done", second, t)
                for j in range(PAIRS):
                    for q in range(2):
                        last = pe.matmul(bank_av[64 * q:64 * q + 64, 2 * VW * j:2 * VW * (j + 1)],
                                         probs_t[:, j, 64 * q:64 * q + 64], v_pair[t.slot(4)][q][:, j // 2, :],
                                         start=True, stop=True)
                last.then_inc(second["av_done"], 1)

            def turn_group(g):
                if first_group(g):
                    pe.wait_ge(second["norm_done"], GROUP_TILES)
                    pe.wait_ge(shifted_done, T)
                    source = x_sb
                else:
                    wait_turn(pe, x_copied, g, 1)
                    wait_turn(pe, shifted3_done, g, 1)
                    source = x_group
                for k, b in enumerate(turn_banks(g)):
                    for j in range(GROUP_TILES):
                        last = pe.transpose(b[:, j * P:j * P + P], source[:, j, k * P:k * P + P], ident[:, :])
                last.then_inc(x_turned, 1)

            def score_group(g):
                wait_turn(pe, xg_split, g)
                if first_group(g):
                    pe.wait_ge(second["qk_hi_set"], T)
                hi, lo = xg_hi[g.parity], xg_lo[g.parity]
                passes = [(w, v, k) for w, v in ((router_hi, hi), (router_lo, hi), (router_hi, lo)) for k in range(KC)]
                for n, (w, v, k) in enumerate(passes):
                    last = pe.matmul(logits_t_bank(g)[0:EXPERTS, :], w[:, k, :], v[:, k, :], start=n == 0, stop=n == 5)
                last.then_inc(logits_t_done, 1)

            def turn_logits(g):
                alone(pe)
                wait_turn(pe, logits_t_moved, g)
                for j in range(GROUP_TILES):
                    last = pe.transpose(logits_bank(g)[:, j * EXPERTS:(j + 1) * EXPERTS], logits_t[:, j * P:j * P + P],
                                        ident[0:EXPERTS, 0:EXPERTS])
                last.then_inc(logits_done, 1)

            def step2(i):
                if not isinstance(i.n, int):
                    pe.wait_ge(second["qk_turned"], i.n - 1)
                    pe.wait_ge(second["qk_turned"], i.n - 2)
                at(i, 4, weigh_context)
                at(i, 2, score_cross)
                at(i, 3, turn_probs)
                at(i, 0, turn_cross_qk)
                at(i, 4, lambda t: pe_turn_o(pe, second, t))
                at(i, 5, lambda t: pe_project(pe, second, t, 1))
                if ending(i) == 2:
                    turn_group(Turn(0))
                if ending(i) == 4:
                    score_group(Turn(0))
                if ending(i) == 5:
                    turn_logits(Turn(0))

            over_tiles(pe, step1, step2)
            pe.wait_ge(second["probs_turned_moved"], T)

            def down(i, g, e):
                wait_turn(pe, h_split, i)
                wait_turn(pe, weighed, i, 2)
                banks = bank_down[e % 2]
                for j in range(GROUP_TILES):
                    cols = slice(j * P, j * P + P)
                    for n, (h, w) in enumerate(((h_hi, ffn_hi), (h_hi, ffn_lo), (h_lo, ffn_hi))):
                        last = pe.matmul(banks[j // 2][:, j % 2 * E:j % 2 * E + E], h[e % 2][:, cols], w[:, 2, e, :],
                                         start=n == 0, stop=n == 2)
                last.then_inc(down_done, 1)

            def gate_or_up(bank, m, g, e):
                hi, lo = xg_hi[g.parity], xg_lo[g.parity]
                passes = [(w, v, k) for w, v in ((ffn_hi, hi), (ffn_lo, hi), (ffn_hi, lo)) for k in range(KC)]
                for n, (w, v, k) in enumerate(passes):
                    last = pe.matmul(bank[:, :], w[:, m, e, k * F:(k + 1) * F], v[:, k, :], start=n == 0, stop=n == 5)
                return last

            def step3(i, g, e):
                if not_last(i):
                    if first_group(g):
                        pe.wait_ge(ffn_split, e + 1)
                    wait_turn(pe, silu_done, i, 1)
                    gate_or_up(bank_gate, 0, g, e).then_inc(gate_done, 1)
                    wait_turn(pe, h_done, i, 1)
                    gate_or_up(bank_up, 1, g, e).then_inc(up_done, 1)
                if e > 0 and not_last(i):
                    down(i.back(1), g, e - 1)
                elif e == 0 and later(g):
                    down(i.back(1), g.back(1), EXPERTS - 1)
                if more(g):
                    if e == 2:
                        turn_group(g.back(-1))
                    if e == 4:
                        score_group(g.back(-1))
                    if e == 5:
                        turn_logits(g.back(-1))

            over_experts(pe, step3)


def rotary_tables():
    inv = (1.0 / np.float32(10000.0) ** (np.arange(0, D, 2, dtype=np.float32) / np.float32(D))).astype(np.float32)
    angle = np.arange(SEQ, dtype=np.float32)[:, None] * inv[None, :]
    cos, sin = np.cos(angle).astype(np.float32), np.sin(angle).astype(np.float32)
    return np.tile(np.concatenate([cos, cos], 1), (2, 1)), np.tile(np.concatenate([-sin, sin], 1), (2, 1))


def kernel(x, ctx_512, L0_attn_w_qkv, L0_attn_w_out, L0_attn_ln_scale, L0_attn_ln_bias, L0_xattn_q_norm_w,
           L0_xattn_k_norm_w, L0_xattn_w_out, L0_ffn_router_w, L0_ffn_gate_proj, L0_ffn_up_proj, L0_ffn_down_proj):
    import concourse.bacc as bacc
    from concourse.bass_utils import run_bass_kernel_spmd

    flat = np.asarray(x).reshape(TOKENS, E)
    cos, sin = rotary_tables()
    pos = np.arange(P) % SEQ
    keep = (pos[:, None] <= np.arange(SEQ)[None, :]).astype(np.float32)
    causal = np.where(np.arange(SEQ)[None, :] <= pos[:, None], 0.0, -1e30).astype(np.float32)
    quarter = (np.arange(P)[:, None] % 64 // D == np.arange(4)[None, :]).astype(np.float32)
    arrays = {
        "x": flat,
        "x_t": np.ascontiguousarray(flat.T),
        "ctx": np.asarray(ctx_512).reshape(TOKENS, CTX),
        "w_qkv": np.asarray(L0_attn_w_qkv),
        "w_out1": np.asarray(L0_attn_w_out),
        "ln_pair": np.ascontiguousarray(np.tile(np.stack([np.asarray(L0_attn_ln_scale), np.asarray(L0_attn_ln_bias)], 1),
                                                (P // D, 1))),
        "q_w": np.asarray(L0_xattn_q_norm_w),
        "k_w": np.asarray(L0_xattn_k_norm_w),
        "w_out2_t": np.ascontiguousarray(np.asarray(L0_xattn_w_out).T),
        "router": np.asarray(L0_ffn_router_w),
        "gate_w": np.asarray(L0_ffn_gate_proj),
        "up_w": np.asarray(L0_ffn_up_proj),
        "down_w": np.asarray(L0_ffn_down_proj),
        "tables": np.concatenate([np.eye(P, dtype=np.float32), cos, sin, keep, causal, quarter,
                                  np.tile(np.arange(EXPERTS, dtype=np.float32), (P, 1))], 1),
    }
    nc = bacc.Bacc("TRN2", target_bir_lowering=False, num_devices=1)
    args = {n: nc.dram_tensor(n, a.shape, mybir.dt.from_np(a.dtype), kind="ExternalInput").ap()
            for n, a in arrays.items()}
    out = nc.dram_tensor("out", (TOKENS, E), mybir.dt.float32, kind="ExternalOutput").ap()
    build_decoder(nc, out=out, **args)
    result = run_bass_kernel_spmd(nc, [arrays], core_ids=[0])
    return result.results[0]["out"].reshape(SEQS, SEQ, E)
```
